# Optimizing a Trainium2 kernel written in Bass

```python
import numpy as np
import jax
import jax.numpy as jnp

def _softmax(x, axis=-1):
    return jax.nn.softmax(x, axis=axis)

def _gelu(x):
    return jax.nn.gelu(x, approximate=True)

def _silu(x):
    return jax.nn.silu(x)

def _sigmoid(x):
    return jax.nn.sigmoid(x)

def _layernorm(x, axis=-1, eps=1e-05):
    m = jnp.mean(x, axis=axis, keepdims=True)
    v = jnp.var(x, axis=axis, keepdims=True)
    return (x - m) / jnp.sqrt(v + eps)

def _scatter_add(tgt, idx, src, axis=0):
    return tgt.at[idx].add(src)

def _segment_sum(src, seg, n):
    return jax.ops.segment_sum(src, seg, n)
kernel_name = 'mk_gnn_preln_d4_gnn_r64_280c49'

def setup_inputs(seed: int=0):
    np.random.seed(seed)
    _w = jnp.asarray

    def _rec_inputs():
        import jax
        import jax.numpy as jnp
        _gk = jax.random.key(seed)
        x = -0.0005121 + 1.001 * jax.random.normal(jax.random.fold_in(_gk, 1), (100000, 32), jnp.float32)
        src = jax.random.randint(jax.random.fold_in(_gk, 2), (25000,), 0, 100000, jnp.int32)
        dst = jax.random.randint(jax.random.fold_in(_gk, 3), (25000,), 0, 100000, jnp.int32)
        _o = jnp.argsort(dst, stable=True)
        src = src[_o]
        dst = dst[_o]
        edge_attr_2 = -5.09086e-05 + 0.577461 * jax.random.normal(jax.random.fold_in(_gk, 12), (25000, 2), jnp.float32)
        return (x, src, dst, edge_attr_2)
    x, src, dst, edge_attr_2 = _rec_inputs()

    def _L0_gnn_setup():
        import jax, jax.numpy as jnp
        import numpy as np
        N_NODES = 100000

        def gcn_conv(x, edge_index, W, b):
            n = x.shape[0]
            loop = jnp.arange(n, dtype=edge_index.dtype)
            src = jnp.concatenate([edge_index[0], loop])
            dst = jnp.concatenate([edge_index[1], loop])
            deg = jax.ops.segment_sum(jnp.ones(src.shape[0], dtype=x.dtype), dst, num_segments=n)
            dinv = jnp.where(deg > 0, jax.lax.rsqrt(jnp.maximum(deg, 1)), 0.0).astype(x.dtype)
            norm = dinv[src] * dinv[dst]
            h = x @ W
            msg = h[src] * norm[:, None]
            out = jax.ops.segment_sum(msg, dst, num_segments=n)
            return out + b
        key = jax.random.key(seed)
        k = jax.random.split(key, 7)
        input_dim, hidden_dim = (32, 16)
        n_edges = 25000
        x = jax.random.normal(k[0], (N_NODES, input_dim), dtype=jnp.float32)
        edge_index = jax.random.randint(k[1], (2, n_edges), 0, N_NODES, dtype=jnp.int64)
        s = 1.0 / np.sqrt(input_dim)
        W1 = jax.random.uniform(k[2], (input_dim, hidden_dim), jnp.float32, -s, s)
        b1 = jnp.zeros((hidden_dim,), jnp.float32)
        s2 = 1.0 / np.sqrt(hidden_dim)
        W2 = jax.random.uniform(k[3], (hidden_dim, input_dim), jnp.float32, -s2, s2)
        b2 = jnp.zeros((input_dim,), jnp.float32)
        return {'x': x, 'edge_index': edge_index, 'W1': W1, 'b1': b1, 'W2': W2, 'b2': b2}
    _L0_gnn_all = _L0_gnn_setup()
    _L0_gnn_in = {k: v for k, v in _L0_gnn_all.items() if k in ('W1', 'b1', 'W2', 'b2')}
    del _L0_gnn_all

    def _L1_gnn_setup():
        import jax, jax.numpy as jnp
        import numpy as np
        N_NODES = 100000
        N_EDGES = 25000
        D_FEAT = 32
        K = 10
        ALPHA = 0.1
        key = jax.random.key(seed)
        k1, k2, k3 = jax.random.split(key, 3)
        feat = jax.random.normal(k1, (N_NODES, D_FEAT), dtype=jnp.float32)
        src = jax.random.randint(k2, (N_EDGES,), 0, N_NODES, dtype=jnp.int64)
        dst = jax.random.randint(k3, (N_EDGES,), 0, N_NODES, dtype=jnp.int64)
        return {'feat': feat, 'src': src, 'dst': dst}
    _L1_gnn_all = _L1_gnn_setup()
    _L1_gnn_in = {k: v for k, v in _L1_gnn_all.items() if k in ()}
    del _L1_gnn_all

    def _L2_gnn_setup():
        import jax, jax.numpy as jnp
        import numpy as np
        N_NODES = 50000
        N_EDGES = 25000
        F_IN = 32
        F_OUT = 32
        BASIS = (4, 4)

        def _tent_basis(u, n):
            centers = jnp.linspace(-1.0, 1.0, n, dtype=u.dtype)
            h = 2.0 / (n - 1)
            return jnp.maximum(0.0, 1.0 - jnp.abs(u[:, None] - centers[None, :]) / h)
        key = jax.random.key(seed)
        k1, k2, k3, k4, k5 = jax.random.split(key, 5)
        x = jax.random.normal(k1, (N_NODES, F_IN), dtype=jnp.float32)
        edge_attr = jax.random.uniform(k2, (N_EDGES, 2), dtype=jnp.float32, minval=-1.0, maxval=1.0)
        weight = jax.random.uniform(k3, (*BASIS, F_IN, F_OUT), dtype=jnp.float32, minval=-0.05, maxval=0.05)
        src = jax.random.randint(k4, (N_EDGES,), 0, N_NODES)
        tgt = jax.random.randint(k5, (N_EDGES,), 0, N_NODES)
        edge_index = jnp.stack([tgt, src], axis=0).astype(jnp.int64)
        return {'x': x, 'edge_attr': edge_attr, 'weight': weight, 'edge_index': edge_index}
    _L2_gnn_all = _L2_gnn_setup()
    _L2_gnn_in = {k: v for k, v in _L2_gnn_all.items() if k in ('weight',)}
    del _L2_gnn_all

    def _L3_gnn_setup():
        import jax, jax.numpy as jnp
        import numpy as np
        N_NODES = 50000
        DEG = 16
        N_HEAD = 4
        F_IN = 32
        F_OUT = 32
        key = jax.random.key(seed)
        k_h, k_w, k_fw, k_fb = jax.random.split(key, 4)
        h = jax.random.normal(k_h, (N_NODES, F_IN), dtype=jnp.float32)
        src = jnp.repeat(jnp.arange(N_NODES, dtype=jnp.int64), DEG)
        offs = (jnp.arange(DEG, dtype=jnp.int64) + 1) * 97
        dst = (src.reshape(N_NODES, DEG) + offs[None, :]).reshape(-1) % N_NODES
        edge_index = jnp.stack([src, dst], axis=0)
        gain = 1.414
        bound_w = gain * np.sqrt(6.0 / (F_IN + F_OUT))
        w = jax.random.uniform(k_w, (N_HEAD, F_IN, F_OUT), jnp.float32, -bound_w, bound_w)
        bound_fc = np.sqrt(1.0 / (2 * F_OUT))
        fc_w = jax.random.uniform(k_fw, (1, 2 * F_OUT), jnp.float32, -bound_fc, bound_fc)
        fc_b = jax.random.uniform(k_fb, (1,), jnp.float32, -bound_fc, bound_fc)
        bias = jnp.zeros((F_OUT,), jnp.float32)
        return {'h': h, 'edge_index': edge_index, 'w': w, 'fc_w': fc_w, 'fc_b': fc_b, 'bias': bias}
    _L3_gnn_all = _L3_gnn_setup()
    _L3_gnn_in = {k: v for k, v in _L3_gnn_all.items() if k in ('w', 'fc_w', 'fc_b', 'bias')}
    del _L3_gnn_all
    return {'x': x, 'src': src, 'dst': dst, 'edge_attr_2': edge_attr_2, 'L0_gnn_W1': _L0_gnn_in['W1'], 'L0_gnn_b1': _L0_gnn_in['b1'], 'L0_gnn_W2': _L0_gnn_in['W2'], 'L0_gnn_b2': _L0_gnn_in['b2'], 'L2_gnn_weight': _L2_gnn_in['weight'], 'L3_gnn_w': _L3_gnn_in['w'], 'L3_gnn_fc_w': _L3_gnn_in['fc_w'], 'L3_gnn_fc_b': _L3_gnn_in['fc_b'], 'L3_gnn_bias': _L3_gnn_in['bias']}

def reference(x, src, dst, edge_attr_2, L0_gnn_W1, L0_gnn_b1, L0_gnn_W2, L0_gnn_b2, L2_gnn_weight, L3_gnn_w, L3_gnn_fc_w, L3_gnn_fc_b, L3_gnn_bias):
    import jax
    import jax.numpy as jnp

    def _L0_gnn_ref(x, edge_index, W1, b1, W2, b2):
        import jax, jax.numpy as jnp
        import numpy as np
        N_NODES = 100000

        def gcn_conv(x, edge_index, W, b):
            n = x.shape[0]
            loop = jnp.arange(n, dtype=edge_index.dtype)
            src = jnp.concatenate([edge_index[0], loop])
            dst = jnp.concatenate([edge_index[1], loop])
            deg = jax.ops.segment_sum(jnp.ones(src.shape[0], dtype=x.dtype), dst, num_segments=n)
            dinv = jnp.where(deg > 0, jax.lax.rsqrt(jnp.maximum(deg, 1)), 0.0).astype(x.dtype)
            norm = dinv[src] * dinv[dst]
            h = x @ W
            msg = h[src] * norm[:, None]
            out = jax.ops.segment_sum(msg, dst, num_segments=n)
            return out + b
        h = gcn_conv(x, edge_index, W1, b1)
        h = jax.nn.relu(h)
        return gcn_conv(h, edge_index, W2, b2)

    def _L1_gnn_ref(feat, src, dst):
        import jax, jax.numpy as jnp
        import numpy as np
        N_NODES = 100000
        N_EDGES = 25000
        D_FEAT = 32
        K = 10
        ALPHA = 0.1
        n = feat.shape[0]
        ones = jnp.ones(src.shape[0], dtype=feat.dtype)
        out_deg = jax.ops.segment_sum(ones, src, num_segments=n)
        in_deg = jax.ops.segment_sum(ones, dst, num_segments=n)
        src_norm = jnp.clip(out_deg, 1.0, None) ** (-0.5)
        dst_norm = jnp.clip(in_deg, 1.0, None) ** (-0.5)
        feat0 = feat

        def step(f, _):
            f = f * src_norm[:, None]
            agg = jax.ops.segment_sum(f[src], dst, num_segments=n)
            f = agg * dst_norm[:, None]
            f = (1.0 - ALPHA) * f + ALPHA * feat0
            return (f, None)
        feat, _ = jax.lax.scan(step, feat, None, length=K)
        return feat

    def _L2_gnn_ref(x, edge_attr, weight, edge_index):
        import jax, jax.numpy as jnp
        import numpy as np
        N_NODES = 50000
        N_EDGES = 25000
        F_IN = 32
        F_OUT = 32
        BASIS = (4, 4)

        def _tent_basis(u, n):
            centers = jnp.linspace(-1.0, 1.0, n, dtype=u.dtype)
            h = 2.0 / (n - 1)
            return jnp.maximum(0.0, 1.0 - jnp.abs(u[:, None] - centers[None, :]) / h)
        k1, k2, f_in, f_out = weight.shape
        n_nodes = x.shape[0]
        bu = _tent_basis(edge_attr[:, 0], k1)
        bv = _tent_basis(edge_attr[:, 1], k2)
        basis = (bu[:, :, None] * bv[:, None, :]).reshape(-1, k1 * k2)
        xj = x[edge_index[1]]
        w2 = weight.reshape(k1 * k2, f_in, f_out)
        msg = basis[:, 0:1] * (xj @ w2[0])
        for k in range(1, k1 * k2):
            msg = msg + basis[:, k:k + 1] * (xj @ w2[k])
        out = jax.ops.segment_sum(msg, edge_index[0], num_segments=n_nodes)
        return out

    def _L3_gnn_ref(h, edge_index, w, fc_w, fc_b, bias):
        import jax, jax.numpy as jnp
        import numpy as np
        N_NODES = 50000
        DEG = 16
        N_HEAD = 4
        F_IN = 32
        F_OUT = 32
        n_head, f_in, f_out = w.shape
        n = h.shape[0]
        src, dst = (edge_index[0], edge_index[1])
        hp = jnp.einsum('nf,hfo->hno', h, w)
        w_src = fc_w[0, :f_out]
        w_dst = fc_w[0, f_out:]
        a_src = jnp.einsum('hnf,f->hn', hp, w_src)
        a_dst = jnp.einsum('hnf,f->hn', hp, w_dst)
        e = a_src[:, src] + a_dst[:, dst] + fc_b[0]
        e = jax.nn.leaky_relu(e, negative_slope=0.2)
        seg_max = jax.ops.segment_max(e.T, src, num_segments=n)
        e = jnp.exp(e - seg_max.T[:, src])
        seg_sum = jax.ops.segment_sum(e.T, src, num_segments=n)
        att = e / seg_sum.T[:, src]
        msg = att[:, :, None] * hp[:, dst, :]
        agg = jax.vmap(lambda m: jax.ops.segment_sum(m, src, num_segments=n))(msg)
        out = agg.mean(axis=0) + bias
        return out
    edge_index = jnp.stack([src, dst])
    h = jnp.maximum(_layernorm(x, axis=-1), 0.0)
    x = x + _L0_gnn_ref(h, edge_index, L0_gnn_W1, L0_gnn_b1, L0_gnn_W2, L0_gnn_b2)
    h = jnp.maximum(_layernorm(x, axis=-1), 0.0)
    x = x + _L1_gnn_ref(h, src, dst)
    h = jnp.maximum(_layernorm(x, axis=-1), 0.0)
    x = x + _L2_gnn_ref(h, edge_attr_2, L2_gnn_weight, edge_index)
    h = jnp.maximum(_layernorm(x, axis=-1), 0.0)
    x = x + _L3_gnn_ref(h, edge_index, L3_gnn_w, L3_gnn_fc_w, L3_gnn_fc_b, L3_gnn_bias)
    return x

_drawn_inputs = setup_inputs


def setup_inputs(seed=0):
    import zlib

    import numpy as np

    out = dict(_drawn_inputs(seed))
    spreads = {'L0_gnn_b1': (0.0, 0.1), 'L0_gnn_b2': (0.0, 0.1), 'L3_gnn_bias': (0.0, 0.1)}
    factors = {'L3_gnn_fc_w': 6.517}
    for name, (base, spread) in spreads.items():
        noise = np.random.default_rng([zlib.crc32(name.encode()), seed]).standard_normal(out[name].shape)
        drawn = base * np.exp(spread * noise) if base else spread * noise
        out[name] = jnp.asarray(drawn.astype(out[name].dtype))
    for name, factor in factors.items():
        out[name] = (out[name] * factor).astype(out[name].dtype)
    return out
```

```python
from contextlib import ExitStack

import concourse.bass as bass
from concourse import mybir

F32 = mybir.dt.float32
I32 = mybir.dt.int32
ALU = mybir.AluOpType
ACT = mybir.ActivationFunctionType
AX = mybir.AxisListType

P = 128
N = 100000
E = 25000
F = 32
HID = 16
HEADS = 4
BASIS = 4
COLS = -(-E // P)
SLOTS = P * COLS
CHUNK = 28
CHUNKS = COLS // CHUNK
FULL_ROWS = E // COLS
REST = E - FULL_ROWS * COLS
INFO = F
ROW = F + 4
NODES = N + 8
DIGIT = 256
HIGH = N // DIGIT + 1
STEPS = 10
ALPHA = 0.1
EPS = 1e-5
SLOPE = 0.2
NOWHERE = float(1 << 22)
HUGE = 1e30
GROUP = 4
DN = 12
DSTEPS = N // (P * DN)
DREST = N - DSTEPS * P * DN
RP = DREST // GROUP
ds = bass.ds


def gnn_kernel(nc, x, src, dst, edge_attr, W1, b1, W2, b2, w_spline, w_gat, fc_w, fc_b, bias, out):
    assert COLS % CHUNK == 0 and REST > 0 and RP * GROUP == DREST and RP <= P

    nodes = nc.dram_tensor("node_rows", (NODES, ROW), F32, kind="Internal").ap()
    sort1 = nc.dram_tensor("sorted_by_low_digit", (SLOTS, 2), F32, kind="Internal").ap()
    sort2 = nc.dram_tensor("sorted_by_src", (SLOTS, 2), F32, kind="Internal").ap()
    t_gcn = nc.dram_tensor("t_gcn", (2 * SLOTS, HID), F32, kind="Internal").ap()
    t_x1 = nc.dram_tensor("t_x1", (2 * SLOTS, F), F32, kind="Internal").ap()
    t_prop = nc.dram_tensor("t_prop", (2 * SLOTS, F), F32, kind="Internal").ap()
    t_x2 = nc.dram_tensor("t_x2", (2 * SLOTS, F), F32, kind="Internal").ap()
    t_x3 = nc.dram_tensor("t_x3", (2 * SLOTS, F), F32, kind="Internal").ap()
    t_pair = nc.dram_tensor("t_pair", (SLOTS, ROW), F32, kind="Internal").ap()

    ctx = ExitStack()
    with ctx:
        def sb(name, shape, dt=F32):
            return ctx.enter_context(nc.sbuf_tensor(name, shape, dt))

        def ps(name, shape):
            return ctx.enter_context(nc.psum_tensor(name, shape, F32))

        def sem(name):
            return ctx.enter_context(nc.semaphore(name))

        big = sb("big", [P, 2 * COLS * ROW])
        XS = big[:, 0:COLS * ROW].rearrange("p (t w) -> p t w", w=ROW)
        XD = big[:, COLS * ROW:].rearrange("p (t w) -> p t w", w=ROW)
        G = sb("gathered", [P, COLS, F])
        V = sb("sums", [P, COLS + 1, F])
        B = sb("own_term", [P, COLS, F])
        G16 = G[:, :, :].rearrange("p t f -> p (t f)")[:, 0:COLS * HID].rearrange("p (t f) -> p t f", f=HID)
        HW = B[:, :, 0:HID]
        Z16 = B[:, :, HID:2 * HID]

        SI = sb("src_i", [P, COLS], I32)
        DI = sb("dst_i", [P, COLS], I32)
        key_s = sb("src_f", [P, COLS])
        key_d = sb("dst_f", [P, COLS])
        key_p = sb("sorted_src_f", [P, COLS])
        dig = sb("digit_f", [P, COLS])
        pos = sb("position", [P, COLS])
        idx = sb("index_i", [P, COLS], I32)
        idx_q = sb("lookup_i", [P, COLS], I32)
        dig_i = idx_q
        idx_perm = sb("perm_i", [P, COLS], I32)
        idx_outd = sb("out_dst_i", [P, COLS], I32)
        idx_outs = sb("out_src_i", [P, COLS], I32)
        pay = sb("payload", [P, COLS, 2])
        iota_e = sb("edge_number", [P, COLS])
        iota_d = sb("digit_values", [P, HIGH])
        hist = sb("histogram", [P, HIGH])
        rank = sb("next_rank", [P, HIGH])
        junk = sb("junk", [P, HIGH])
        ident = sb("identity", [P, P])
        later = sb("later", [P, P])
        earlier = sb("earlier", [P, P])
        ones = sb("ones", [P, P])
        kb = sb("key_columns", [P, P])
        nf = sb("next_first", [P, 2])
        seg = {}
        for s in "dp":
            for n in ("same", "last", "notlast", "head", "tail"):
                seg[s, n] = sb(f"{n}_{s}", [P, COLS])
            seg[s, "fwd"] = sb(f"fwd_{s}", [P, P])
            seg[s, "bwd"] = sb(f"bwd_{s}", [P, P])
        neg_same, neg_head = key_s, key_d
        neg_bwd = sb("neg_bwd", [P, P])
        roots = sb("roots", [P, 5, COLS])
        inv = sb("inverse_roots", [P, 5, COLS])
        GCN_S, GCN_D, IN_D, OUT_S, OUT_D = range(5)
        a_d = sb("prop_scale", [P, COLS])
        hasnot = sb("no_incoming", [P, COLS])
        hc = sb("staged", [P, CHUNK * F])
        hT = sb("staged_turned", [P, CHUNK * F])
        xc = sb("centred", [P, CHUNK, F])
        sq = hc[:, :].rearrange("p (t f) -> p t f", f=F)
        mean = sb("mean", [P, CHUNK])
        var = sb("variance", [P, CHUNK])
        std = sb("std", [P, CHUNK])
        rstd = sb("rstd", [P, CHUNK])
        gS = sb("local_rows", [P, CHUNK, F])
        carry = sb("carry", [P, F])
        eps = sb("eps", [P, 1])
        zero = sb("zero", [P, 8])
        w1bd = sb("w1_blocks", [P, GROUP * HID])
        w2bd = sb("w2_blocks", [7 * HID, 7 * F])
        wsp = sb("w_spline_rows", [P, BASIS * BASIS * F])
        wg = sb("w_gat_rows", [P, HEADS, F])
        wsum = sb("w_att", [P, 2, HEADS])
        prod = sb("prod", [P, 512])
        wa_s = sb("w_att_src_blocks", [P, GROUP * HEADS])
        wa_d = sb("w_att_dst_blocks", [P, GROUP * HEADS])
        b1r = sb("b1_rows", [P, HID])
        b2r = sb("b2_rows", [P, F])
        br = sb("bias_rows", [P, F])
        fcr = sb("fc_rows", [P, 2 * F])
        fbr = sb("fc_bias_rows", [P, 1])
        ea = sb("edge_attr", [P, COLS, 2])
        tent = sb("tents", [P, CHUNK, 2 * BASIS])
        basis = sb("basis", [P, CHUNK, BASIS * BASIS])
        sc4 = sb("scores", [P, COLS, HEADS])
        v4 = sb("per_segment", [P, COLS + 1, HEADS])
        w4 = sb("whole_segment", [P, COLS + 1, HEADS])
        dx = sb("dense_x", [P, DN, F])
        dx1 = sb("dense_x1", [P, DN, F])
        dout = sb("dense_out", [P, DN, F])

        psT = ps("turned", [P, 1024])
        psY = ps("products", [P, 1024])
        psB = [ps(f"wide{i}", [P, 512]) for i in range(4)]

        names = ("loads zeroed patterns weights_placed node_rows_done keys_ready keys_turned shift_done "
                 "hist_ready base_ready order_ready table_ready sorted_done info_scattered cols_ready "
                 "roots_ready roots_done var_ready std_ready h_ready ht_ps ht_sb y_ready "
                 "tail_ready carry_ready rows_ready rows_stored lookup_ready wide_ready wide_used "
                 "att_ready att_done exp_ready exp_done dense_in dense_used dense_ready dense_stored "
                 "out_rows_ready pay_ready reloaded own_kept local_ready local_stored rounds").split()
        S = {n: sem(n) for n in names}
        chunk_sem = [sem(f"gather_chunk{c}") for c in range(CHUNKS)]
        scat = sem("scattered")

        def bc(ap, n):
            return ap.unsqueeze(2).to_broadcast([ap.shape[0], ap.shape[1], n])

        def bt(ap, t):
            return ap.unsqueeze(1).to_broadcast([ap.shape[0], t, ap.shape[1]])

        order = [("s1", CHUNKS, 1, ("w1",)), ("d1", CHUNKS, 1, ("w1",)), ("s1b", CHUNKS, 0, ("w2",)),
                 ("d1b", CHUNKS, 0, ("w2",)), ("h1s", CHUNKS, 1, ()), ("h1d", CHUNKS, 1, ()),
                 ("dense", DSTEPS, 2, ("w1", "w2")), ("dense_rest", 1, 2, ("w1", "w2")),
                 ("spline", CHUNKS, 1, ("wide",)),
                 ("att", CHUNKS, 2, ("was", "wad")), ("msg", CHUNKS, 0, ("hp",))]
        ln0, lin0, y0 = {}, {}, {}
        a = b = d = 0
        for n, times, lns, kinds in order:
            ln0[n], lin0[n], y0[n] = a, b, d
            a += times * lns
            d += times * len(kinds) * (kinds not in (("wide",), ("hp",)))
            b += times * len(kinds)
        gathers = ["xs", "xd", "g", "x1"] + [f"f{k}" for k in range(1, STEPS)] + ["pair", "x2", "x3"]
        col0 = {n: i * CHUNKS for i, n in enumerate(gathers)}

        block = ctx.enter_context(nc.Block())

        @block.sync
        def _(sp):
            L = S["loads"]
            sp.wait_ge(S["zeroed"], 1)
            n = 0
            for tile, arr in ((SI, src), (DI, dst)):
                sp.dma_start(tile[0:FULL_ROWS, :], arr[0:FULL_ROWS * COLS].rearrange("(p t) -> p t", t=COLS)).then_inc(L, 16)
                sp.dma_start(tile[FULL_ROWS:FULL_ROWS + 1, 0:REST], arr[FULL_ROWS * COLS:E].rearrange("(p t) -> p t", t=REST)).then_inc(L, 16)
            sp.dma_start(ea[0:FULL_ROWS, :, :], edge_attr[0:FULL_ROWS * COLS, :].rearrange("(p t) c -> p t c", t=COLS)).then_inc(L, 16)
            sp.dma_start(ea[FULL_ROWS:FULL_ROWS + 1, 0:REST, :], edge_attr[FULL_ROWS * COLS:E, :].rearrange("(p t) c -> p t c", t=REST)).then_inc(L, 16)
            for g in range(GROUP):
                sp.dma_start(w1bd[g * F:(g + 1) * F, g * HID:(g + 1) * HID], W1).then_inc(L, 16)
                sp.dma_start(wsp[g * F:(g + 1) * F, :].rearrange("p (k o) -> p k o", o=F), w_spline.rearrange("a b f o -> f (a b) o")).then_inc(L, 16)
                sp.dma_start(wg[g * F:(g + 1) * F, :, :], w_gat.rearrange("h f o -> f h o")).then_inc(L, 16)
            for g in range(7):
                sp.dma_start(w2bd[g * HID:(g + 1) * HID, g * F:(g + 1) * F], W2).then_inc(L, 16)
            for tile, arr in ((b1r, b1), (b2r, b2), (br, bias), (fbr, fc_b)):
                sp.dma_start(tile[:, :], arr.partition_broadcast(P)).then_inc(L, 16)
            sp.dma_start(fcr[:, :], fc_w[0, :].partition_broadcast(P)).then_inc(L, 16)
            sp.dma_start(nodes[0:N, 0:F], x).then_inc(S["node_rows_done"], 16)
            sp.dma_start(nodes[0:N, F:ROW].rearrange("(p t) w -> p t w", p=32), zero[0:32, 0:4].unsqueeze(1).to_broadcast([32, N // 32, 4])).then_inc(S["node_rows_done"], 16)
            sp.dma_start(nodes[N:NODES, :].rearrange("r (a w) -> r a w", w=4), zero[0:NODES - N, 0:4].unsqueeze(1).to_broadcast([NODES - N, ROW // 4, 4])).then_inc(S["node_rows_done"], 16)
            for i, key in enumerate((key_d, key_p)):
                sp.wait_ge(S["keys_ready"], i + 1)
                sp.dma_start(nf[0:P - 1, i:i + 1], key[1:P, 0:1]).then_inc(S["shift_done"], 16)
                if i == 0:
                    for k, table in enumerate((sort1, sort2)):
                        sp.wait_ge(S["sorted_done"], k + 1)
                        sp.dma_start(pay[:, :, :], table.rearrange("(p t) c -> p t c", t=COLS)).then_inc(S["reloaded"], 16)
            stored = 0
            locals_ = 0

            def store_local(table, width, chunks=CHUNKS):
                nonlocal locals_
                tail = table[SLOTS:2 * SLOTS, :].rearrange("(p t) w -> p t w", t=COLS)
                with sp.Fori(0, CHUNKS) as c:
                    sp.wait_ge(S["local_ready"], c + (locals_ + 1))
                    sp.dma_start(tail[:, ds(c * CHUNK, CHUNK), :], gS[:, :, 0:width]).then_inc(S["local_stored"], 16)
                locals_ += CHUNKS

            def store_rows(table, tile, rows_ready):
                sp.wait_ge(S["rows_ready"], rows_ready)
                sp.dma_start(table, tile).then_inc(S["rows_stored"], 16)

            def front(table):
                return table[0:SLOTS, :].rearrange("(p t) w -> p t w", t=COLS)

            def back(table):
                return table[SLOTS:2 * SLOTS, :].rearrange("(p t) w -> p t w", t=COLS)

            store_local(t_gcn, HID)
            store_rows(front(t_gcn), G16, 1)
            store_local(t_x1, F)
            store_rows(front(t_x1), V[:, 1:, :], 2)
            store_local(t_prop, F)
            store_rows(front(t_prop), V[:, 1:, :], 3)
            store_rows(back(t_x2), XS[:, :, 0:F], 3)

            def span(arr, k):
                return arr[ds(k * P * DN, P * DN), :].rearrange("(p t) f -> p t f", t=DN)

            rest_in, rest_out = (a_[DSTEPS * P * DN:N, :].rearrange("(p t) f -> p t f", t=GROUP) for a_ in (x, out))
            sp.dma_start(dx[:, :, :], span(x, 0)).then_inc(S["dense_in"], 16)
            with sp.Fori(0, DSTEPS - 1) as k:
                sp.wait_ge(S["dense_used"], k + 1)
                sp.dma_start(dx[:, :, :], span(x, k + 1)).then_inc(S["dense_in"], 16)
                sp.wait_ge(S["dense_ready"], k + 1)
                sp.dma_start(span(out, k), dout[:, :, :]).then_inc(S["dense_stored"], 16)
            sp.wait_ge(S["dense_used"], DSTEPS)
            sp.dma_start(dx[0:RP, 0:GROUP, :], rest_in).then_inc(S["dense_in"], 16)
            sp.wait_ge(S["dense_ready"], DSTEPS)
            sp.dma_start(span(out, DSTEPS - 1), dout[:, :, :]).then_inc(S["dense_stored"], 16)
            sp.wait_ge(S["dense_ready"], DSTEPS + 1)
            sp.dma_start(rest_out, dout[0:RP, 0:GROUP, :]).then_inc(S["dense_stored"], 16)
            with sp.Fori(0, STEPS - 2) as r:
                sp.wait_ge(S["rows_ready"], r + 4)
                sp.dma_start(front(t_prop), V[:, 1:, :]).then_inc(S["rows_stored"], 16)
            store_rows(front(t_x2), V[:, 1:, :], STEPS + 3)
            store_rows(t_pair.rearrange("(p t) w -> p t w", t=COLS), XD, STEPS + 4)
            store_rows(back(t_x3), XS[:, :, 0:F], STEPS + 5)
            store_rows(front(t_x3), V[:, 1:, :], STEPS + 5)

        @block.scalar
        def _(act):
            def roots_step():
                act.wait_ge(S["roots_ready"], 1)
                nc.scalar.activation(roots[:, :, :], roots[:, :, :], ACT.Sqrt).then_inc(S["roots_done"], 1)

            def norm(n, k, width):
                act.wait_ge(S["var_ready"], k)
                nc.scalar.activation(std[0:n, 0:width], var[0:n, 0:width], ACT.Sqrt, bias=eps[0:n, :], scale=1.0 / F).then_inc(S["std_ready"], 1)

            def turned(rows, cols, k):
                act.wait_ge(S["ht_ps"], k)
                nc.scalar.copy(hT[0:rows, 0:cols], psT[0:rows, 0:cols]).then_inc(S["ht_sb"], 1)

            roots_step()
            for st in ("s1", "d1"):
                with act.Fori(0, CHUNKS) as c:
                    norm(P, c + (ln0[st] + 1), CHUNK)
                    turned(P, CHUNK * F, c + (lin0[st] + 1))
            for st in ("s1b", "d1b"):
                with act.Fori(0, CHUNKS) as c:
                    turned(7 * HID, 4 * P, c + (lin0[st] + 1))
            for st in ("h1s", "h1d"):
                with act.Fori(0, CHUNKS) as c:
                    norm(P, c + (ln0[st] + 1), CHUNK)

            def dense_step(st, k, rows, cols):
                norm(rows, k * 2 + (ln0[st] + 1), cols)
                turned(P, (cols // GROUP) * P if rows == P else rows, k * 2 + (lin0[st] + 1))
                turned(min(cols, 6) * HID, (cols // 6) * P if rows == P else rows, k * 2 + (lin0[st] + 2))
                norm(rows, k * 2 + (ln0[st] + 2), cols)

            with act.Fori(0, DSTEPS) as k:
                dense_step("dense", k, P, DN)
            dense_step("dense_rest", 0, RP, GROUP)
            with act.Fori(0, CHUNKS) as c:
                norm(P, c + (ln0["spline"] + 1), CHUNK)
                turned(P, CHUNK * F, c + (lin0["spline"] + 1))
            with act.Fori(0, CHUNKS) as c:
                norm(P, c * 2 + (ln0["att"] + 1), CHUNK)
                turned(P, CHUNK * F, c * 2 + (lin0["att"] + 1))
                norm(P, c * 2 + (ln0["att"] + 2), CHUNK)
                turned(P, CHUNK * F, c * 2 + (lin0["att"] + 2))
            act.wait_ge(S["exp_ready"], 1)
            nc.scalar.activation(sc4[:, :, :], sc4[:, :, :], ACT.Exp).then_inc(S["exp_done"], 1)
            with act.Fori(0, CHUNKS) as c:
                turned(P, CHUNK * F, c + (lin0["msg"] + 1))

        @block.tensor
        def _(pe):
            pe.wait_ge(S["patterns"], 1)
            pe.wait_ge(S["loads"], 16 * 30)

            def key_matrices(k):
                for j in range(2):
                    pe.wait_ge(S["tail_ready"], k + j + 1)
                    nc.tensor.transpose(psT[:, 0:P], kb[:, :], ident[:, :]).then_inc(S["carry_ready"], 1)

            def carry_row(k, M, rhs, w):
                pe.wait_ge(S["tail_ready"], k)
                nc.tensor.matmul(psY[:, 0:w], M[:, :], rhs, start=True, stop=True).then_inc(S["carry_ready"], 1)

            def turn_max(k):
                pe.wait_ge(S["tail_ready"], k)
                nc.tensor.transpose(psT[:, 0:P], kb[:, :], ident[:, :]).then_inc(S["carry_ready"], 1)

            def ranks(k, width):
                pe.wait_ge(S["hist_ready"], k)
                nc.tensor.matmul(psT[:, 0:width], later[:, :], hist[:, 0:width], start=True, stop=True)
                nc.tensor.matmul(psT[:, 512:512 + width], ones[:, :], hist[:, 0:width], start=True, stop=True).then_inc(S["base_ready"], 1)

            def turn(n, groups, gw, k):
                pe.wait_ge(S["h_ready"], k)
                for g in range(groups):
                    i = nc.tensor.transpose(psT[0:gw, g * P:g * P + n], hc[0:n, g * gw:(g + 1) * gw], ident[0:n, 0:n])
                i.then_inc(S["ht_ps"], 1)
                pe.wait_ge(S["ht_sb"], k)

            def lin(n, cols, kind, k):
                if kind == "w1":
                    turn(n, cols // GROUP, GROUP * F, k)
                    for g in range(cols // GROUP):
                        i = nc.tensor.matmul(psY[0:n, g * GROUP * HID:(g + 1) * GROUP * HID], hT[:, g * P:g * P + n], w1bd[:, :], start=True, stop=True)
                elif kind == "w2":
                    m = 7 if cols == CHUNK else min(cols, 6)
                    turn(n, cols // m, m * HID, k)
                    for g in range(cols // m):
                        o = (g // 2) * 512 + (g % 2) * m * F
                        i = nc.tensor.matmul(psY[0:n, o:o + m * F], hT[0:m * HID, g * P:g * P + n], w2bd[0:m * HID, 0:m * F], start=True, stop=True)
                elif kind in ("was", "wad"):
                    turn(n, cols // GROUP, GROUP * F, k)
                    w = wa_s if kind == "was" else wa_d
                    for g in range(cols // GROUP):
                        i = nc.tensor.matmul(psY[0:n, g * GROUP * HEADS:(g + 1) * GROUP * HEADS], hT[:, g * P:g * P + n], w[:, :], start=True, stop=True)
                i.then_inc(S["y_ready"], 1)

            def wide(c, st):
                w = wsp if st == "spline" else wg[:, :, :].rearrange("p h o -> p (h o)")
                width = BASIS * BASIS * F if st == "spline" else HEADS * F
                turn(P, CHUNK // GROUP, GROUP * F, c + (lin0[st] + 1))
                first = 0 if st == "spline" else COLS
                for t in range(CHUNK):
                    q = t % GROUP
                    if t >= 4:
                        pe.wait_ge(S["wide_used"], c * CHUNK + (first + t - 3))
                    i = nc.tensor.matmul(psB[t % 4][:, 0:width], hT[q * F:(q + 1) * F, (t // GROUP) * P:(t // GROUP + 1) * P],
                                         w[q * F:(q + 1) * F, :], start=True, stop=True)
                    i.then_inc(S["wide_ready"], 1)

            key_matrices(0)
            carry_row(3, seg["d", "fwd"], V[:, COLS, 0:1], 1)
            ranks(1, DIGIT)
            ranks(2, HIGH)
            key_matrices(3)
            carry_row(6, seg["p", "fwd"], V[:, COLS, 0:1], 1)
            with pe.Fori(0, CHUNKS) as c:
                lin(P, CHUNK, "w1", c + (lin0["s1"] + 1))
            carry_row(7, seg["d", "fwd"], V[:, COLS, 0:HID], HID)
            with pe.Fori(0, CHUNKS) as c:
                lin(P, CHUNK, "w1", c + (lin0["d1"] + 1))
            with pe.Fori(0, CHUNKS) as c:
                lin(P, CHUNK, "w2", c + (lin0["s1b"] + 1))
            carry_row(8, seg["d", "fwd"], V[:, COLS, 0:HID], HID)
            with pe.Fori(0, CHUNKS) as c:
                lin(P, CHUNK, "w2", c + (lin0["d1b"] + 1))
            carry_row(9, seg["d", "fwd"], V[:, COLS, :], F)
            with pe.Fori(0, DSTEPS) as k:
                lin(P, DN, "w1", k * 2 + (lin0["dense"] + 1))
                lin(P, DN, "w2", k * 2 + (lin0["dense"] + 2))
            lin(RP, GROUP, "w1", lin0["dense_rest"] + 1)
            lin(RP, GROUP, "w2", lin0["dense_rest"] + 2)
            with pe.Fori(0, STEPS - 1) as r:
                carry_row(r + 10, seg["d", "fwd"], V[:, COLS, :], F)
            carry_row(STEPS + 9, seg["d", "bwd"], XD[:, 0, 0:F], F)
            with pe.Fori(0, CHUNKS) as c:
                wide(c, "spline")
            k = STEPS + 10
            carry_row(k, seg["p", "fwd"], V[:, COLS, :], F)
            carry_row(k + 1, seg["p", "bwd"], G[:, 0, :], F)
            with pe.Fori(0, CHUNKS) as c:
                lin(P, CHUNK, "was", c * 2 + (lin0["att"] + 1))
                lin(P, CHUNK, "wad", c * 2 + (lin0["att"] + 2))
            k += 2
            for h in range(HEADS):
                turn_max(k + h)
            k += HEADS
            carry_row(k, seg["p", "bwd"], w4[:, 0, :], HEADS)
            carry_row(k + 1, seg["p", "fwd"], v4[:, COLS, :], HEADS)
            carry_row(k + 2, seg["p", "bwd"], w4[:, 0, :], HEADS)
            with pe.Fori(0, CHUNKS) as c:
                wide(c, "msg")
            carry_row(k + 3, seg["p", "fwd"], V[:, COLS, :], F)

        @block.gpsimd
        def _(pool):
            pool.iota(iota_e[:, :], [[1, COLS]], base=0, channel_multiplier=COLS, allow_small_or_imprecise_dtypes=True)
            pool.iota(iota_d[:, :], [[1, HIGH]], base=0, channel_multiplier=0, allow_small_or_imprecise_dtypes=True)
            pool.memset(ones[:, :], 1.0)
            pool.drain()
            pool.affine_select(out=later[:, :], in_=ones[:, :], compare_op=ALU.is_gt, fill=0.0, base=0, pattern=[[1, P]], channel_multiplier=-1)
            pool.affine_select(out=earlier[:, :], in_=ones[:, :], compare_op=ALU.is_gt, fill=0.0, base=0, pattern=[[-1, P]], channel_multiplier=1)
            pool.affine_select(out=ident[:, :], in_=ones[:, :], compare_op=ALU.is_equal, fill=0.0, base=0, pattern=[[-1, P]], channel_multiplier=1)
            pool.drain().then_inc(S["patterns"], 1)

            def offs(t, i):
                return bass.IndirectOffsetOnAxis(ap=i[:, t:t + 1], axis=0)

            def scatter(view, i, rows, limit, done, value):
                for t in range(COLS):
                    pool.indirect_dma_start(view, offs(t, i), rows(t), None, bounds_check=limit, oob_is_err=False).then_inc(scat, 16)
                pool.wait_ge(scat, 16 * COLS * value)
                pool.sem_inc(done, 1)

            def gather(table, i, cols, times, count):
                for c in range(CHUNKS + 1):
                    if c < CHUNKS:
                        for t in range(c * CHUNK, (c + 1) * CHUNK):
                            pool.indirect_dma_start(cols(t), None, table, offs(t, i)).then_inc(chunk_sem[c], 16)
                    if c > 0:
                        pool.wait_ge(chunk_sem[c - 1], count)
                        pool.sem_inc(S["cols_ready"], 1)

            per = 16 * CHUNK
            info_limit = NODES * (ROW // 2) - 1
            pool.wait_ge(S["node_rows_done"], 48)
            pool.wait_ge(S["pay_ready"], 1)
            scatter(nodes.rearrange("n (a w) -> (n a) w", w=2), idx, lambda t: pay[:, t, :], info_limit, S["info_scattered"], 1)
            pool.wait_ge(S["pay_ready"], 2)
            scatter(sort1, idx, lambda t: pay[:, t, :], SLOTS - 1, S["sorted_done"], 2)
            pool.wait_ge(S["pay_ready"], 3)
            scatter(sort2, idx, lambda t: pay[:, t, :], SLOTS - 1, S["sorted_done"], 3)
            pool.wait_ge(S["pay_ready"], 4)
            scatter(nodes.rearrange("n (a w) -> (n a) w", w=2), idx, lambda t: pay[:, t, :], info_limit, S["info_scattered"], 4)

            gather(nodes, SI, lambda t: XS[:, t, :], 0, per)
            gather(nodes, DI, lambda t: XD[:, t, :], 0, 2 * per)
            pool.wait_ge(S["lookup_ready"], 1)
            pool.wait_ge(S["local_stored"], 16 * CHUNKS)
            pool.wait_ge(S["rows_stored"], 16)
            pool.wait_ge(S["own_kept"], 1)
            gather(t_gcn, idx_q, lambda t: G16[:, t, :], 0, 3 * per)
            pool.wait_ge(S["local_stored"], 32 * CHUNKS)
            pool.wait_ge(S["rows_stored"], 32)
            gather(t_x1, idx_q, lambda t: G[:, t, :], 0, 4 * per)
            pool.wait_ge(S["local_stored"], 48 * CHUNKS)
            with pool.Fori(0, STEPS - 1) as r:
                pool.wait_ge(S["rows_stored"], r * 16 + 64)
                pool.sem_inc(S["rounds"], 1)
                gather(t_prop, idx_q, lambda t: G[:, t, :], 0, r * per + 5 * per)
            n = 4 + STEPS - 1
            pool.wait_ge(S["rows_stored"], 16 * (STEPS + 4))
            gather(t_pair, idx_perm, lambda t: XS[:, t, :], 0, (n + 1) * per)
            pool.wait_ge(S["lookup_ready"], 2)
            gather(t_x2, idx_q, lambda t: G[:, t, :], 0, (n + 2) * per)
            pool.wait_ge(S["dense_stored"], 16 * (DSTEPS + 1))
            pool.wait_ge(S["out_rows_ready"], 1)
            scatter(out, idx_outd, lambda t: B[:, t, :], N - 1, S["info_scattered"], 5)
            pool.wait_ge(S["rows_stored"], 16 * (STEPS + 6))
            gather(t_x3, SI, lambda t: XS[:, t, 0:F], 0, (n + 3) * per)
            pool.wait_ge(S["out_rows_ready"], 2)
            scatter(out, idx_outs, lambda t: V[:, t + 1, :], N - 1, S["info_scattered"], 6)

        @block.vector
        def _(v):
            state = {"tail": 0, "cols": 0, "local": 0, "wide": 0}
            TT, TS, STT = v.tensor_tensor, v.tensor_scalar, v.scalar_tensor_tensor

            def D():
                v.drain()

            def signal(name):
                v.drain().then_inc(S[name], 1)

            def ask():
                state["tail"] += 1
                signal("tail_ready")
                v.wait_ge(S["carry_ready"], state["tail"])

            v.memset(SI[:, :], N)
            v.memset(DI[:, :], N)
            v.memset(ea[:, :, :], 0.0)
            v.memset(w1bd[:, :], 0.0)
            v.memset(w2bd[:, :], 0.0)
            v.memset(zero[:, :], 0.0)
            v.memset(eps[:, :], EPS)
            v.memset(nf[:, :], -1.0)
            signal("zeroed")
            v.memset(V[:, 0, :], 0.0)
            v.memset(v4[:, 0, :], 0.0)
            v.memset(w4[:, COLS, :], 0.0)
            v.wait_ge(S["patterns"], 1)
            v.wait_ge(S["loads"], 16 * 30)
            v.tensor_copy(key_s[:, :], SI[:, :])
            v.tensor_copy(key_d[:, :], DI[:, :])
            for side in range(2):
                D()
                TT(prod[:, 0:HEADS * F].rearrange("p (h o) -> p h o", o=F), wg[:, :, :], bt(fcr[:, side * F:(side + 1) * F], HEADS), ALU.mult)
                D()
                v.tensor_reduce(wsum[:, side, :], prod[:, 0:HEADS * F].rearrange("p (h o) -> p h o", o=F), AX.X, ALU.add)
                D()
                w = (wa_s, wa_d)[side]
                v.memset(w[:, :], 0.0)
                D()
                for g in range(GROUP):
                    v.tensor_copy(w[g * F:(g + 1) * F, g * HEADS:(g + 1) * HEADS], wsum[g * F:(g + 1) * F, side, :])
            D()

            def segments(s, key, i):
                g = lambda n: seg[s, n]
                signal("keys_ready")
                v.memset(g("same")[:, 0:1], 0.0)
                TT(g("same")[:, 1:COLS], key[:, 1:COLS], key[:, 0:COLS - 1], ALU.is_equal)
                TT(g("last")[:, 0:COLS - 1], key[:, 1:COLS], key[:, 0:COLS - 1], ALU.not_equal)
                v.wait_ge(S["shift_done"], 16 * (i + 1))
                TT(g("last")[:, COLS - 1:COLS], key[:, COLS - 1:COLS], nf[:, i:i + 1], ALU.not_equal)
                D()
                TS(g("notlast")[:, :], g("last")[:, :], -1.0, 1.0, ALU.mult, ALU.add)
                D()
                TS(g("head")[:, :], key[:, :], key[:, 0:1], None, ALU.is_equal)
                TS(g("tail")[:, :], key[:, :], key[:, COLS - 1:COLS], g("notlast")[:, COLS - 1:COLS], ALU.is_equal, ALU.mult)
                v.tensor_copy(kb[:, :], key[:, 0:1].to_broadcast([P, P]))
                ask()
                STT(g("fwd")[:, :], psT[:, 0:P], key[:, COLS - 1:COLS], later[:, :], ALU.is_equal, ALU.mult)
                v.tensor_copy(kb[:, :], key[:, COLS - 1:COLS].to_broadcast([P, P]))
                ask()
                STT(g("bwd")[:, :], psT[:, 0:P], key[:, 0:1], earlier[:, :], ALU.is_equal, ALU.mult)
                D()

            def scan(s, c, src_, dst_, width, n=CHUNK):
                t0 = c * n
                for f in range(width):
                    v.tensor_tensor_scan(dst_[:, ds(t0 + 1, n), f], seg[s, "same"][:, ds(t0, n)], src_[:, ds(t0, n), f],
                                         dst_[:, ds(t0, 1), f], ALU.mult, ALU.add)
                D()

            def carry_in(s, tile, tmp, width):
                ask()
                v.tensor_copy(carry[:, 0:width], psY[:, 0:width])
                D()
                TT(tmp, bc(seg[s, "head"][:, :], width), bt(carry[:, 0:width], COLS), ALU.mult)
                D()
                TT(tile, tile, tmp, ALU.add)
                D()

            def spread(s, src_, tmp, dst_, width):
                TT(tmp, src_, bc(seg[s, "last"][:, :], width), ALU.mult)
                D()
                for f in range(width):
                    v.tensor_tensor_scan(dst_[:, COLS - 1::-1, f] if dst_.shape[1] == COLS else dst_[:, COLS - 1::-1, f],
                                         seg[s, "notlast"][:, ::-1], tmp[:, ::-1, f], 0.0, ALU.mult, ALU.add)
                D()
                ask()
                v.tensor_copy(carry[:, 0:width], psY[:, 0:width])
                D()
                TT(tmp, bc(seg[s, "tail"][:, :], width), bt(carry[:, 0:width], COLS), ALU.mult)
                D()
                TT(dst_[:, 0:COLS, :], dst_[:, 0:COLS, :], tmp, ALU.add)
                D()

            def count_segments(s):
                v.memset(pos[:, :], 1.0)
                D()
                v.tensor_tensor_scan(V[:, 1:COLS + 1, 0], seg[s, "same"][:, :], pos[:, :], 0.0, ALU.mult, ALU.add)
                ask()
                v.tensor_copy(carry[:, 0:1], psY[:, 0:1])
                D()
                STT(pos[:, :], seg[s, "head"][:, :], carry[:, 0:1], V[:, 1:COLS + 1, 0], ALU.mult, ALU.add)
                D()

            def at_last(s, key, mult, add, index):
                TS(dig[:, :], key[:, :], float(mult), float(add) - NOWHERE, ALU.mult, ALU.add)
                D()
                TT(dig[:, :], dig[:, :], seg[s, "last"][:, :], ALU.mult)
                D()
                TS(index[:, :], dig[:, :], NOWHERE, None, ALU.add)
                D()

            segments("d", key_d, 0)
            count_segments("d")
            v.tensor_copy(pay[:, :, 1], pos[:, :])
            TS(pay[:, :, 0], iota_e[:, :], 1.0, None, ALU.add)
            at_last("d", key_d, ROW // 2, INFO // 2, idx)
            at_last("d", key_d, 1, 0, idx_outd)
            signal("pay_ready")

            def digit_pass(k, width):
                UN = 7
                v.memset(hist[:, 0:width], 0.0)
                D()
                with v.Fori(0, COLS // UN) as t:
                    for u in range(UN):
                        STT(hist[:, 0:width], iota_d[:, 0:width], dig[:, ds(t * UN + u, 1)], hist[:, 0:width], ALU.is_equal, ALU.add)
                        D()
                signal("hist_ready")
                v.wait_ge(S["base_ready"], k)
                v.tensor_copy(junk[:, 0:width], psT[:, 512:512 + width])
                v.memset(hist[:, 0:width], 1.0)
                D()
                v.tensor_tensor_scan(rank[:, 0:width], hist[:, 0:width], junk[:, 0:width], 0.0, ALU.mult, ALU.add)
                D()
                TT(rank[:, 0:width], rank[:, 0:width], junk[:, 0:width], ALU.subtract)
                D()
                TT(rank[:, 0:width], rank[:, 0:width], psT[:, 0:width], ALU.add)
                D()
                with v.Fori(0, COLS // UN) as t:
                    for u in range(UN):
                        STT(junk[:, 0:width], iota_d[:, 0:width], dig[:, ds(t * UN + u, 1)], rank[:, 0:width], ALU.is_equal, ALU.mult,
                            accum_out=pos[:, ds(t * UN + u, 1)])
                        STT(rank[:, 0:width], iota_d[:, 0:width], dig[:, ds(t * UN + u, 1)], rank[:, 0:width], ALU.is_equal, ALU.add)
                        D()

            TS(dig_i[:, :], SI[:, :], DIGIT - 1, None, ALU.bitwise_and)
            D()
            v.tensor_copy(dig[:, :], dig_i[:, :])
            D()
            digit_pass(1, DIGIT)
            v.wait_ge(S["info_scattered"], 1)
            v.tensor_copy(idx[:, :], pos[:, :])
            v.tensor_copy(pay[:, :, 0], key_s[:, :])
            v.tensor_copy(pay[:, :, 1], iota_e[:, :])
            signal("pay_ready")
            v.wait_ge(S["reloaded"], 16)
            v.tensor_copy(dig_i[:, :], pay[:, :, 0])
            D()
            TS(dig_i[:, :], dig_i[:, :], 8, None, ALU.logical_shift_right)
            D()
            v.tensor_copy(dig[:, :], dig_i[:, :])
            D()
            digit_pass(2, HIGH)
            v.tensor_copy(idx[:, :], pos[:, :])
            signal("pay_ready")
            v.wait_ge(S["reloaded"], 32)
            v.tensor_copy(key_p[:, :], pay[:, :, 0])
            v.tensor_copy(idx_perm[:, :], pay[:, :, 1])
            D()
            segments("p", key_p, 1)
            count_segments("p")
            v.tensor_copy(pay[:, :, 0], pos[:, :])
            TS(pay[:, :, 1], iota_e[:, :], 1.0, None, ALU.add)
            at_last("p", key_p, ROW // 2, INFO // 2 + 1, idx)
            at_last("p", key_p, 1, 0, idx_outs)
            signal("pay_ready")

            v.wait_ge(S["cols_ready"], 2 * CHUNKS)
            TS(roots[:, GCN_S, :], XS[:, :, INFO + 1], 1.0, None, ALU.add)
            TS(roots[:, GCN_D, :], XD[:, :, INFO + 1], 1.0, None, ALU.add)
            TS(roots[:, IN_D, :], XD[:, :, INFO + 1], 1.0, None, ALU.max)
            TS(roots[:, OUT_S, :], XS[:, :, INFO + 2], 1.0, None, ALU.max)
            TS(roots[:, OUT_D, :], XD[:, :, INFO + 2], 1.0, None, ALU.max)
            signal("roots_ready")

            def lookup(last, index):
                TS(hasnot[:, :], last, 0.0, None, ALU.is_equal)
                TS(dig[:, :], iota_e[:, :], float(SLOTS), None, ALU.add)
                D()
                TT(dig[:, :], dig[:, :], hasnot[:, :], ALU.mult)
                D()
                TT(dig[:, :], dig[:, :], last, ALU.add)
                D()
                TT(dig[:, :], dig[:, :], hasnot[:, :], ALU.add)
                D()
                TS(dig[:, :], dig[:, :], -1.0, None, ALU.add)
                D()
                v.tensor_copy(index[:, :], dig[:, :])

            lookup(XS[:, :, INFO], idx_q)
            v.tensor_copy(pos[:, :], dig[:, :])
            signal("lookup_ready")
            v.wait_ge(S["roots_done"], 1)
            v.reciprocal(inv[:, :, :], roots[:, :, :])
            D()
            STT(a_d[:, :], inv[:, IN_D, :], 1.0 - ALPHA, inv[:, OUT_D, :], ALU.mult, ALU.mult)
            D()

            def norm(n, X, cols, k, o):
                v.tensor_reduce(mean[0:n, 0:cols], X, AX.X, ALU.add)
                D()
                STT(xc[0:n, 0:cols, :], bc(mean[0:n, 0:cols], F), -1.0 / F, X, ALU.mult, ALU.add)
                D()
                TT(sq[0:n, 0:cols, :], xc[0:n, 0:cols, :], xc[0:n, 0:cols, :], ALU.mult)
                D()
                v.tensor_reduce(var[0:n, 0:cols], sq[0:n, 0:cols, :], AX.X, ALU.add)
                signal("var_ready")
                v.wait_ge(S["std_ready"], k)
                v.reciprocal(rstd[0:n, 0:cols], std[0:n, 0:cols])
                D()
                STT(o, xc[0:n, 0:cols, :], 0.0, bc(rstd[0:n, 0:cols], F), ALU.max, ALU.mult)
                D()

            def product(k):
                signal("h_ready")
                v.wait_ge(S["y_ready"], k)

            def chunk(tile, c, n=CHUNK):
                return tile[:, ds(c * n, n), :]

            def col(a_, c):
                return a_[:, ds(c * CHUNK, CHUNK)]

            hcf = hc[:, :].rearrange("p (t f) -> p t f", f=F)
            hc16 = hc[:, 0:CHUNK * HID].rearrange("p (t f) -> p t f", f=HID)
            y16 = psY[:, 0:CHUNK * HID].rearrange("p (t f) -> p t f", f=HID)
            y32 = psY[:, :].rearrange("p (b r) -> p b r", b=2)[:, :, 0:14 * F].rearrange("p b (t f) -> p b t f", f=F)

            def local_free(c, base):
                if base == 0:
                    return
                v.wait_ge(S["local_stored"], c * 16 + 16 * base)

            def s1(c, wait):
                norm(P, XS[:, ds(c * CHUNK, CHUNK), 0:F], CHUNK, c + (ln0["s1"] + 1), hcf)
                product(c + (y0["s1"] + 1))
                TT(G16[:, ds(c * CHUNK, CHUNK), :], y16, bc(col(inv[:, GCN_S, :], c), HID), ALU.mult)
                TT(gS[:, :, HID:2 * HID], y16, bt(b1r[:, :], CHUNK), ALU.add)
                D()
                if wait:
                    v.wait_ge(S["local_stored"], c * 16)
                TS(gS[:, :, 0:HID], gS[:, :, HID:2 * HID], 0.0, None, ALU.max)
                scan("d", c, G16, V, HID)
                signal("local_ready")
            s1(0, False)
            with v.Fori(1, CHUNKS) as c:
                s1(c, True)
            carry_in("d", V[:, 1:, 0:HID], B[:, :, 0:HID], HID)
            with v.Fori(0, CHUNKS) as c:
                norm(P, XD[:, ds(c * CHUNK, CHUNK), 0:F], CHUNK, c + (ln0["d1"] + 1), hcf)
                product(c + (y0["d1"] + 1))
                TT(hc16, y16, bc(col(inv[:, GCN_D, :], c), HID), ALU.mult)
                D()
                TT(hc16, hc16, V[:, ds(c * CHUNK + 1, CHUNK), 0:HID], ALU.add)
                D()
                TT(hc16, hc16, bc(col(inv[:, GCN_D, :], c), HID), ALU.mult)
                D()
                TT(hc16, hc16, bt(b1r[:, :], CHUNK), ALU.add)
                D()
                STT(G16[:, ds(c * CHUNK, CHUNK), :], hc16, 0.0, bc(col(inv[:, GCN_D, :], c), HID), ALU.max, ALU.mult)
                D()
            signal("rows_ready")
            v.wait_ge(S["rows_stored"], 16)
            v.tensor_copy(Z16, G16)
            D()
            signal("own_kept")
            with v.Fori(0, CHUNKS) as c:
                v.wait_ge(S["cols_ready"], c + (col0["g"] + 1))
                v.tensor_copy(hc16, G16[:, ds(c * CHUNK, CHUNK), :])
                product(c + (y0["s1b"] + 1))
                v.wait_ge(S["local_stored"], c * 16 + 16 * CHUNKS)
                TT(gS[:, :, :].rearrange("p (b t) f -> p b t f", b=2), y32, XS[:, ds(c * CHUNK, CHUNK), 0:F].rearrange("p (b t) f -> p b t f", b=2), ALU.add)
                D()
                TT(gS[:, :, :], gS[:, :, :], bt(b2r[:, :], CHUNK), ALU.add)
                scan("d", c, G16, V, HID)
                signal("local_ready")
            carry_in("d", V[:, 1:, 0:HID], B[:, :, 0:HID], HID)
            with v.Fori(0, CHUNKS) as c:
                TT(hc16, V[:, ds(c * CHUNK + 1, CHUNK), 0:HID], Z16[:, ds(c * CHUNK, CHUNK), :], ALU.add)
                D()
                TT(hc16, hc16, bc(col(inv[:, GCN_D, :], c), HID), ALU.mult)
                product(c + (y0["d1b"] + 1))
                TT(xc[:, :, :].rearrange("p (b t) f -> p b t f", b=2), y32, XD[:, ds(c * CHUNK, CHUNK), 0:F].rearrange("p (b t) f -> p b t f", b=2), ALU.add)
                D()
                TT(XD[:, ds(c * CHUNK, CHUNK), 0:F], xc[:, :, :], bt(b2r[:, :], CHUNK), ALU.add)
                D()
            v.tensor_copy(V[:, 1:, :], XD[:, :, 0:F])
            signal("rows_ready")
            v.wait_ge(S["rows_stored"], 32)

            with v.Fori(0, CHUNKS) as c:
                v.wait_ge(S["cols_ready"], c + (col0["x1"] + 1))
                v.tensor_copy(XS[:, ds(c * CHUNK, CHUNK), 0:F], chunk(G, c))
                norm(P, chunk(G, c), CHUNK, c + (ln0["h1s"] + 1), hcf)
                TT(hcf, hcf, bc(col(inv[:, OUT_S, :], c), F), ALU.mult)
                D()
                v.tensor_copy(chunk(G, c), hcf)
                v.wait_ge(S["local_stored"], c * 16 + 32 * CHUNKS)
                TS(gS[:, :, :], hcf, ALPHA, None, ALU.mult)
                D()
                scan("d", c, G, V, F)
                signal("local_ready")
            with v.Fori(0, CHUNKS) as c:
                norm(P, XD[:, ds(c * CHUNK, CHUNK), 0:F], CHUNK, c + (ln0["h1d"] + 1), hcf)
                STT(chunk(B, c), hcf, ALPHA, bc(col(inv[:, OUT_D, :], c), F), ALU.mult, ALU.mult)
                D()

            def update():
                ask()
                v.tensor_copy(carry[:, :], psY[:, 0:F])
                D()
                TT(G[:, :, :], bc(seg["d", "head"][:, :], F), bt(carry[:, :], COLS), ALU.mult)
                D()
                TT(V[:, 1:, :], V[:, 1:, :], G[:, :, :], ALU.add)
                D()
                TT(V[:, 1:, :], V[:, 1:, :], bc(a_d[:, :], F), ALU.mult)
                D()
                TT(V[:, 1:, :], V[:, 1:, :], B[:, :, :], ALU.add)

            v.wait_ge(S["local_stored"], 48 * CHUNKS)
            TT(G[:, :, :], G[:, :, :], bc(roots[:, OUT_S, :], F), ALU.mult)
            D()
            STT(XS[:, :, 0:F], G[:, :, :], ALPHA, XS[:, :, 0:F], ALU.mult, ALU.add)
            D()
            update()
            signal("rows_ready")

            def dense_step(k, st, n, cols, wait):
                v.wait_ge(S["dense_in"], (k + 1) * 16 if st == "dense" else 16 * (DSTEPS + 1))
                X = dx[0:n, 0:cols, :]
                X1 = dx1[0:n, 0:cols, :]
                m = min(cols, 6)
                norm(n, X, cols, k * 2 + (ln0[st] + 1), hcf[0:n, 0:cols, :])
                product(k * 2 + (y0[st] + 1))
                TT(xc[0:n, 0:cols, 0:HID], psY[0:n, 0:cols * HID].rearrange("p (t f) -> p t f", f=HID), bt(b1r[0:n, :], cols), ALU.add)
                D()
                TS(hc16[0:n, 0:cols, :], xc[0:n, 0:cols, 0:HID], 0.0, None, ALU.max)
                product(k * 2 + (y0[st] + 2))
                TT(X1, psY[0:n, 0:cols * F].rearrange("p (t f) -> p t f", f=F), X, ALU.add)
                v.drain().then_inc(S["dense_used"], 1)
                TT(X1, X1, bt(b2r[0:n, :], cols), ALU.add)
                D()
                norm(n, X1, cols, k * 2 + (ln0[st] + 2), hcf[0:n, 0:cols, :])
                if wait is not None:
                    v.wait_ge(S["dense_stored"], wait)
                STT(dout[0:n, 0:cols, :], hcf[0:n, 0:cols, :], ALPHA, X1, ALU.mult, ALU.add)
                D()
                TT(dout[0:n, 0:cols, :], dout[0:n, 0:cols, :], bt(br[0:n, :], cols), ALU.add)
                signal("dense_ready")

            dense_step(0, "dense", P, DN, None)
            with v.Fori(1, DSTEPS) as k:
                dense_step(k, "dense", P, DN, k * 16)
            dense_step(0, "dense_rest", RP, GROUP, 16 * DSTEPS)

            with v.Fori(0, STEPS - 1) as r:
                v.wait_ge(S["rows_stored"], r * 16 + 64)
                for c in range(CHUNKS):
                    v.wait_ge(S["cols_ready"], r * CHUNKS + (col0["f1"] + c + 1))
                    scan("d", c, G, V, F)
                v.drain().then_inc(S["tail_ready"], 1)
                v.wait_ge(S["carry_ready"], r + 10)
                v.tensor_copy(carry[:, :], psY[:, 0:F])
                D()
                TT(G[:, :, :], bc(seg["d", "head"][:, :], F), bt(carry[:, :], COLS), ALU.mult)
                D()
                TT(V[:, 1:, :], V[:, 1:, :], G[:, :, :], ALU.add)
                D()
                TT(V[:, 1:, :], V[:, 1:, :], bc(a_d[:, :], F), ALU.mult)
                D()
                TT(V[:, 1:, :], V[:, 1:, :], B[:, :, :], ALU.add)
                signal("rows_ready")
            state["tail"] += STEPS - 1
            TT(V[:, 1:, :], V[:, 1:, :], bc(roots[:, OUT_D, :], F), ALU.mult)
            D()
            TT(V[:, 1:, :], V[:, 1:, :], XD[:, :, 0:F], ALU.add)
            D()
            TT(B[:, :, :], V[:, 1:, :], bt(br[:, :], COLS), ALU.add)
            signal("rows_ready")
            signal("out_rows_ready")
            spread("d", V[:, 1:, :], G[:, :, :], XD[:, :, 0:F], F)
            v.tensor_copy(XD[:, :, INFO + 2], XD[:, :, INFO + 3])
            v.tensor_copy(XD[:, :, INFO:INFO + 2], ea[:, :, :])
            D()
            v.tensor_copy(XD[:, :, INFO + 3], pos[:, :])
            signal("rows_ready")

            v.wait_ge(S["cols_ready"], col0["pair"] + CHUNKS)
            v.tensor_copy(idx_q[:, :], XS[:, :, INFO + 3])
            lookup(XS[:, :, INFO + 2], SI)
            signal("lookup_ready")
            with v.Fori(0, CHUNKS) as c:
                U = XS[:, ds(c * CHUNK, CHUNK), INFO:INFO + 2]
                h = 2.0 / (BASIS - 1)
                for k in range(BASIS):
                    TS(tent[:, :, k::BASIS], U, 1.0 - k * h, 1.0 / h, ALU.add, ALU.mult)
                D()
                TS(basis[:, :, 0:2 * BASIS], tent[:, :, :], -1.0, 1.0, ALU.mult, ALU.add)
                TS(tent[:, :, :], tent[:, :, :], 1.0, None, ALU.add)
                D()
                TT(tent[:, :, :], tent[:, :, :], basis[:, :, 0:2 * BASIS], ALU.min)
                D()
                TS(tent[:, :, :], tent[:, :, :], 0.0, None, ALU.max)
                D()
                for k in range(BASIS):
                    TT(basis[:, :, k * BASIS:(k + 1) * BASIS], tent[:, :, BASIS:2 * BASIS], tent[:, :, k:k + 1].to_broadcast([P, CHUNK, BASIS]), ALU.mult)
                norm(P, XS[:, ds(c * CHUNK, CHUNK), 0:F], CHUNK, c + (ln0["spline"] + 1), hcf)
                signal("h_ready")
                for t in range(CHUNK):
                    v.wait_ge(S["wide_ready"], c * CHUNK + (t + 1))
                    TT(prod[:, :].rearrange("p (k o) -> p k o", o=F), psB[t % 4][:, :].rearrange("p (k o) -> p k o", o=F), bc(basis[:, t, :], F), ALU.mult)
                    v.drain().then_inc(S["wide_used"], 1)
                    v.tensor_reduce(hcf[:, t, :], prod[:, :].rearrange("p (k o) -> p o k", o=F), AX.X, ALU.add)
                    D()
                v.tensor_copy(XD[:, ds(c * CHUNK, CHUNK), 0:F], hcf)
                D()
                scan("p", c, XD, V, F)
            carry_in("p", V[:, 1:, :], XD[:, :, 0:F], F)
            v.wait_ge(S["cols_ready"], col0["x2"] + CHUNKS)
            TT(V[:, 1:, :], V[:, 1:, :], G[:, :, :], ALU.add)
            signal("rows_ready")
            spread("p", V[:, 1:, :], XD[:, :, 0:F], G, F)

            with v.Fori(0, CHUNKS) as c:
                norm(P, chunk(G, c), CHUNK, c * 2 + (ln0["att"] + 1), hcf)
                product(c * 2 + (y0["att"] + 1))
                v.tensor_copy(chunk(sc4, c), psY[:, 0:CHUNK * HEADS].rearrange("p (t h) -> p t h", h=HEADS))
                v.wait_ge(S["cols_ready"], c + (col0["x3"] + 1))
                norm(P, XS[:, ds(c * CHUNK, CHUNK), 0:F], CHUNK, c * 2 + (ln0["att"] + 2), hcf)
                v.tensor_copy(XS[:, ds(c * CHUNK, CHUNK), 0:F], hcf)
                product(c * 2 + (y0["att"] + 2))
                TT(chunk(sc4, c), chunk(sc4, c), psY[:, 0:CHUNK * HEADS].rearrange("p (t h) -> p t h", h=HEADS), ALU.add)
                D()
            TS(sc4[:, :, :], sc4[:, :, :], fbr[:, 0:1], None, ALU.add)
            D()
            STT(sc4[:, :, :], sc4[:, :, :], SLOPE, sc4[:, :, :], ALU.mult, ALU.max)
            TS(neg_same[:, :], seg["p", "same"][:, :], -1.0, HUGE, ALU.add, ALU.mult)
            TS(neg_head[:, :], seg["p", "head"][:, :], -1.0, HUGE, ALU.add, ALU.mult)
            TS(neg_bwd[:, :], seg["p", "bwd"][:, :], -1.0, HUGE, ALU.add, ALU.mult)
            D()
            for h in range(HEADS):
                v.tensor_tensor_scan(v4[:, 1:COLS + 1, h], neg_same[:, :], sc4[:, :, h], 0.0, ALU.add, ALU.max)
            D()
            for h in range(HEADS):
                v.tensor_copy(kb[:, :], v4[:, COLS, h:h + 1].to_broadcast([P, P]))
                ask()
                TT(junk[:, 0:P], psT[:, 0:P], neg_bwd[:, :], ALU.add)
                D()
                v.tensor_reduce(carry[:, h:h + 1], junk[:, 0:P], AX.X, ALU.max)
                D()
                TS(pos[:, :], neg_head[:, :], carry[:, h:h + 1], None, ALU.add)
                D()
                TT(v4[:, 1:COLS + 1, h], v4[:, 1:COLS + 1, h], pos[:, :], ALU.max)
                D()
            tmp4 = XD[:, :, 0:HEADS]
            spread("p", v4[:, 1:, :], tmp4, w4, HEADS)
            TT(sc4[:, :, :], sc4[:, :, :], w4[:, 0:COLS, :], ALU.subtract)
            signal("exp_ready")
            v.wait_ge(S["exp_done"], 1)
            for h in range(HEADS):
                v.tensor_tensor_scan(v4[:, 1:COLS + 1, h], seg["p", "same"][:, :], sc4[:, :, h], 0.0, ALU.mult, ALU.add)
            D()
            carry_in("p", v4[:, 1:, :], tmp4, HEADS)
            spread("p", v4[:, 1:, :], tmp4, w4, HEADS)
            v.reciprocal(v4[:, 1:, :], w4[:, 0:COLS, :])
            D()
            STT(sc4[:, :, :], sc4[:, :, :], 1.0 / HEADS, v4[:, 1:, :], ALU.mult, ALU.mult)
            D()
            with v.Fori(0, CHUNKS) as c:
                v.tensor_copy(hcf, XS[:, ds(c * CHUNK, CHUNK), 0:F])
                signal("h_ready")
                v.tensor_copy(basis[:, :, 0:HEADS], chunk(sc4, c))
                D()
                for t in range(CHUNK):
                    v.wait_ge(S["wide_ready"], c * CHUNK + (COLS + t + 1))
                    TT(prod[:, 0:HEADS * F].rearrange("p (k o) -> p k o", o=F), psB[t % 4][:, 0:HEADS * F].rearrange("p (k o) -> p k o", o=F), bc(basis[:, t, 0:HEADS], F), ALU.mult)
                    v.drain().then_inc(S["wide_used"], 1)
                    v.tensor_reduce(gS[:, t, :], prod[:, 0:HEADS * F].rearrange("p (k o) -> p o k", o=F), AX.X, ALU.add)
                    D()
                v.tensor_copy(XD[:, ds(c * CHUNK, CHUNK), 0:F], gS[:, :, :])
                D()
                scan("p", c, XD, V, F)
            carry_in("p", V[:, 1:, :], XD[:, :, 0:F], F)
            TT(V[:, 1:, :], V[:, 1:, :], bt(br[:, :], COLS), ALU.add)
            D()
            TT(V[:, 1:, :], V[:, 1:, :], G[:, :, :], ALU.add)
            signal("out_rows_ready")


_INS = ["x", "src", "dst", "edge_attr_2", "L0_gnn_W1", "L0_gnn_b1", "L0_gnn_W2", "L0_gnn_b2", "L2_gnn_weight",
        "L3_gnn_w", "L3_gnn_fc_w", "L3_gnn_fc_b", "L3_gnn_bias"]


def kernel(**inputs):
    import numpy as _np
    import concourse.bacc as _bacc
    from concourse import mybir as _mybir
    from concourse.bass_utils import run_bass_kernel_spmd as _run

    nc = _bacc.Bacc("TRN2", target_bir_lowering=False, num_devices=1)
    arrays, args = {}, []
    for name in _INS:
        a = _np.ascontiguousarray(inputs[name])
        arrays[f"in_{name}_dram"] = a
        args.append(nc.dram_tensor(f"in_{name}_dram", a.shape, _mybir.dt.from_np(a.dtype), kind="ExternalInput").ap())
    args.append(nc.dram_tensor("out_0_dram", (N, F), F32, kind="ExternalOutput").ap())
    gnn_kernel(nc, *args)
    r = _run(nc, [arrays], core_ids=[0])
    return r.results[0]["out_0_dram"]
```

```python
from contextlib import ExitStack

import concourse.bass as bass
from concourse import mybir

F32 = mybir.dt.float32
I32 = mybir.dt.int32
ALU = mybir.AluOpType
ACT = mybir.ActivationFunctionType
AX = mybir.AxisListType

P = 128
N = 100000
E = 25000
F = 32
HID = 16
HEADS = 4
BASIS = 4
COLS = -(-E // P)
SLOTS = P * COLS
CHUNK = 28
CHUNKS = COLS // CHUNK
LIVE = 7
LIVES = COLS // LIVE
PART = 49
PARTS = COLS // PART
FULL_ROWS = E // COLS
REST = E - FULL_ROWS * COLS
INFO = F
ROW = F + 4
NODES = N + 8
DIGIT = 256
HIGH = N // DIGIT + 1
STEPS = 10
ALPHA = 0.1
EPS = 1e-5
SLOPE = 0.2
NOWHERE = float(1 << 22)
HUGE = 1e30
GROUP = 4
DN = 20
DSTEPS = N // (P * DN)
DREST = N - DSTEPS * P * DN
RP = DREST // GROUP
DENSE_PARTS = 3
DPART = DSTEPS // DENSE_PARTS
ds = bass.ds


def gnn_kernel(nc, x, src, dst, edge_attr, W1, b1, W2, b2, w_spline, w_gat, fc_w, fc_b, bias, out):
    assert DPART * DENSE_PARTS == DSTEPS
    assert COLS % CHUNK == 0 and REST > 0 and RP * GROUP == DREST and RP <= P

    nodes = nc.dram_tensor("node_rows", (NODES, ROW), F32, kind="Internal").ap()
    sort1 = nc.dram_tensor("sorted_by_low_digit", (SLOTS, 2), F32, kind="Internal").ap()
    sort2 = nc.dram_tensor("sorted_by_src", (SLOTS, 2), F32, kind="Internal").ap()
    t_gcn = nc.dram_tensor("t_gcn", (2 * SLOTS, HID), F32, kind="Internal").ap()
    t_x1 = nc.dram_tensor("t_x1", (2 * SLOTS, F), F32, kind="Internal").ap()
    t_prop = nc.dram_tensor("t_prop", (SLOTS, F), F32, kind="Internal").ap()
    t_x2 = nc.dram_tensor("t_x2", (2 * SLOTS, F), F32, kind="Internal").ap()
    t_x3 = nc.dram_tensor("t_x3", (2 * SLOTS, F), F32, kind="Internal").ap()
    t_own = nc.dram_tensor("t_own", (SLOTS, ROW), F32, kind="Internal").ap()
    t_live = nc.dram_tensor("t_live", (2 * SLOTS, F), F32, kind="Internal").ap()
    live_rows = nc.dram_tensor("live_rows", (SLOTS, 4), F32, kind="Internal").ap()
    t_pair = nc.dram_tensor("t_pair", (SLOTS, ROW), F32, kind="Internal").ap()

    ctx = ExitStack()
    with ctx:
        def sb(name, shape, dt=F32):
            return ctx.enter_context(nc.sbuf_tensor(name, shape, dt))

        def ps(name, shape):
            return ctx.enter_context(nc.psum_tensor(name, shape, F32))

        def sem(name):
            return ctx.enter_context(nc.semaphore(name))

        big = sb("big", [P, 2 * COLS * ROW])
        XS = big[:, 0:COLS * ROW].rearrange("p (t w) -> p t w", w=ROW)
        XD = big[:, COLS * ROW:].rearrange("p (t w) -> p t w", w=ROW)
        G = sb("gathered", [P, COLS, F])
        V = sb("sums", [P, COLS + 1, F])
        B = sb("own_term", [P, COLS, F])
        G16 = G[:, :, :].rearrange("p t f -> p (t f)")[:, 0:COLS * HID].rearrange("p (t f) -> p t f", f=HID)
        HW = B[:, :, 0:HID]
        Z16 = B[:, :, HID:2 * HID]

        SI = sb("src_i", [P, COLS], I32)
        DI = sb("dst_i", [P, COLS], I32)
        idx_cq = sb("live_src_i", [P, COLS], I32)
        idx_cd = sb("live_dst_i", [P, COLS], I32)
        idx_cl = sb("live_lookup_i", [P, COLS], I32)
        idx_cu = sb("live_out_i", [P, COLS], I32)
        cpay = sb("live_payload", [P, COLS, 4])
        same_c = sb("same_live", [P, COLS])
        head_c = sb("head_live", [P, COLS])
        a_c = sb("prop_scale_live", [P, COLS])
        cpos = sb("live_place", [P, COLS])
        fwd_c = sb("fwd_live", [P, P])
        last_c = sb("last_live", [P, F])
        groups_i = sb("live_groups", [P, 1], I32)
        sm = sb("small", [P, 8])
        padrow = sb("pad_row", [P, 4])
        key_s = sb("src_f", [P, COLS])
        key_d = sb("dst_f", [P, COLS])
        key_p = sb("sorted_src_f", [P, COLS])
        dig = sb("digit_f", [P, COLS])
        pos = sb("position", [P, COLS])
        idx = sb("index_i", [P, COLS], I32)
        idx_q = sb("lookup_i", [P, COLS], I32)
        dig_i = idx_q
        idx_perm = sb("perm_i", [P, COLS], I32)
        idx_outd = sb("out_dst_i", [P, COLS], I32)
        idx_outs = sb("out_src_i", [P, COLS], I32)
        pay = sb("payload", [P, COLS, 2])
        iota_e = sb("edge_number", [P, COLS])
        iota_d = sb("digit_values", [P, HIGH])
        hist = sb("histogram", [P, HIGH])
        rank = sb("next_rank", [P, HIGH])
        junk = sb("junk", [P, HIGH])
        ident = sb("identity", [P, P])
        later = sb("later", [P, P])
        earlier = sb("earlier", [P, P])
        ones = sb("ones", [P, P])
        kb = sb("key_columns", [P, P])
        nf = sb("next_first", [P, 2])
        seg = {}
        for s in "dp":
            for n in ("same", "last", "notlast", "head", "tail"):
                seg[s, n] = sb(f"{n}_{s}", [P, COLS])
            seg[s, "fwd"] = sb(f"fwd_{s}", [P, P])
            seg[s, "bwd"] = sb(f"bwd_{s}", [P, P])
        neg_same, neg_head = key_s, key_d
        neg_bwd = sb("neg_bwd", [P, P])
        roots = sb("roots", [P, 5, COLS])
        inv = sb("inverse_roots", [P, 5, COLS])
        GCN_S, OUT_S, GCN_D, IN_D, OUT_D = range(5)
        ROOTS_S, ROOTS_D = slice(0, 2), slice(2, 5)
        a_d = sb("prop_scale", [P, COLS])
        a_head = sb("prop_scale_head", [P, COLS])
        hasnot = sb("no_incoming", [P, COLS])
        hc = sb("staged", [P, CHUNK * F])
        hT = sb("staged_turned", [P, CHUNK * F])
        xc = sb("centred", [P, CHUNK, F])
        sq = hc[:, :].rearrange("p (t f) -> p t f", f=F)
        mean = sb("mean", [P, CHUNK])
        var = sb("variance", [P, CHUNK])
        std = sb("std", [P, CHUNK])
        rstd = sb("rstd", [P, CHUNK])
        gS = sb("local_rows", [P, CHUNK, F])
        carry = sb("carry", [P, F])
        eps = sb("eps", [P, 1])
        zero = sb("zero", [P, 8])
        w1bd = sb("w1_blocks", [P, GROUP * HID])
        w2bd = sb("w2_blocks", [7 * HID, 7 * F])
        wsp = sb("w_spline_rows", [P, BASIS * BASIS * F])
        wg = sb("w_gat_rows", [P, HEADS, F])
        wgbd = sb("w_gat_blocks", [P, GROUP * HEADS * F])
        wsum = sb("w_att", [P, 2, HEADS])
        prod = sb("prod", [P, 512])
        wa_s = sb("w_att_src_blocks", [P, GROUP * HEADS])
        wa_d = sb("w_att_dst_blocks", [P, GROUP * HEADS])
        b1r = sb("b1_rows", [P, HID])
        b2r = sb("b2_rows", [P, F])
        br = sb("bias_rows", [P, F])
        fcr = sb("fc_rows", [P, 2 * F])
        fbr = sb("fc_bias_rows", [P, 1])
        ea = sb("edge_attr", [P, COLS, 2])
        tent = sb("tents", [P, CHUNK, 2 * BASIS])
        basis = sb("basis", [P, CHUNK, BASIS * BASIS])
        att = sb("weights", [P, CHUNK * HEADS])
        Bf = B[:, :, :].rearrange("p t f -> p (t f)")
        sc4, v4, w4 = (Bf[:, i * (COLS + 1) * HEADS:(i + 1) * (COLS + 1) * HEADS].rearrange("p (t h) -> p t h", h=HEADS) for i in range(3))
        sc4 = sc4[:, 0:COLS, :]
        dx, dx1, dout = (B[:, i * DN:(i + 1) * DN, :] for i in range(3))

        psT = ps("turned", [P, 1024])
        psY = ps("products", [P, 1024])
        psB = [ps(f"wide{i}", [P, 512]) for i in range(4)]

        live_chunk = [sem(f"live_gather{c}") for c in range(LIVES)]
        part_stored = [sem(f"live_part_stored{c}") for c in range(PARTS)]
        names = ("loads zeroed patterns weights_placed node_rows_done keys_ready keys_turned shift_done "
                 "hist_ready base_ready order_ready table_ready sorted_done info_scattered cols_ready "
                 "roots_done var_ready std_ready h_ready ht_ps ht_sb y_ready "
                 "tail_ready carry_ready rows_ready rows_stored lookup_ready wide_ready wide_used "
                 "att_ready att_done exp_ready exp_done dense_in dense_used dense_ready dense_stored "
                 "out_rows_ready pay_ready reloaded own_kept local_ready local_stored rounds_open live_cleared live_counted own_rows_kept prop_ready consts_ready live_out_ready own_stored").split()
        S = {n: sem(n) for n in names}
        chunk_sem = [sem(f"gather_chunk{c}") for c in range(CHUNKS)]
        scat = sem("scattered")

        def bc(ap, n):
            return ap.unsqueeze(2).to_broadcast([ap.shape[0], ap.shape[1], n])

        def bt(ap, t):
            return ap.unsqueeze(1).to_broadcast([ap.shape[0], t, ap.shape[1]])

        order = [(f"dense{i}", DPART, 2, ("w1", "w2")) for i in range(DENSE_PARTS)]
        order += [("dense_rest", 1, 2, ("w1", "w2")), ("s1", CHUNKS, 1, ("w1",)), ("d1", CHUNKS, 1, ("w1",)),
                  ("x1", CHUNKS, 0, ("w2", "w2")), ("x1carry", 1, 0, ("w2",)), ("h1s", CHUNKS, 1, ()), ("h1d", CHUNKS, 1, ()),
                  ("spline", CHUNKS, 1, ("wide",)), ("att", CHUNKS, 2, ("was", "wad")), ("msg", CHUNKS, 0, ("hp",))]
        ln0, lin0, y0 = {}, {}, {}
        a = b = d = 0
        for n, times, lns, kinds in order:
            ln0[n], lin0[n], y0[n] = a, b, d
            a += times * lns
            d += times * len(kinds) * (kinds not in (("wide",), ("hp",)))
            b += times * len(kinds)
        gathers = ["xs", "xd", "g", "x1", "pair", "x2", "x3"]
        col0 = {n: i * CHUNKS for i, n in enumerate(gathers)}

        def nest(eng, groups, n, body, c=0):
            body(c)
            if c + 1 < n:
                with eng.If(groups > c + 1):
                    nest(eng, groups, n, body, c + 1)

        def parts(eng, groups, body, j=0):
            body(j)
            if j + 1 < PARTS:
                with eng.If(groups > (j + 1) * (PART // LIVE)):
                    parts(eng, groups, body, j + 1)

        block = ctx.enter_context(nc.Block())

        @block.sync
        def _(sp):
            L = S["loads"]
            sp.wait_ge(S["zeroed"], 1)
            n = 0
            for tile, arr in ((SI, src), (DI, dst)):
                sp.dma_start(tile[0:FULL_ROWS, :], arr[0:FULL_ROWS * COLS].rearrange("(p t) -> p t", t=COLS)).then_inc(L, 16)
                sp.dma_start(tile[FULL_ROWS:FULL_ROWS + 1, 0:REST], arr[FULL_ROWS * COLS:E].rearrange("(p t) -> p t", t=REST)).then_inc(L, 16)
            sp.dma_start(ea[0:FULL_ROWS, :, :], edge_attr[0:FULL_ROWS * COLS, :].rearrange("(p t) c -> p t c", t=COLS)).then_inc(L, 16)
            sp.dma_start(ea[FULL_ROWS:FULL_ROWS + 1, 0:REST, :], edge_attr[FULL_ROWS * COLS:E, :].rearrange("(p t) c -> p t c", t=REST)).then_inc(L, 16)
            for g in range(GROUP):
                sp.dma_start(w1bd[g * F:(g + 1) * F, g * HID:(g + 1) * HID], W1).then_inc(L, 16)
                sp.dma_start(wsp[g * F:(g + 1) * F, :].rearrange("p (k o) -> p k o", o=F), w_spline.rearrange("a b f o -> f (a b) o")).then_inc(L, 16)
                sp.dma_start(wg[g * F:(g + 1) * F, :, :], w_gat.rearrange("h f o -> f h o")).then_inc(L, 16)
            for g in range(7):
                sp.dma_start(w2bd[g * HID:(g + 1) * HID, g * F:(g + 1) * F], W2).then_inc(L, 16)
            for tile, arr in ((b1r, b1), (b2r, b2), (br, bias), (fbr, fc_b)):
                sp.dma_start(tile[:, :], arr.partition_broadcast(P)).then_inc(L, 16)
            sp.dma_start(fcr[:, :], fc_w[0, :].partition_broadcast(P)).then_inc(L, 16)
            sp.dma_start(nodes[0:N, 0:F], x).then_inc(S["node_rows_done"], 16)
            sp.dma_start(nodes[0:N, F:ROW].rearrange("(p t) w -> p t w", p=32), zero[0:32, 0:4].unsqueeze(1).to_broadcast([32, N // 32, 4])).then_inc(S["node_rows_done"], 16)
            sp.dma_start(nodes[N:NODES, :].rearrange("r (a w) -> r a w", w=4), zero[0:NODES - N, 0:4].unsqueeze(1).to_broadcast([NODES - N, ROW // 4, 4])).then_inc(S["node_rows_done"], 16)

            def span(arr, k):
                return arr[ds(k * P * DN, P * DN), :].rearrange("(p t) f -> p t f", t=DN)

            rest_in, rest_out = (a_[DSTEPS * P * DN:N, :].rearrange("(p t) f -> p t f", t=GROUP) for a_ in (x, out))

            def dense_part(i):
                if i == 0:
                    sp.dma_start(dx[:, :, :], span(x, 0)).then_inc(S["dense_in"], 16)
                last = i == DENSE_PARTS - 1
                with sp.Fori(i * DPART, (i + 1) * DPART - last) as k:
                    sp.wait_ge(S["dense_used"], k + 1)
                    sp.dma_start(dx[:, :, :], span(x, k + 1)).then_inc(S["dense_in"], 16)
                    sp.wait_ge(S["dense_ready"], k + 1)
                    sp.dma_start(span(out, k), dout[:, :, :]).then_inc(S["dense_stored"], 16)
                if last:
                    sp.wait_ge(S["dense_used"], DSTEPS)
                    sp.dma_start(dx[0:RP, 0:GROUP, :], rest_in).then_inc(S["dense_in"], 16)
                    sp.wait_ge(S["dense_ready"], DSTEPS)
                    sp.dma_start(span(out, DSTEPS - 1), dout[:, :, :]).then_inc(S["dense_stored"], 16)

            for half in range(2):
                sp.dma_start(t_live[half * SLOTS:(half + 1) * SLOTS, :].rearrange("(p t) w -> p t w", t=COLS), G[:, :, :]).then_inc(S["live_cleared"], 16)
            sp.dma_start(live_rows.rearrange("(p t) w -> p t w", t=COLS), padrow[:, :].unsqueeze(1).to_broadcast([P, COLS, 4])).then_inc(S["live_cleared"], 16)
            for i, key in enumerate((key_d, key_p)):
                sp.wait_ge(S["keys_ready"], i + 1)
                sp.dma_start(nf[0:P - 1, i:i + 1], key[1:P, 0:1]).then_inc(S["shift_done"], 16)
                if i == 0:
                    for k, table in enumerate((sort1, sort2)):
                        dense_part(k)
                        sp.wait_ge(S["sorted_done"], k + 1)
                        sp.dma_start(pay[:, :, :], table.rearrange("(p t) c -> p t c", t=COLS)).then_inc(S["reloaded"], 16)
            dense_part(2)
            sp.wait_ge(S["dense_ready"], DSTEPS + 1)
            sp.dma_start(rest_out, dout[0:RP, 0:GROUP, :]).then_inc(S["dense_stored"], 16)
            stored = 0
            locals_ = 0

            def store_local(table, width, chunks=CHUNKS):
                nonlocal locals_
                tail = table[SLOTS:2 * SLOTS, :].rearrange("(p t) w -> p t w", t=COLS)
                with sp.Fori(0, CHUNKS) as c:
                    sp.wait_ge(S["local_ready"], c + (locals_ + 1))
                    sp.dma_start(tail[:, ds(c * CHUNK, CHUNK), :], gS[:, :, 0:width]).then_inc(S["local_stored"], 16)
                locals_ += CHUNKS

            def store_rows(table, tile, rows_ready):
                sp.wait_ge(S["rows_ready"], rows_ready)
                sp.dma_start(table, tile).then_inc(S["rows_stored"], 16)

            def front(table):
                return table[0:SLOTS, :].rearrange("(p t) w -> p t w", t=COLS)

            def back(table):
                return table[SLOTS:2 * SLOTS, :].rearrange("(p t) w -> p t w", t=COLS)

            store_local(t_gcn, HID)
            store_rows(front(t_gcn), G16, 1)
            sp.wait_ge(S["sorted_done"], 3)
            sp.dma_start(cpay[:, :, :], live_rows.rearrange("(p t) c -> p t c", t=COLS)).then_inc(S["reloaded"], 16)
            sp.wait_ge(S["live_counted"], 1)
            groups = sp.value_load(groups_i[0:1, 0:1], min_val=1, max_val=LIVES)
            store_local(t_x1, F)
            store_rows(front(t_x1), V[:, 1:, :], 2)
            store_local(t_x2, F)
            store_rows(t_prop.rearrange("(p t) w -> p t w", t=COLS), G[:, :, :], 3)
            sp.wait_ge(S["rows_ready"], 4)
            sp.dma_start(t_own.rearrange("(p t) w -> p t w", t=COLS), XS).then_inc(S["own_stored"], 16)

            def store_live(view, tile):
                def part(j):
                    at = slice(j * PART, (j + 1) * PART)
                    sp.dma_start(view[:, at, :], tile[:, at, 0:F]).then_inc(part_stored[j], 16)
                parts(sp, groups, part)

            sp.wait_ge(S["prop_ready"], 1)
            store_live(front(t_live), G)
            sp.wait_ge(S["consts_ready"], 1)
            store_live(back(t_live), XS)
            with sp.Fori(0, STEPS - 3) as r:
                sp.wait_ge(S["prop_ready"], r + 2)
                store_live(front(t_live), G)
            sp.wait_ge(S["sorted_done"], 4)
            sp.dma_start(XS, t_own.rearrange("(p t) w -> p t w", t=COLS)).then_inc(S["reloaded"], 16)
            store_rows(front(t_x2), V[:, 1:, :], 5)
            store_rows(t_pair.rearrange("(p t) w -> p t w", t=COLS), XD, 6)
            store_rows(back(t_x3), XS[:, :, 0:F], 7)
            store_rows(front(t_x3), V[:, 1:, :], 7)

        @block.scalar
        def _(act):
            def norm(n, k, width):
                act.wait_ge(S["var_ready"], k)
                nc.scalar.activation(std[0:n, 0:width], var[0:n, 0:width], ACT.Sqrt, bias=eps[0:n, :], scale=1.0 / F).then_inc(S["std_ready"], 1)

            def turned(rows, cols, k):
                act.wait_ge(S["ht_ps"], k)
                nc.scalar.copy(hT[0:rows, 0:cols], psT[0:rows, 0:cols]).then_inc(S["ht_sb"], 1)

            def dense_step(st, k, rows, cols):
                m = 5 if cols == DN else cols
                norm(rows, k * 2 + (ln0[st] + 1), cols)
                turned(P, (cols // GROUP) * P if rows == P else rows, k * 2 + (lin0[st] + 1))
                turned(m * HID, (cols // m) * P if rows == P else rows, k * 2 + (lin0[st] + 2))
                norm(rows, k * 2 + (ln0[st] + 2), cols)

            for i in range(DENSE_PARTS):
                with act.Fori(0, DPART) as k:
                    dense_step(f"dense{i}", k, P, DN)
            dense_step("dense_rest", 0, RP, GROUP)
            for st, rows in (("s1", ROOTS_S), ("d1", ROOTS_D)):
                with act.Fori(0, CHUNKS) as c:
                    norm(P, c + (ln0[st] + 1), CHUNK)
                    i = nc.scalar.activation(roots[:, rows, ds(c * CHUNK, CHUNK)], roots[:, rows, ds(c * CHUNK, CHUNK)], ACT.Sqrt)
                    i.then_inc(S["roots_done"], 1)
                    turned(P, CHUNK * F, c + (lin0[st] + 1))
            with act.Fori(0, CHUNKS) as c:
                turned(7 * HID, 4 * P, c * 2 + (lin0["x1"] + 1))
                turned(7 * HID, 4 * P, c * 2 + (lin0["x1"] + 2))
            turned(HID, P, lin0["x1carry"] + 1)
            for st in ("h1s", "h1d"):
                with act.Fori(0, CHUNKS) as c:
                    norm(P, c + (ln0[st] + 1), CHUNK)

            with act.Fori(0, CHUNKS) as c:
                norm(P, c + (ln0["spline"] + 1), CHUNK)
                turned(P, CHUNK * F, c + (lin0["spline"] + 1))
            with act.Fori(0, CHUNKS) as c:
                norm(P, c * 2 + (ln0["att"] + 1), CHUNK)
                turned(P, CHUNK * F, c * 2 + (lin0["att"] + 1))
                norm(P, c * 2 + (ln0["att"] + 2), CHUNK)
                turned(P, CHUNK * F, c * 2 + (lin0["att"] + 2))
            act.wait_ge(S["exp_ready"], 1)
            nc.scalar.activation(sc4, sc4, ACT.Exp).then_inc(S["exp_done"], 1)
            with act.Fori(0, CHUNKS) as c:
                turned(P, CHUNK * F, c + (lin0["msg"] + 1))

        @block.tensor
        def _(pe):
            pe.wait_ge(S["patterns"], 1)
            pe.wait_ge(S["loads"], 16 * 30)

            def key_matrices(k):
                for j in range(2):
                    pe.wait_ge(S["tail_ready"], k + j + 1)
                    nc.tensor.transpose(psT[:, 0:P], kb[:, :], ident[:, :]).then_inc(S["carry_ready"], 1)

            def carry_row(k, M, rhs, w):
                pe.wait_ge(S["tail_ready"], k)
                nc.tensor.matmul(psY[:, 0:w], M[:, :], rhs, start=True, stop=True).then_inc(S["carry_ready"], 1)

            def turn_row(k):
                pe.wait_ge(S["tail_ready"], k)
                nc.tensor.transpose(psT[:, 0:P], kb[:, :], ident[:, :]).then_inc(S["carry_ready"], 1)

            def ranks(k, width):
                pe.wait_ge(S["hist_ready"], k)
                nc.tensor.matmul(psT[:, 0:width], later[:, :], hist[:, 0:width], start=True, stop=True)
                nc.tensor.matmul(psT[:, 512:512 + width], ones[:, :], hist[:, 0:width], start=True, stop=True).then_inc(S["base_ready"], 1)

            def turn(n, groups, gw, k):
                pe.wait_ge(S["h_ready"], k)
                for g in range(groups):
                    i = nc.tensor.transpose(psT[0:gw, g * P:g * P + n], hc[0:n, g * gw:(g + 1) * gw], ident[0:n, 0:n])
                i.then_inc(S["ht_ps"], 1)
                pe.wait_ge(S["ht_sb"], k)

            def lin(n, cols, kind, k):
                if kind == "w1":
                    turn(n, cols // GROUP, GROUP * F, k)
                    for g in range(cols // GROUP):
                        i = nc.tensor.matmul(psY[0:n, g * GROUP * HID:(g + 1) * GROUP * HID], hT[:, g * P:g * P + n], w1bd[:, :], start=True, stop=True)
                elif kind == "w2":
                    m = {CHUNK: 7, DN: 5}.get(cols, cols)
                    turn(n, cols // m, m * HID, k)
                    for g in range(cols // m):
                        o = (g // 2) * 512 + (g % 2) * m * F
                        i = nc.tensor.matmul(psY[0:n, o:o + m * F], hT[0:m * HID, g * P:g * P + n], w2bd[0:m * HID, 0:m * F], start=True, stop=True)
                elif kind in ("was", "wad"):
                    turn(n, cols // GROUP, GROUP * F, k)
                    w = wa_s if kind == "was" else wa_d
                    for g in range(cols // GROUP):
                        i = nc.tensor.matmul(psY[0:n, g * GROUP * HEADS:(g + 1) * GROUP * HEADS], hT[:, g * P:g * P + n], w[:, :], start=True, stop=True)
                i.then_inc(S["y_ready"], 1)

            def wide(c, st):
                turn(P, CHUNK // GROUP, GROUP * F, c + (lin0[st] + 1))
                if st == "msg":
                    n = CHUNK // GROUP
                    for g in range(n):
                        if g >= 4:
                            pe.wait_ge(S["wide_used"], c * n + (COLS + g - 3))
                        nc.tensor.matmul(psB[g % 4][:, :], hT[:, g * P:(g + 1) * P], wgbd[:, :], start=True, stop=True).then_inc(S["wide_ready"], 1)
                    return
                for t in range(CHUNK):
                    q = t % GROUP
                    if t >= 4:
                        pe.wait_ge(S["wide_used"], c * CHUNK + (t - 3))
                    i = nc.tensor.matmul(psB[t % 4][:, :], hT[q * F:(q + 1) * F, (t // GROUP) * P:(t // GROUP + 1) * P],
                                         wsp[q * F:(q + 1) * F, :], start=True, stop=True)
                    i.then_inc(S["wide_ready"], 1)

            def dense(i):
                with pe.Fori(0, DPART) as k:
                    lin(P, DN, "w1", k * 2 + (lin0[f"dense{i}"] + 1))
                    lin(P, DN, "w2", k * 2 + (lin0[f"dense{i}"] + 2))

            key_matrices(0)
            carry_row(3, seg["d", "fwd"], V[:, COLS, 0:1], 1)
            ranks(1, DIGIT)
            dense(0)
            ranks(2, HIGH)
            dense(1)
            key_matrices(3)
            carry_row(6, seg["p", "fwd"], V[:, COLS, 0:1], 1)
            dense(2)
            lin(RP, GROUP, "w1", lin0["dense_rest"] + 1)
            lin(RP, GROUP, "w2", lin0["dense_rest"] + 2)
            with pe.Fori(0, CHUNKS) as c:
                lin(P, CHUNK, "w1", c + (lin0["s1"] + 1))
            pe.wait_ge(S["tail_ready"], 7)
            nc.tensor.matmul(psY[:, 0:1], later[:, :], V[:, COLS, HID + 1:HID + 2], start=True, stop=True)
            nc.tensor.matmul(psY[:, 512:513], ones[:, :], V[:, COLS, HID + 1:HID + 2], start=True, stop=True).then_inc(S["carry_ready"], 1)
            carry_row(8, seg["d", "fwd"], V[:, COLS, HID:HID + 1], 1)
            with pe.Fori(0, CHUNKS) as c:
                lin(P, CHUNK, "w1", c + (lin0["d1"] + 1))
            carry_row(9, seg["d", "fwd"], V[:, COLS, 0:HID], HID)
            turn_row(10)
            with pe.Fori(0, CHUNKS) as c:
                lin(P, CHUNK, "w2", c * 2 + (lin0["x1"] + 1))
                lin(P, CHUNK, "w2", c * 2 + (lin0["x1"] + 2))
            carry_row(11, seg["d", "fwd"], V[:, COLS, 0:HID], HID)
            lin(P, 1, "w2", lin0["x1carry"] + 1)
            carry_row(12, seg["d", "fwd"], V[:, COLS, :], F)
            carry_row(13, seg["d", "fwd"], XS[:, COLS - 1, 0:F], F)
            carry_row(14, fwd_c, last_c[:, :], F)
            with pe.Fori(0, STEPS - 2) as r:
                carry_row(r + 15, fwd_c, last_c[:, :], F)
            k = STEPS + 13
            carry_row(k, seg["d", "bwd"], XD[:, 0, 0:F], F)
            k += 1
            with pe.Fori(0, CHUNKS) as c:
                wide(c, "spline")
            carry_row(k, seg["p", "fwd"], V[:, COLS, :], F)
            carry_row(k + 1, seg["p", "bwd"], G[:, 0, :], F)
            with pe.Fori(0, CHUNKS) as c:
                lin(P, CHUNK, "was", c * 2 + (lin0["att"] + 1))
                lin(P, CHUNK, "wad", c * 2 + (lin0["att"] + 2))
            k += 2
            for h in range(HEADS):
                turn_row(k + h)
            k += HEADS
            carry_row(k, seg["p", "bwd"], w4[:, 0, :], HEADS)
            carry_row(k + 1, seg["p", "fwd"], v4[:, COLS, :], HEADS)
            carry_row(k + 2, seg["p", "bwd"], w4[:, 0, :], HEADS)
            with pe.Fori(0, CHUNKS) as c:
                wide(c, "msg")
            carry_row(k + 3, seg["p", "fwd"], V[:, COLS, :], F)

        @block.gpsimd
        def _(pool):
            pool.iota(iota_e[:, :], [[1, COLS]], base=0, channel_multiplier=COLS, allow_small_or_imprecise_dtypes=True)
            pool.iota(iota_d[:, :], [[1, HIGH]], base=0, channel_multiplier=0, allow_small_or_imprecise_dtypes=True)
            pool.memset(ones[:, :], 1.0)
            pool.drain()
            pool.affine_select(out=later[:, :], in_=ones[:, :], compare_op=ALU.is_gt, fill=0.0, base=0, pattern=[[1, P]], channel_multiplier=-1)
            pool.affine_select(out=earlier[:, :], in_=ones[:, :], compare_op=ALU.is_gt, fill=0.0, base=0, pattern=[[-1, P]], channel_multiplier=1)
            pool.affine_select(out=ident[:, :], in_=ones[:, :], compare_op=ALU.is_equal, fill=0.0, base=0, pattern=[[-1, P]], channel_multiplier=1)
            pool.drain().then_inc(S["patterns"], 1)

            def offs(t, i):
                return bass.IndirectOffsetOnAxis(ap=i[:, t:t + 1], axis=0)

            def scatter(view, i, rows, limit, done, value):
                for t in range(COLS):
                    pool.indirect_dma_start(view, offs(t, i), rows(t), None, bounds_check=limit, oob_is_err=False).then_inc(scat, 16)
                pool.wait_ge(scat, 16 * COLS * value)
                pool.sem_inc(done, 1)

            def gather(table, i, cols, count, lookups=None):
                for c in range(CHUNKS + 1):
                    if c < CHUNKS and lookups is not None:
                        pool.wait_ge(S["lookup_ready"], lookups + c + 1)
                    if c < CHUNKS:
                        for t in range(c * CHUNK, (c + 1) * CHUNK):
                            pool.indirect_dma_start(cols(t), None, table, offs(t, i)).then_inc(chunk_sem[c], 16)
                    if c > 0:
                        pool.wait_ge(chunk_sem[c - 1], count)
                        pool.sem_inc(S["cols_ready"], 1)

            per = 16 * CHUNK
            info_limit = NODES * (ROW // 2) - 1
            pool.wait_ge(S["node_rows_done"], 48)
            pool.wait_ge(S["pay_ready"], 1)
            scatter(nodes.rearrange("n (a w) -> (n a) w", w=2), idx, lambda t: pay[:, t, :], info_limit, S["info_scattered"], 1)
            pool.wait_ge(S["pay_ready"], 2)
            scatter(sort1, idx, lambda t: pay[:, t, :], SLOTS - 1, S["sorted_done"], 2)
            pool.wait_ge(S["pay_ready"], 3)
            scatter(sort2, idx, lambda t: pay[:, t, :], SLOTS - 1, S["sorted_done"], 3)
            pool.wait_ge(S["pay_ready"], 4)
            scatter(nodes.rearrange("n (a w) -> (n a) w", w=2), idx, lambda t: pay[:, t, :], info_limit, S["info_scattered"], 4)

            gather(nodes, SI, lambda t: XS[:, t, :], per)
            gather(nodes, DI, lambda t: XD[:, t, :], 2 * per)
            pool.wait_ge(S["live_cleared"], 48)
            pool.wait_ge(S["pay_ready"], 5)
            scatter(live_rows, idx, lambda t: cpay[:, t, :], SLOTS - 1, S["sorted_done"], 5)
            pool.wait_ge(S["lookup_ready"], 1)
            pool.wait_ge(S["local_stored"], 16 * CHUNKS)
            pool.wait_ge(S["rows_stored"], 16)
            pool.wait_ge(S["own_kept"], 1)
            gather(t_gcn, idx_q, lambda t: G16[:, t, :], 3 * per)
            pool.wait_ge(S["local_stored"], 32 * CHUNKS)
            pool.wait_ge(S["rows_stored"], 32)
            pool.wait_ge(S["live_counted"], 1)
            gather(t_x1, idx_q, lambda t: G[:, t, :], 4 * per)
            groups = pool.value_load(groups_i[0:1, 0:1], min_val=1, max_val=LIVES)
            lper = 16 * LIVE

            def gather_live(table, i, cols):
                def group(c):
                    for t in range(c * LIVE, (c + 1) * LIVE):
                        pool.indirect_dma_start(cols(t), None, table, offs(t, i)).then_inc(live_chunk[c], 16)
                nest(pool, groups, LIVES, group)

            pool.wait_ge(S["rows_stored"], 48)
            gather_live(t_prop, idx_cq, lambda t: G[:, t, :])
            pool.wait_ge(S["own_stored"], 16)
            gather_live(t_own, idx_cd, lambda t: XS[:, t, :])
            pool.wait_ge(S["own_rows_kept"], 1)
            gather_live(t_own, idx_cq, lambda t: XS[:, t, :])
            with pool.Fori(0, STEPS - 2) as r:
                def part(j):
                    pool.wait_ge(part_stored[j], r * 16 + 32)
                    pool.sem_inc(S["rounds_open"], 1)
                parts(pool, groups, part)
                gather_live(t_live, idx_cl, lambda t: G[:, t, :])
            pool.wait_ge(S["live_out_ready"], 1)

            def group(c):
                for t in range(c * LIVE, (c + 1) * LIVE):
                    pool.indirect_dma_start(t_own, offs(t, idx_cu), XS[:, t, :], None, bounds_check=SLOTS - 1, oob_is_err=False).then_inc(live_chunk[c], 16)
            nest(pool, groups, LIVES, group)
            nest(pool, groups, LIVES, lambda c: pool.wait_ge(live_chunk[c], (STEPS + 2) * lper))
            pool.sem_inc(S["sorted_done"], 1)
            pool.wait_ge(S["dense_stored"], 16 * (DSTEPS + 1))
            pool.wait_ge(S["out_rows_ready"], 1)
            scatter(out, idx_outd, lambda t: B[:, t, :], N - 1, S["info_scattered"], 6)
            pool.wait_ge(S["rows_stored"], 16 * 5)
            gather(t_pair, idx_perm, lambda t: XS[:, t, :], 5 * per)
            gather(t_x2, idx_q, lambda t: G[:, t, :], 6 * per, lookups=1)
            pool.wait_ge(S["rows_stored"], 16 * 7)
            gather(t_x3, SI, lambda t: XS[:, t, 0:F], 7 * per)
            pool.wait_ge(S["out_rows_ready"], 2)
            scatter(out, idx_outs, lambda t: V[:, t + 1, :], N - 1, S["info_scattered"], 7)

        @block.vector
        def _(v):
            state = {"tail": 0, "cols": 0, "local": 0, "wide": 0}
            TT, TS, STT = v.tensor_tensor, v.tensor_scalar, v.scalar_tensor_tensor

            def D():
                v.drain()

            def signal(name):
                v.drain().then_inc(S[name], 1)

            def ask():
                state["tail"] += 1
                signal("tail_ready")
                v.wait_ge(S["carry_ready"], state["tail"])

            v.memset(SI[:, :], N)
            v.memset(DI[:, :], N)
            v.memset(ea[:, :, :], 0.0)
            v.memset(w1bd[:, :], 0.0)
            v.memset(w2bd[:, :], 0.0)
            v.memset(zero[:, :], 0.0)
            v.memset(eps[:, :], EPS)
            v.memset(nf[:, :], -1.0)
            v.memset(padrow[:, :], 0.0)
            v.memset(G[:, :, :], 0.0)
            D()
            v.memset(padrow[:, 2:3], -1.0)
            v.memset(a_c[:, :], 0.0)
            signal("zeroed")
            v.memset(V[:, 0, :], 0.0)
            v.wait_ge(S["patterns"], 1)
            v.wait_ge(S["loads"], 16 * 30)
            v.tensor_copy(key_s[:, :], SI[:, :])
            v.tensor_copy(key_d[:, :], DI[:, :])
            for side in range(2):
                D()
                TT(prod[:, 0:HEADS * F].rearrange("p (h o) -> p h o", o=F), wg[:, :, :], bt(fcr[:, side * F:(side + 1) * F], HEADS), ALU.mult)
                D()
                v.tensor_reduce(wsum[:, side, :], prod[:, 0:HEADS * F].rearrange("p (h o) -> p h o", o=F), AX.X, ALU.add)
                D()
                if side == 0:
                    v.memset(wgbd[:, :], 0.0)
                    D()
                    for g in range(GROUP):
                        v.tensor_copy(wgbd[g * F:(g + 1) * F, g * HEADS * F:(g + 1) * HEADS * F].rearrange("p (h o) -> p h o", o=F), wg[g * F:(g + 1) * F, :, :])
                w = (wa_s, wa_d)[side]
                v.memset(w[:, :], 0.0)
                D()
                for g in range(GROUP):
                    v.tensor_copy(w[g * F:(g + 1) * F, g * HEADS:(g + 1) * HEADS], wsum[g * F:(g + 1) * F, side, :])
            D()

            def segments(s, key, i):
                g = lambda n: seg[s, n]
                signal("keys_ready")
                v.memset(g("same")[:, 0:1], 0.0)
                TT(g("same")[:, 1:COLS], key[:, 1:COLS], key[:, 0:COLS - 1], ALU.is_equal)
                TT(g("last")[:, 0:COLS - 1], key[:, 1:COLS], key[:, 0:COLS - 1], ALU.not_equal)
                v.wait_ge(S["shift_done"], 16 * (i + 1))
                TT(g("last")[:, COLS - 1:COLS], key[:, COLS - 1:COLS], nf[:, i:i + 1], ALU.not_equal)
                D()
                TS(g("notlast")[:, :], g("last")[:, :], -1.0, 1.0, ALU.mult, ALU.add)
                D()
                TS(g("head")[:, :], key[:, :], key[:, 0:1], None, ALU.is_equal)
                TS(g("tail")[:, :], key[:, :], key[:, COLS - 1:COLS], g("notlast")[:, COLS - 1:COLS], ALU.is_equal, ALU.mult)
                v.tensor_copy(kb[:, :], key[:, 0:1].to_broadcast([P, P]))
                ask()
                STT(g("fwd")[:, :], psT[:, 0:P], key[:, COLS - 1:COLS], later[:, :], ALU.is_equal, ALU.mult)
                v.tensor_copy(kb[:, :], key[:, COLS - 1:COLS].to_broadcast([P, P]))
                ask()
                STT(g("bwd")[:, :], psT[:, 0:P], key[:, 0:1], earlier[:, :], ALU.is_equal, ALU.mult)
                D()

            def scan(s, c, src_, dst_, width, n=CHUNK):
                t0 = c * n
                for f in range(width):
                    v.tensor_tensor_scan(dst_[:, ds(t0 + 1, n), f], seg[s, "same"][:, ds(t0, n)], src_[:, ds(t0, n), f],
                                         dst_[:, ds(t0, 1), f], ALU.mult, ALU.add)
                D()

            def carry_in(s, tile, tmp, width):
                ask()
                v.tensor_copy(carry[:, 0:width], psY[:, 0:width])
                D()
                TT(tmp, bc(seg[s, "head"][:, :], width), bt(carry[:, 0:width], COLS), ALU.mult)
                D()
                TT(tile, tile, tmp, ALU.add)
                D()

            def spread(s, src_, tmp, dst_, width):
                TT(tmp, src_, bc(seg[s, "last"][:, :], width), ALU.mult)
                D()
                for f in range(width):
                    v.tensor_tensor_scan(dst_[:, COLS - 1::-1, f] if dst_.shape[1] == COLS else dst_[:, COLS - 1::-1, f],
                                         seg[s, "notlast"][:, ::-1], tmp[:, ::-1, f], 0.0, ALU.mult, ALU.add)
                D()
                ask()
                v.tensor_copy(carry[:, 0:width], psY[:, 0:width])
                D()
                TT(tmp, bc(seg[s, "tail"][:, :], width), bt(carry[:, 0:width], COLS), ALU.mult)
                D()
                TT(dst_[:, 0:COLS, :], dst_[:, 0:COLS, :], tmp, ALU.add)
                D()

            def count_segments(s):
                v.memset(pos[:, :], 1.0)
                D()
                v.tensor_tensor_scan(V[:, 1:COLS + 1, 0], seg[s, "same"][:, :], pos[:, :], 0.0, ALU.mult, ALU.add)
                ask()
                v.tensor_copy(carry[:, 0:1], psY[:, 0:1])
                D()
                STT(pos[:, :], seg[s, "head"][:, :], carry[:, 0:1], V[:, 1:COLS + 1, 0], ALU.mult, ALU.add)
                D()

            def at_last(s, key, mult, add, index):
                TS(dig[:, :], key[:, :], float(mult), float(add) - NOWHERE, ALU.mult, ALU.add)
                D()
                TT(dig[:, :], dig[:, :], seg[s, "last"][:, :], ALU.mult)
                D()
                TS(index[:, :], dig[:, :], NOWHERE, None, ALU.add)
                D()

            def norm(n, X, cols, k, o):
                v.tensor_reduce(mean[0:n, 0:cols], X, AX.X, ALU.add)
                D()
                STT(xc[0:n, 0:cols, :], bc(mean[0:n, 0:cols], F), -1.0 / F, X, ALU.mult, ALU.add)
                D()
                TT(sq[0:n, 0:cols, :], xc[0:n, 0:cols, :], xc[0:n, 0:cols, :], ALU.mult)
                D()
                v.tensor_reduce(var[0:n, 0:cols], sq[0:n, 0:cols, :], AX.X, ALU.add)
                signal("var_ready")
                v.wait_ge(S["std_ready"], k)
                v.reciprocal(rstd[0:n, 0:cols], std[0:n, 0:cols])
                D()
                STT(o, xc[0:n, 0:cols, :], 0.0, bc(rstd[0:n, 0:cols], F), ALU.max, ALU.mult)
                D()

            def product(k):
                signal("h_ready")
                v.wait_ge(S["y_ready"], k)

            def chunk(tile, c, n=CHUNK):
                return tile[:, ds(c * n, n), :]

            def col(a_, c):
                return a_[:, ds(c * CHUNK, CHUNK)]

            hcf = hc[:, :].rearrange("p (t f) -> p t f", f=F)
            hc16 = hc[:, 0:CHUNK * HID].rearrange("p (t f) -> p t f", f=HID)
            y16 = psY[:, 0:CHUNK * HID].rearrange("p (t f) -> p t f", f=HID)
            y32 = psY[:, :].rearrange("p (b r) -> p b r", b=2)[:, :, 0:14 * F].rearrange("p b (t f) -> p b t f", f=F)

            def dense_step(k, st, j, n, cols, wait):
                v.wait_ge(S["dense_in"], k * 16 + 16)
                X = dx[0:n, 0:cols, :]
                X1 = dx1[0:n, 0:cols, :]
                norm(n, X, cols, j * 2 + (ln0[st] + 1), hcf[0:n, 0:cols, :])
                product(j * 2 + (y0[st] + 1))
                TT(xc[0:n, 0:cols, 0:HID], psY[0:n, 0:cols * HID].rearrange("p (t f) -> p t f", f=HID), bt(b1r[0:n, :], cols), ALU.add)
                D()
                TS(hc16[0:n, 0:cols, :], xc[0:n, 0:cols, 0:HID], 0.0, None, ALU.max)
                TT(X, X, bt(b2r[0:n, :], cols), ALU.add)
                product(j * 2 + (y0[st] + 2))
                m = 5 if cols == DN else cols
                b = -(-cols // (2 * m))
                y = psY[0:n, 0:512 * b].rearrange("p (b r) -> p b r", b=b)[:, :, 0:cols // b * F].rearrange("p b (t f) -> p b t f", f=F)
                TT(X1.rearrange("p (b t) f -> p b t f", b=b), y, X.rearrange("p (b t) f -> p b t f", b=b), ALU.add)
                v.drain().then_inc(S["dense_used"], 1)
                norm(n, X1, cols, j * 2 + (ln0[st] + 2), hcf[0:n, 0:cols, :])
                TT(X1, X1, bt(br[0:n, :], cols), ALU.add)
                D()
                if wait is not None:
                    v.wait_ge(S["dense_stored"], wait)
                STT(dout[0:n, 0:cols, :], hcf[0:n, 0:cols, :], ALPHA, X1, ALU.mult, ALU.add)
                signal("dense_ready")

            def dense(i):
                if i == 0:
                    dense_step(0, "dense0", 0, P, DN, None)
                with v.Fori(i == 0, DPART) as j:
                    k = j + i * DPART
                    dense_step(k, f"dense{i}", j, P, DN, k * 16)

            segments("d", key_d, 0)
            count_segments("d")
            v.tensor_copy(pay[:, :, 1], pos[:, :])
            TS(pay[:, :, 0], iota_e[:, :], 1.0, None, ALU.add)
            at_last("d", key_d, ROW // 2, INFO // 2, idx)
            at_last("d", key_d, 1, 0, idx_outd)
            signal("pay_ready")

            def digit_pass(k, width):
                UN = 7
                v.memset(hist[:, 0:width], 0.0)
                D()
                with v.Fori(0, COLS // UN) as t:
                    for u in range(UN):
                        STT(hist[:, 0:width], iota_d[:, 0:width], dig[:, ds(t * UN + u, 1)], hist[:, 0:width], ALU.is_equal, ALU.add)
                        D()
                signal("hist_ready")
                v.wait_ge(S["base_ready"], k)
                v.tensor_copy(junk[:, 0:width], psT[:, 512:512 + width])
                v.memset(hist[:, 0:width], 1.0)
                D()
                v.tensor_tensor_scan(rank[:, 0:width], hist[:, 0:width], junk[:, 0:width], 0.0, ALU.mult, ALU.add)
                D()
                TT(rank[:, 0:width], rank[:, 0:width], junk[:, 0:width], ALU.subtract)
                D()
                TT(rank[:, 0:width], rank[:, 0:width], psT[:, 0:width], ALU.add)
                D()
                with v.Fori(0, COLS // UN) as t:
                    for u in range(UN):
                        STT(junk[:, 0:width], iota_d[:, 0:width], dig[:, ds(t * UN + u, 1)], rank[:, 0:width], ALU.is_equal, ALU.mult,
                            accum_out=pos[:, ds(t * UN + u, 1)])
                        STT(rank[:, 0:width], iota_d[:, 0:width], dig[:, ds(t * UN + u, 1)], rank[:, 0:width], ALU.is_equal, ALU.add)
                        D()

            TS(dig_i[:, :], SI[:, :], DIGIT - 1, None, ALU.bitwise_and)
            D()
            v.tensor_copy(dig[:, :], dig_i[:, :])
            D()
            digit_pass(1, DIGIT)
            v.wait_ge(S["info_scattered"], 1)
            v.tensor_copy(idx[:, :], pos[:, :])
            v.tensor_copy(pay[:, :, 0], key_s[:, :])
            v.tensor_copy(pay[:, :, 1], iota_e[:, :])
            signal("pay_ready")
            dense(0)
            v.wait_ge(S["reloaded"], 16)
            v.tensor_copy(dig_i[:, :], pay[:, :, 0])
            D()
            TS(dig_i[:, :], dig_i[:, :], 8, None, ALU.logical_shift_right)
            D()
            v.tensor_copy(dig[:, :], dig_i[:, :])
            D()
            digit_pass(2, HIGH)
            v.tensor_copy(idx[:, :], pos[:, :])
            signal("pay_ready")
            dense(1)
            v.wait_ge(S["reloaded"], 32)
            v.tensor_copy(key_p[:, :], pay[:, :, 0])
            v.tensor_copy(idx_perm[:, :], pay[:, :, 1])
            D()
            segments("p", key_p, 1)
            count_segments("p")
            v.tensor_copy(pay[:, :, 0], pos[:, :])
            TS(pay[:, :, 1], iota_e[:, :], 1.0, None, ALU.add)
            at_last("p", key_p, ROW // 2, INFO // 2 + 1, idx)
            at_last("p", key_p, 1, 0, idx_outs)
            signal("pay_ready")

            dense(2)
            dense_step(DSTEPS, "dense_rest", 0, RP, GROUP, 16 * DSTEPS)

            def lookup(last, index, at):
                a_, b_ = dig[:, at], hasnot[:, at]
                TS(b_, last, 0.0, None, ALU.is_equal)
                TS(a_, iota_e[:, at], float(SLOTS), None, ALU.add)
                D()
                TT(a_, a_, b_, ALU.mult)
                D()
                TT(a_, a_, last, ALU.add)
                D()
                TT(a_, a_, b_, ALU.add)
                D()
                TS(a_, a_, -1.0, None, ALU.add)
                D()
                v.tensor_copy(index[:, at], a_)

            def inverse_roots(rows, c, k):
                v.wait_ge(S["roots_done"], k)
                v.reciprocal(inv[:, rows, ds(c * CHUNK, CHUNK)], roots[:, rows, ds(c * CHUNK, CHUNK)])

            def s1(c, wait):
                at = ds(c * CHUNK, CHUNK)
                v.wait_ge(S["cols_ready"], c + (col0["xs"] + 1))
                TS(roots[:, GCN_S, at], XS[:, at, INFO + 1], 1.0, None, ALU.add)
                TS(roots[:, OUT_S, at], XS[:, at, INFO + 2], 1.0, None, ALU.max)
                norm(P, XS[:, at, 0:F], CHUNK, c + (ln0["s1"] + 1), hcf)
                inverse_roots(ROOTS_S, c, c + 1)
                product(c + (y0["s1"] + 1))
                TT(G16[:, at, :], y16, bc(col(inv[:, GCN_S, :], c), HID), ALU.mult)
                TT(gS[:, :, HID:2 * HID], y16, bt(b1r[:, :], CHUNK), ALU.add)
                D()
                if wait:
                    v.wait_ge(S["local_stored"], c * 16)
                TS(gS[:, :, 0:HID], gS[:, :, HID:2 * HID], 0.0, None, ALU.max)
                scan("d", c, G16, V, HID)
                signal("local_ready")
            s1(0, False)
            with v.Fori(1, CHUNKS) as c:
                s1(c, True)
            lookup(XS[:, :, INFO], idx_q, slice(0, COLS))
            v.tensor_copy(pos[:, :], dig[:, :])
            signal("lookup_ready")

            live, place, rows = hist[:, 0:COLS], rank[:, 0:COLS], junk[:, 0:COLS]
            count, ofseg = V[:, 1:, HID + 1], V[:, 1:, HID]
            TS(live, hasnot[:, :], -1.0, 1.0, ALU.mult, ALU.add)
            v.memset(place, 1.0)
            D()
            v.tensor_tensor_scan(count, place, live, 0.0, ALU.mult, ALU.add)
            v.tensor_tensor_scan(ofseg, seg["d", "same"][:, :], live, 0.0, ALU.mult, ALU.add)
            ask()
            v.tensor_copy(sm[:, 0:1], psY[:, 0:1])
            TS(sm[:, 1:2], psY[:, 512:513], 1.0 / (P * LIVE), (P * LIVE - 0.5) / (P * LIVE) - 0.5, ALU.mult, ALU.add)
            D()
            v.tensor_copy(groups_i[:, :], sm[:, 1:2])
            D()
            TS(sm[:, 1:2], groups_i[:, :], 1.0, None, ALU.max)
            D()
            v.tensor_copy(groups_i[:, :], sm[:, 1:2])
            TS(sm[:, 2:3], sm[:, 1:2], float(LIVE), None, ALU.mult)
            D()
            v.reciprocal(sm[:, 3:4], sm[:, 2:3])
            TS(sm[:, 4:5], sm[:, 2:3], -1.0, float(COLS), ALU.mult, ALU.add)
            TS(count, count, sm[:, 0:1], -1.0, ALU.add, ALU.add)
            D()
            TS(rows, count, 0.5, sm[:, 3:4], ALU.add, ALU.mult)
            D()
            TS(rows, rows, -0.5, None, ALU.add)
            D()
            v.tensor_copy(idx[:, :], rows)
            D()
            v.tensor_copy(rows, idx[:, :])
            D()
            TS(place, rows, sm[:, 2:3], None, ALU.mult)
            D()
            TT(place, count, place, ALU.subtract)
            D()
            TS(dig[:, :], place, sm[:, 2:3], None, ALU.is_ge)
            TS(place, place, 0.0, None, ALU.is_lt)
            D()
            TT(rows, rows, dig[:, :], ALU.add)
            D()
            TT(rows, rows, place, ALU.subtract)
            D()
            STT(place, rows, sm[:, 4:5], count, ALU.mult, ALU.add)
            D()
            TS(dig[:, :], place, -NOWHERE, None, ALU.add)
            TS(place, place, 1.0, None, ALU.add)
            D()
            TT(dig[:, :], dig[:, :], live, ALU.mult)
            D()
            TS(idx[:, :], dig[:, :], NOWHERE, None, ALU.add)
            ask()
            v.tensor_copy(carry[:, 0:1], psY[:, 0:1])
            D()
            STT(ofseg, seg["d", "head"][:, :], carry[:, 0:1], ofseg, ALU.mult, ALU.add)
            D()
            STT(cpos[:, :], ofseg, 0.0, place, ALU.is_gt, ALU.mult)
            signal("live_counted")
            v.wait_ge(S["dense_stored"], 16 * (DSTEPS + 1))
            with v.Fori(0, CHUNKS) as c:
                at = ds(c * CHUNK, CHUNK)
                v.wait_ge(S["cols_ready"], c + (col0["xd"] + 1))
                TS(roots[:, GCN_D, at], XD[:, at, INFO + 1], 1.0, None, ALU.add)
                TS(roots[:, IN_D, at], XD[:, at, INFO + 1], 1.0, None, ALU.max)
                TS(roots[:, OUT_D, at], XD[:, at, INFO + 2], 1.0, None, ALU.max)
                norm(P, XD[:, at, 0:F], CHUNK, c + (ln0["d1"] + 1), hcf)
                inverse_roots(ROOTS_D, c, c + (CHUNKS + 1))
                product(c + (y0["d1"] + 1))
                TT(Z16[:, at, :], y16, bc(col(inv[:, GCN_D, :], c), HID), ALU.mult)
                D()
            v.tensor_copy(cpay[:, :, 0], pos[:, :])
            TS(cpay[:, :, 1], XD[:, :, INFO], -1.0, None, ALU.add)
            v.tensor_copy(cpay[:, :, 2], key_d[:, :])
            v.memset(cpay[:, :, 3], 0.0)
            signal("pay_ready")
            STT(a_d[:, :], inv[:, IN_D, :], 1.0 - ALPHA, inv[:, OUT_D, :], ALU.mult, ALU.mult)
            carry_in("d", V[:, 1:, 0:HID], B[:, :, 0:HID], HID)
            TT(V[:, 1:, 0:HID], V[:, 1:, 0:HID], Z16, ALU.add)
            TT(a_head[:, :], a_d[:, :], seg["d", "head"][:, :], ALU.mult)
            D()
            TT(V[:, 1:, 0:HID], V[:, 1:, 0:HID], bc(inv[:, GCN_D, :], HID), ALU.mult)
            D()
            TT(V[:, 1:, 0:HID], V[:, 1:, 0:HID], bt(b1r[:, :], COLS), ALU.add)
            D()
            STT(G16, V[:, 1:, 0:HID], 0.0, bc(inv[:, GCN_D, :], HID), ALU.max, ALU.mult)
            signal("rows_ready")
            v.wait_ge(S["rows_stored"], 16)
            v.tensor_copy(Z16, G16)
            D()
            signal("own_kept")
            v.wait_ge(S["reloaded"], 48)
            groups = v.value_load(groups_i[0:1, 0:1], min_val=1, max_val=LIVES)
            key_c = cpay[:, :, 2]
            v.tensor_copy(idx_cq[:, :], cpay[:, :, 0])
            v.tensor_copy(idx_cd[:, :], cpay[:, :, 1])
            v.memset(same_c[:, 0:1], 0.0)
            TT(same_c[:, 1:COLS], cpay[:, 1:COLS, 2], cpay[:, 0:COLS - 1, 2], ALU.is_equal)
            TS(head_c[:, :], key_c, cpay[:, 0, 2:3], None, ALU.is_equal)
            v.tensor_copy(sm[:, 5:6], cpay[:, ds(groups * LIVE - 1, 1), 2])
            v.tensor_copy(kb[:, :], cpay[:, 0, 2:3].to_broadcast([P, P]))
            ask()
            STT(fwd_c[:, :], psT[:, 0:P], sm[:, 5:6], later[:, :], ALU.is_equal, ALU.mult)
            D()
            with v.Fori(0, CHUNKS) as c:
                v.wait_ge(S["cols_ready"], c + (col0["g"] + 1))
                v.tensor_copy(hc16, G16[:, ds(c * CHUNK, CHUNK), :])
                product(c * 2 + (y0["x1"] + 1))
                v.wait_ge(S["local_stored"], c * 16 + 16 * CHUNKS)
                TT(gS[:, :, :].rearrange("p (b t) f -> p b t f", b=2), y32, XS[:, ds(c * CHUNK, CHUNK), 0:F].rearrange("p (b t) f -> p b t f", b=2), ALU.add)
                D()
                TT(gS[:, :, :], gS[:, :, :], bt(b2r[:, :], CHUNK), ALU.add)
                signal("local_ready")
                scan("d", c, G16, V, HID)
                TT(hc16, V[:, ds(c * CHUNK + 1, CHUNK), 0:HID], Z16[:, ds(c * CHUNK, CHUNK), :], ALU.add)
                D()
                TT(hc16, hc16, bc(col(inv[:, GCN_D, :], c), HID), ALU.mult)
                product(c * 2 + (y0["x1"] + 2))
                TT(xc[:, :, :].rearrange("p (b t) f -> p b t f", b=2), y32, XD[:, ds(c * CHUNK, CHUNK), 0:F].rearrange("p (b t) f -> p b t f", b=2), ALU.add)
                D()
                TT(XD[:, ds(c * CHUNK, CHUNK), 0:F], xc[:, :, :], bt(b2r[:, :], CHUNK), ALU.add)
                D()
            ask()
            v.tensor_copy(hc[:, 0:HID], psY[:, 0:HID])
            TT(junk[:, 0:COLS], inv[:, GCN_D, :], seg["d", "head"][:, :], ALU.mult)
            product(y0["x1carry"] + 1)
            v.tensor_copy(carry[:, :], psY[:, 0:F])
            D()
            for f in range(F):
                STT(V[:, 1:, f], junk[:, 0:COLS], carry[:, f:f + 1], XD[:, :, f], ALU.mult, ALU.add)
            signal("rows_ready")
            v.tensor_copy(XD[:, :, 0:F], V[:, 1:, :])
            D()
            v.wait_ge(S["rows_stored"], 32)

            with v.Fori(0, CHUNKS) as c:
                v.wait_ge(S["cols_ready"], c + (col0["x1"] + 1))
                at = ds(c * CHUNK, CHUNK)
                norm(P, chunk(G, c), CHUNK, c + (ln0["h1s"] + 1), hcf)
                v.wait_ge(S["local_stored"], c * 16 + 32 * CHUNKS)
                STT(gS[:, :, :], hcf, ALPHA, chunk(G, c), ALU.mult, ALU.add)
                v.drain().then_inc(S["local_ready"], 1)
                TT(hcf, hcf, bc(col(inv[:, OUT_S, :], c), F), ALU.mult)
                D()
                v.tensor_copy(chunk(G, c), hcf)
                STT(XS[:, at, 0:F], hcf, ALPHA, bc(col(hasnot, c), F), ALU.mult, ALU.mult)
                D()
                scan("d", c, G, V, F)
            with v.Fori(0, CHUNKS) as c:
                norm(P, XD[:, ds(c * CHUNK, CHUNK), 0:F], CHUNK, c + (ln0["h1d"] + 1), hcf)
                STT(chunk(B, c), hcf, ALPHA, bc(col(inv[:, OUT_D, :], c), F), ALU.mult, ALU.mult)
                D()

            def own(c):
                at = ds(c * CHUNK, CHUNK)
                TT(G[:, at, :], V[:, ds(c * CHUNK + 1, CHUNK), :], bc(col(a_d, c), F), ALU.mult)
                D()
                TT(G[:, at, :], G[:, at, :], B[:, at, :], ALU.add)
                D()

            def earlier_rows():
                v.tensor_copy(carry[:, :], psY[:, 0:F])
                D()
                for f in range(F):
                    STT(G[:, :, f], a_head[:, :], carry[:, f:f + 1], G[:, :, f], ALU.mult, ALU.add)
                signal("rows_ready")

            with v.Fori(0, CHUNKS) as c:
                own(c)
            ask()
            earlier_rows()

            for f in range(F):
                v.tensor_tensor_scan(XS[:, :, f], seg["d", "same"][:, :], XS[:, :, f], 0.0, ALU.mult, ALU.add)
            ask()
            v.tensor_copy(carry[:, :], psY[:, 0:F])
            D()
            for f in range(F):
                STT(XS[:, :, f], seg["d", "head"][:, :], carry[:, f:f + 1], XS[:, :, f], ALU.mult, ALU.add)
            D()
            TT(XS[:, :, 0:F], XS[:, :, 0:F], bc(a_d[:, :], F), ALU.mult)
            v.tensor_copy(XS[:, :, INFO], a_d[:, :])
            v.tensor_copy(XS[:, :, INFO + 1], cpos[:, :])
            D()
            TT(XS[:, :, 0:F], XS[:, :, 0:F], B[:, :, :], ALU.add)
            signal("rows_ready")
            lper = 16 * LIVE

            def keep(c):
                at = slice(c * LIVE, (c + 1) * LIVE)
                v.wait_ge(live_chunk[c], 2 * lper)
                v.tensor_copy(B[:, at, :], XS[:, at, 0:F])
                v.tensor_copy(a_c[:, at], XS[:, at, INFO])
                v.tensor_copy(cpos[:, at], XS[:, at, INFO + 1])
            nest(v, groups, LIVES, keep)
            signal("own_rows_kept")
            TT(a_head[:, :], a_c[:, :], head_c[:, :], ALU.mult)
            TS(dig[:, :], iota_e[:, :], 1.0, None, ALU.add)
            D()
            TT(dig[:, :], dig[:, :], cpos[:, :], ALU.is_equal)
            TS(junk[:, 0:COLS], cpay[:, :, 1], -NOWHERE, None, ALU.add)
            D()
            TT(dig[:, :], dig[:, :], junk[:, 0:COLS], ALU.mult)
            D()
            TS(idx_cu[:, :], dig[:, :], NOWHERE, None, ALU.add)

            def step(tail, count):
                def group(c):
                    at = slice(c * LIVE, (c + 1) * LIVE)
                    v.wait_ge(live_chunk[c], count)
                    for f in range(F):
                        v.tensor_tensor_scan(V[:, c * LIVE + 1:(c + 1) * LIVE + 1, f], same_c[:, at], G[:, at, f], V[:, c * LIVE:c * LIVE + 1, f], ALU.mult, ALU.add)
                    D()
                    TT(G[:, at, :], V[:, c * LIVE + 1:(c + 1) * LIVE + 1, :], bc(a_c[:, at], F), ALU.mult)
                    v.tensor_copy(last_c[:, :], V[:, (c + 1) * LIVE, :])
                    D()
                    TT(G[:, at, :], G[:, at, :], B[:, at, :], ALU.add)
                nest(v, groups, LIVES, group)
                v.drain().then_inc(S["tail_ready"], 1)
                v.wait_ge(S["carry_ready"], tail)
                v.tensor_copy(carry[:, :], psY[:, 0:F])
                D()

                def part(j):
                    at = slice(j * PART, (j + 1) * PART)
                    for f in range(F):
                        STT(G[:, at, f], a_head[:, at], carry[:, f:f + 1], G[:, at, f], ALU.mult, ALU.add)
                parts(v, groups, part)
                signal("prop_ready")

            step(14, lper)
            nest(v, groups, LIVES, lambda c: v.wait_ge(live_chunk[c], 3 * lper))
            lookup(XS[:, :, INFO + 1], idx_cl, slice(0, COLS))
            signal("consts_ready")
            with v.Fori(0, STEPS - 2) as r:
                step(r + 15, r * lper + 4 * lper)
            state["tail"] += STEPS - 1

            def out_rows(c):
                at = slice(c * LIVE, (c + 1) * LIVE)
                v.tensor_copy(XS[:, at, 0:F], G[:, at, :])
            nest(v, groups, LIVES, out_rows)
            signal("live_out_ready")
            v.wait_ge(S["reloaded"], 64)
            TT(V[:, 1:, :], XS[:, :, 0:F], bc(roots[:, OUT_D, :], F), ALU.mult)
            D()
            TT(V[:, 1:, :], V[:, 1:, :], XD[:, :, 0:F], ALU.add)
            D()
            TT(B[:, :, :], V[:, 1:, :], bt(br[:, :], COLS), ALU.add)
            signal("rows_ready")
            signal("out_rows_ready")
            spread("d", V[:, 1:, :], G[:, :, :], XD[:, :, 0:F], F)
            v.tensor_copy(XD[:, :, INFO + 2], XD[:, :, INFO + 3])
            v.tensor_copy(XD[:, :, INFO:INFO + 2], ea[:, :, :])
            D()
            v.tensor_copy(XD[:, :, INFO + 3], pos[:, :])
            signal("rows_ready")

            def lookups(c):
                at = ds(c * CHUNK, CHUNK)
                v.wait_ge(S["cols_ready"], c + (col0["pair"] + 1))
                v.tensor_copy(idx_q[:, at], XS[:, at, INFO + 3])
                lookup(XS[:, at, INFO + 2], SI, at)
                signal("lookup_ready")

            def spline(c):
                U = XS[:, ds(c * CHUNK, CHUNK), INFO:INFO + 2]
                h = 2.0 / (BASIS - 1)
                for k in range(BASIS):
                    TS(tent[:, :, k::BASIS], U, 1.0 - k * h, 1.0 / h, ALU.add, ALU.mult)
                D()
                TS(basis[:, :, 0:2 * BASIS], tent[:, :, :], -1.0, 1.0, ALU.mult, ALU.add)
                TS(tent[:, :, :], tent[:, :, :], 1.0, None, ALU.add)
                D()
                TT(tent[:, :, :], tent[:, :, :], basis[:, :, 0:2 * BASIS], ALU.min)
                D()
                TS(tent[:, :, :], tent[:, :, :], 0.0, None, ALU.max)
                D()
                for k in range(BASIS):
                    TT(basis[:, :, k * BASIS:(k + 1) * BASIS], tent[:, :, BASIS:2 * BASIS], tent[:, :, k:k + 1].to_broadcast([P, CHUNK, BASIS]), ALU.mult)
                norm(P, XS[:, ds(c * CHUNK, CHUNK), 0:F], CHUNK, c + (ln0["spline"] + 1), hcf)
                signal("h_ready")
                for t in range(CHUNK):
                    v.wait_ge(S["wide_ready"], c * CHUNK + (t + 1))
                    TT(prod[:, :].rearrange("p (k o) -> p k o", o=F), psB[t % 4][:, :].rearrange("p (k o) -> p k o", o=F), bc(basis[:, t, :], F), ALU.mult)
                    v.drain().then_inc(S["wide_used"], 1)
                    v.tensor_reduce(hcf[:, t, :], prod[:, :].rearrange("p (k o) -> p o k", o=F), AX.X, ALU.add)
                    D()
                v.tensor_copy(XD[:, ds(c * CHUNK, CHUNK), 0:F], hcf)
                D()
                scan("p", c, XD, V, F)

            v.wait_ge(S["rows_stored"], 16 * 5)
            with v.Fori(0, CHUNKS // 2) as c:
                lookups(c * 2)
                lookups(c * 2 + 1)
                spline(c)
            lookups(CHUNKS - 1)
            with v.Fori(CHUNKS // 2, CHUNKS) as c:
                spline(c)
            carry_in("p", V[:, 1:, :], XD[:, :, 0:F], F)
            v.wait_ge(S["cols_ready"], col0["x2"] + CHUNKS)
            TT(V[:, 1:, :], V[:, 1:, :], G[:, :, :], ALU.add)
            signal("rows_ready")
            spread("p", V[:, 1:, :], XD[:, :, 0:F], G, F)

            with v.Fori(0, CHUNKS) as c:
                norm(P, chunk(G, c), CHUNK, c * 2 + (ln0["att"] + 1), hcf)
                product(c * 2 + (y0["att"] + 1))
                v.tensor_copy(chunk(sc4, c), psY[:, 0:CHUNK * HEADS].rearrange("p (t h) -> p t h", h=HEADS))
                v.wait_ge(S["cols_ready"], c + (col0["x3"] + 1))
                norm(P, XS[:, ds(c * CHUNK, CHUNK), 0:F], CHUNK, c * 2 + (ln0["att"] + 2), hcf)
                v.tensor_copy(XS[:, ds(c * CHUNK, CHUNK), 0:F], hcf)
                product(c * 2 + (y0["att"] + 2))
                TT(chunk(sc4, c), chunk(sc4, c), psY[:, 0:CHUNK * HEADS].rearrange("p (t h) -> p t h", h=HEADS), ALU.add)
                D()
            TS(sc4, sc4, fbr[:, 0:1], None, ALU.add)
            D()
            STT(sc4, sc4, SLOPE, sc4, ALU.mult, ALU.max)
            TS(neg_same[:, :], seg["p", "same"][:, :], -1.0, HUGE, ALU.add, ALU.mult)
            TS(neg_head[:, :], seg["p", "head"][:, :], -1.0, HUGE, ALU.add, ALU.mult)
            TS(neg_bwd[:, :], seg["p", "bwd"][:, :], -1.0, HUGE, ALU.add, ALU.mult)
            D()
            for h in range(HEADS):
                v.tensor_tensor_scan(v4[:, 1:COLS + 1, h], neg_same[:, :], sc4[:, :, h], 0.0, ALU.add, ALU.max)
            D()
            for h in range(HEADS):
                v.tensor_copy(kb[:, :], v4[:, COLS, h:h + 1].to_broadcast([P, P]))
                ask()
                TT(junk[:, 0:P], psT[:, 0:P], neg_bwd[:, :], ALU.add)
                D()
                v.tensor_reduce(carry[:, h:h + 1], junk[:, 0:P], AX.X, ALU.max)
                D()
                TS(pos[:, :], neg_head[:, :], carry[:, h:h + 1], None, ALU.add)
                D()
                TT(v4[:, 1:COLS + 1, h], v4[:, 1:COLS + 1, h], pos[:, :], ALU.max)
                D()
            tmp4 = XD[:, :, 0:HEADS]
            spread("p", v4[:, 1:, :], tmp4, w4, HEADS)
            TT(sc4, sc4, w4[:, 0:COLS, :], ALU.subtract)
            signal("exp_ready")
            v.wait_ge(S["exp_done"], 1)
            for h in range(HEADS):
                v.tensor_tensor_scan(v4[:, 1:COLS + 1, h], seg["p", "same"][:, :], sc4[:, :, h], 0.0, ALU.mult, ALU.add)
            D()
            carry_in("p", v4[:, 1:, :], tmp4, HEADS)
            spread("p", v4[:, 1:, :], tmp4, w4, HEADS)
            v.reciprocal(v4[:, 1:, :], w4[:, 0:COLS, :])
            D()
            STT(sc4, sc4, 1.0 / HEADS, v4[:, 1:, :], ALU.mult, ALU.mult)
            D()
            with v.Fori(0, CHUNKS) as c:
                v.tensor_copy(hcf, XS[:, ds(c * CHUNK, CHUNK), 0:F])
                signal("h_ready")
                v.tensor_copy(att[:, :].rearrange("p (t h) -> p t h", h=HEADS), chunk(sc4, c))
                D()
                for g in range(CHUNK // GROUP):
                    v.wait_ge(S["wide_ready"], c * (CHUNK // GROUP) + (COLS + g + 1))
                    TT(prod[:, :].rearrange("p (k o) -> p k o", o=F), psB[g % 4][:, :].rearrange("p (k o) -> p k o", o=F),
                       bc(att[:, g * GROUP * HEADS:(g + 1) * GROUP * HEADS], F), ALU.mult)
                    v.drain().then_inc(S["wide_used"], 1)
                    v.tensor_reduce(gS[:, g * GROUP:(g + 1) * GROUP, :], prod[:, :].rearrange("p (t h o) -> p t o h", h=HEADS, o=F), AX.X, ALU.add)
                    D()
                v.tensor_copy(XD[:, ds(c * CHUNK, CHUNK), 0:F], gS[:, :, :])
                D()
                scan("p", c, XD, V, F)
            carry_in("p", V[:, 1:, :], XD[:, :, 0:F], F)
            TT(V[:, 1:, :], V[:, 1:, :], bt(br[:, :], COLS), ALU.add)
            D()
            TT(V[:, 1:, :], V[:, 1:, :], G[:, :, :], ALU.add)
            signal("out_rows_ready")


_INS = ["x", "src", "dst", "edge_attr_2", "L0_gnn_W1", "L0_gnn_b1", "L0_gnn_W2", "L0_gnn_b2", "L2_gnn_weight",
        "L3_gnn_w", "L3_gnn_fc_w", "L3_gnn_fc_b", "L3_gnn_bias"]


def kernel(**inputs):
    import numpy as _np
    import concourse.bacc as _bacc
    from concourse import mybir as _mybir
    from concourse.bass_utils import run_bass_kernel_spmd as _run

    nc = _bacc.Bacc("TRN2", target_bir_lowering=False, num_devices=1)
    arrays, args = {}, []
    for name in _INS:
        a = _np.ascontiguousarray(inputs[name])
        arrays[f"in_{name}_dram"] = a
        args.append(nc.dram_tensor(f"in_{name}_dram", a.shape, _mybir.dt.from_np(a.dtype), kind="ExternalInput").ap())
    args.append(nc.dram_tensor("out_0_dram", (N, F), F32, kind="ExternalOutput").ap())
    gnn_kernel(nc, *args)
    r = _run(nc, [arrays], core_ids=[0])
    return r.results[0]["out_0_dram"]
```

```python
from contextlib import ExitStack

import concourse.bass as bass
from concourse import mybir

F32 = mybir.dt.float32
BF16 = mybir.dt.bfloat16
I32 = mybir.dt.int32
ALU = mybir.AluOpType
ACT = mybir.ActivationFunctionType
AX = mybir.AxisListType

P = 128
N = 100000
E = 25000
F = 32
HID = 16
HEADS = 4
BASIS = 4
COLS = -(-E // P)
SLOTS = P * COLS
CHUNK = 28
CHUNKS = COLS // CHUNK
LIVE = 7
LIVES = COLS // LIVE
PART = 49
PARTS = COLS // PART
FULL_ROWS = E // COLS
REST = E - FULL_ROWS * COLS
INFO = F
ROW = F + 4
NODES = N + 8
DIGIT = 256
HIGH = N // DIGIT + 1
STEPS = 10
ALPHA = 0.1
EPS = 1e-5
SLOPE = 0.2
NOWHERE = float(1 << 22)
HUGE = 1e30
GROUP = 4
DN = CHUNK
DSTEPS = -(-N // (P * DN))
DENSE = (6, 6, 12, 4)
PAIR_ROWS = 98
RING = 6
BANKS = 3
OUT_SPLIT = (98, 126)
OUT_HALVES = (slice(0, OUT_SPLIT[0]), slice(OUT_SPLIT[0], COLS))
NIBBLE = 16
UPPER = -(-HIGH // NIBBLE)
FOUR = 4
INFO_SPLIT = 172
ds = bass.ds


def gnn_kernel(nc, x, src, dst, edge_attr, W1, b1, W2, b2, w_spline, w_gat, fc_w, fc_b, bias, out):
    assert sum(DENSE) == DSTEPS and PAIR_ROWS * 2 * P == SLOTS
    dense0 = [sum(DENSE[:i]) for i in range(len(DENSE) + 1)]
    assert COLS % CHUNK == 0 and REST > 0

    nodes = nc.dram_tensor("node_rows", (NODES, ROW), F32, kind="Internal").ap()
    sort1 = nc.dram_tensor("sorted_by_low_digit", (SLOTS, 2), F32, kind="Internal").ap()
    sort2 = nc.dram_tensor("sorted_by_src", (SLOTS, 2), F32, kind="Internal").ap()
    t_gcn = nc.dram_tensor("t_gcn", (2 * SLOTS, HID), F32, kind="Internal").ap()
    t_x1 = nc.dram_tensor("t_x1", (2 * SLOTS, F), F32, kind="Internal").ap()
    t_prop = nc.dram_tensor("t_prop", (SLOTS, F), F32, kind="Internal").ap()
    t_x2 = nc.dram_tensor("t_x2", (2 * SLOTS, F), F32, kind="Internal").ap()
    t_x3 = nc.dram_tensor("t_x3", (2 * SLOTS, F), F32, kind="Internal").ap()
    t_own = nc.dram_tensor("t_own", (SLOTS, ROW), F32, kind="Internal").ap()
    t_live = nc.dram_tensor("t_live", (2 * SLOTS, F), F32, kind="Internal").ap()
    live_rows = nc.dram_tensor("live_rows", (SLOTS, 4), F32, kind="Internal").ap()
    t_pair = nc.dram_tensor("t_pair", (SLOTS, ROW), F32, kind="Internal").ap()

    ctx = ExitStack()
    with ctx:
        def sb(name, shape, dt=F32):
            return ctx.enter_context(nc.sbuf_tensor(name, shape, dt))

        def ps(name, shape):
            return ctx.enter_context(nc.psum_tensor(name, shape, F32))

        def sem(name):
            return ctx.enter_context(nc.semaphore(name))

        big = sb("big", [P, 2 * COLS * ROW])
        XS = big[:, 0:COLS * ROW].rearrange("p (t w) -> p t w", w=ROW)
        XD = big[:, COLS * ROW:].rearrange("p (t w) -> p t w", w=ROW)
        G = sb("gathered", [P, COLS, F])
        V = sb("sums", [P, COLS + 1, F])
        B = sb("own_term", [P, COLS, F])
        G16 = G[:, :, :].rearrange("p t f -> p (t f)")[:, 0:COLS * HID].rearrange("p (t f) -> p t f", f=HID)
        HW = B[:, :, 0:HID]
        Z16 = B[:, :, HID:2 * HID]

        SI = sb("src_i", [P, COLS], I32)
        DI = sb("dst_i", [P, COLS], I32)
        idx_cq = sb("live_src_i", [P, COLS], I32)
        idx_cd = sb("live_dst_i", [P, COLS], I32)
        idx_cl = sb("live_lookup_i", [P, COLS], I32)
        idx_cu = sb("live_out_i", [P, COLS], I32)
        cpay = sb("live_payload", [P, COLS, 4])
        same_c = sb("same_live", [P, COLS])
        within_c = sb("within_live", [P, COLS])
        head_c = sb("head_live", [P, COLS])
        a_c = sb("prop_scale_live", [P, COLS])
        cpos = sb("live_place", [P, COLS])
        fwd_c = sb("fwd_live", [P, P])
        last_c = sb("last_live", [P, F])
        groups_i = sb("live_groups", [P, 1], I32)
        sm = sb("small", [P, 8])
        head_i = sb("head_out_i", [P, 1], I32)
        head_row = sb("head_row", [P, F])
        padrow = sb("pad_row", [P, 4])
        key_s = sb("src_f", [P, COLS])
        key_d = sb("dst_f", [P, COLS])
        key_p = sb("sorted_src_f", [P, COLS])
        dig = sb("digit_f", [P, COLS])
        pos = sb("position", [P, COLS])
        idx = sb("index_i", [P, COLS], I32)
        idx_q = sb("lookup_i", [P, COLS], I32)
        dig_i = idx_q
        idx_perm = sb("perm_i", [P, COLS], I32)
        idx_outd = sb("out_dst_i", [P, COLS], I32)
        idx_outs = sb("out_src_i", [P, COLS], I32)
        pay = sb("payload", [P, COLS, 2])
        iota_e = sb("edge_number", [P, COLS])
        iota_low = sb("low_digits", [P, DIGIT], BF16)
        iota_high = sb("high_digits", [P, HIGH], BF16)
        onehot = big[:, 0:RING * HIGH // 2].bitcast(BF16).rearrange("p (u h) -> p u h", h=HIGH)
        ones_b = sb("ones_b", [P, P], BF16)
        later_b = sb("later_b", [P, P], BF16)
        upto_b = sb("upto_b", [P, P], BF16)
        junk = sb("junk", [P, HIGH])
        ident = sb("identity", [P, P])
        later = sb("later", [P, P])
        earlier = sb("earlier", [P, P])
        ones = sb("ones", [P, P])
        kb = sb("key_columns", [P, P])
        nf = sb("next_first", [P, 2])
        seg = {}
        for s in "dp":
            for n in ("same", "last", "notlast", "head", "tail"):
                seg[s, n] = sb(f"{n}_{s}", [P, COLS])
            seg[s, "fwd"] = sb(f"fwd_{s}", [P, P])
            seg[s, "bwd"] = sb(f"bwd_{s}", [P, P])
        neg_same, neg_head = key_s, key_d
        neg_bwd = sb("neg_bwd", [P, P])
        roots = sb("roots", [P, 5, COLS])
        inv = sb("inverse_roots", [P, 5, COLS])
        GCN_S, OUT_S, GCN_D, IN_D, OUT_D = range(5)
        ROOTS_S, ROOTS_D = slice(0, 2), slice(2, 5)
        a_d = sb("prop_scale", [P, COLS])
        a_head = sb("prop_scale_head", [P, COLS])
        hasnot = sb("no_incoming", [P, COLS])
        hc = sb("staged", [P, CHUNK * F])
        hT = sb("staged_turned", [P, CHUNK * F])
        xc = sb("centred", [P, CHUNK, F])
        src_rows = hc[:, 0:2 * P].bitcast(I32)
        key_a, iota_a = a_head, hasnot
        hist = hT[:, 0:HIGH]
        rank = xc[:, :, :].rearrange("p t f -> p (t f)")[:, 0:HIGH]
        halves = V[:, :, :].rearrange("p t f -> p (t f)")[:, F:F + COLS * (UPPER + NIBBLE) // 2].bitcast(BF16)
        hot_upper = halves[:, 0:COLS * UPPER]
        hot_lower = halves[:, COLS * UPPER:]
        by_halves = hT[0:FOUR * UPPER, 0:UPPER * NIBBLE]
        of_column = sb("of_column", [FOUR * UPPER, FOUR])
        of_upper = sb("of_upper", [FOUR * UPPER, UPPER])
        read_out = (junk, hist, xc[:, :, :].rearrange("p t f -> p (t f)")[:, 400:400 + HIGH])
        sq = hc[:, :].rearrange("p (t f) -> p t f", f=F)
        mean = sb("mean", [P, CHUNK])
        var = sb("variance", [P, CHUNK])
        std = sb("std", [P, CHUNK])
        rstd = sb("rstd", [P, CHUNK])
        gS = sb("local_rows", [P, CHUNK, F])
        carry = sb("carry", [P, F])
        eps = sb("eps", [P, 1])
        zero = sb("zero", [P, 8])
        w1bd = sb("w1_blocks", [P, GROUP * HID])
        w2bd = sb("w2_blocks", [7 * HID, 7 * F])
        wsp = sb("w_spline_rows", [P, BASIS, F])
        wg = sb("w_gat_rows", [P, HEADS, F])
        wgbd = sb("w_gat_blocks", [P, GROUP * HEADS * F])
        wsum = sb("w_att", [P, 2, HEADS])
        prod = sb("prod", [P, 512])
        prod2 = sb("prod2", [P, 512])
        wa_s = sb("w_att_src_blocks", [P, GROUP * HEADS])
        wa_d = sb("w_att_dst_blocks", [P, GROUP * HEADS])
        b1r = sb("b1_rows", [P, HID])
        b2r = sb("b2_rows", [P, F])
        br = sb("bias_rows", [P, F])
        fcr = sb("fc_rows", [P, 2 * F])
        fbr = sb("fc_bias_rows", [P, 1])
        ea = sb("edge_attr", [P, COLS, 2])
        tent = sb("tents", [P, CHUNK, 2 * BASIS])
        falling = sb("falling", [P, CHUNK, 2 * BASIS])
        att = sb("weights", [P, CHUNK * HEADS])
        Bf = B[:, :, :].rearrange("p t f -> p (t f)")
        sc4, v4, w4 = (Bf[:, i * (COLS + 1) * HEADS:(i + 1) * (COLS + 1) * HEADS].rearrange("p (t h) -> p t h", h=HEADS) for i in range(3))
        sc4 = sc4[:, 0:COLS, :]
        outer = (prod2[:, :], xc[:, :, :].rearrange("p t f -> p (t f)")[:, 0:512])
        outer_t = (hT[:, 0:512], gS[:, :, :].rearrange("p t f -> p (t f)")[:, 0:512])
        dx, dx1, dout = (G[:, COLS // 2 + i * DN:COLS // 2 + (i + 1) * DN, :] for i in range(3))

        psT = ps("turned", [P, 1024])
        psY = ps("products", [P, 1024])
        psB = [ps(f"wide{i}", [P, 512]) for i in range(4)]

        live_chunk = [sem(f"live_gather{c}") for c in range(LIVES)]
        part_stored = [sem(f"live_part_stored{c}") for c in range(PARTS)]
        names = ("loads src_cleared src_loaded rows_cleared zeroed patterns node_rows_done keys_ready shift_done "
                 "sorted_done info_scattered rows_f rows_turned onehot_ready halves_ready counted starts_ready "
                 "rank_ready rank_used cols_ready roots_done var_ready std_ready h_ready ht_ps ht_sb y_ready "
                 "tail_ready carry_ready rows_ready rows_stored lookup_ready outer_ready outer_turned outer_kept "
                 "outer_used result_used wide_ready wide_used out_chunk exp_ready exp_done dense_in dense_used "
                 "dense_ready dense_stored out_rows_ready pay_ready reloaded own_kept local_ready local_stored "
                 "rounds_open live_cleared live_counted own_rows_kept prop_ready consts_ready live_out_ready "
                 "own_stored live_rows_cleared").split()
        S = {n: sem(n) for n in names}
        chunk_sem = [sem(f"gather_chunk{c}") for c in range(CHUNKS)]
        scat = sem("scattered")
        d_info = sem("d_info_scattered")
        own_reloaded = [sem(f"own_reloaded{i}") for i in range(2)]

        def bc(ap, n):
            return ap.unsqueeze(2).to_broadcast([ap.shape[0], ap.shape[1], n])

        def bt(ap, t):
            return ap.unsqueeze(1).to_broadcast([ap.shape[0], t, ap.shape[1]])

        order = [(f"dense{i}", DENSE[i], 2, ("w1", "w2")) for i in range(3)]
        order += [("s1", CHUNKS, 1, ("w1",)), ("d1", CHUNKS, 1, ("w1",)),
                  ("dense3", DENSE[3], 2, ("w1", "w2")),
                  ("x1", CHUNKS, 0, ("w2", "w2")), ("x1carry", 1, 0, ("w2",)), ("h1d", CHUNKS, 1, ()), ("h1s", CHUNKS, 1, ()),
                  ("spline", CHUNKS, 1, ()), ("att_src", CHUNKS, 1, ("was",)), ("att_dst", CHUNKS, 1, ("wad",)), ("msg", CHUNKS, 0, ("hp",))]
        ln0, lin0, y0 = {}, {}, {}
        a = b = d = 0
        for n, times, lns, kinds in order:
            ln0[n], lin0[n], y0[n] = a, b, d
            a += times * lns
            d += times * len(kinds) * (kinds != ("hp",))
            b += times * len(kinds)
        gathers = ["xs", "xd", "g", "x1", "pair", "x2", "x3"]
        col0 = {n: i * CHUNKS for i, n in enumerate(gathers)}

        def nest(eng, groups, n, body, c=0):
            body(c)
            if c + 1 < n:
                with eng.If(groups > c + 1):
                    nest(eng, groups, n, body, c + 1)

        def parts(eng, groups, body, j=0):
            body(j)
            if j + 1 < PARTS:
                with eng.If(groups > (j + 1) * (PART // LIVE)):
                    parts(eng, groups, body, j + 1)

        block = ctx.enter_context(nc.Block())

        @block.sync
        def _(sp):
            L = S["loads"]
            sp.wait_ge(S["src_cleared"], 1)
            sp.dma_start(src_rows[0:E // (2 * P), :], src[0:E // (2 * P) * 2 * P].rearrange("(p t) -> p t", t=2 * P)).then_inc(S["src_loaded"], 16)
            sp.dma_start(src_rows[E // (2 * P):PAIR_ROWS, 0:E % (2 * P)], src[E // (2 * P) * 2 * P:E].rearrange("(p t) -> p t", p=1)).then_inc(S["src_loaded"], 16)
            sp.wait_ge(S["zeroed"], 1)
            for tile, arr in ((SI, src), (DI, dst)):
                sp.dma_start(tile[0:FULL_ROWS, :], arr[0:FULL_ROWS * COLS].rearrange("(p t) -> p t", t=COLS)).then_inc(L, 16)
                sp.dma_start(tile[FULL_ROWS:FULL_ROWS + 1, 0:REST], arr[FULL_ROWS * COLS:E].rearrange("(p t) -> p t", t=REST)).then_inc(L, 16)
            sp.dma_start(ea[0:FULL_ROWS, :, :], edge_attr[0:FULL_ROWS * COLS, :].rearrange("(p t) c -> p t c", t=COLS)).then_inc(L, 16)
            sp.dma_start(ea[FULL_ROWS:FULL_ROWS + 1, 0:REST, :], edge_attr[FULL_ROWS * COLS:E, :].rearrange("(p t) c -> p t c", t=REST)).then_inc(L, 16)
            for g in range(GROUP):
                sp.dma_start(w1bd[g * F:(g + 1) * F, g * HID:(g + 1) * HID], W1).then_inc(L, 16)
                sp.dma_start(wg[g * F:(g + 1) * F, :, :], w_gat.rearrange("h f o -> f h o")).then_inc(L, 16)
            for a_ in range(BASIS):
                sp.dma_start(wsp[:, a_, :], w_spline[a_, :, :, :].rearrange("b f o -> (b f) o")).then_inc(L, 16)
            for g in range(7):
                sp.dma_start(w2bd[g * HID:(g + 1) * HID, g * F:(g + 1) * F], W2).then_inc(L, 16)
            for tile, arr in ((b1r, b1), (b2r, b2), (br, bias), (fbr, fc_b)):
                sp.dma_start(tile[:, :], arr.partition_broadcast(P)).then_inc(L, 16)
            sp.dma_start(fcr[:, :], fc_w[0, :].partition_broadcast(P)).then_inc(L, 16)
            sp.dma_start(nodes[0:N, 0:F], x).then_inc(S["node_rows_done"], 16)
            sp.dma_start(nodes[0:N, F:ROW].rearrange("(p t) w -> p t w", p=32), zero[0:32, 0:4].unsqueeze(1).to_broadcast([32, N // 32, 4])).then_inc(S["node_rows_done"], 16)
            sp.dma_start(nodes[N:NODES, :].rearrange("r (a w) -> r a w", w=4), zero[0:NODES - N, 0:4].unsqueeze(1).to_broadcast([NODES - N, ROW // 4, 4])).then_inc(S["node_rows_done"], 16)

            def span(arr, k):
                at = slice(N - P * DN, N) if isinstance(k, int) and k == DSTEPS - 1 else ds(k * P * DN, P * DN)
                return arr[at, :].rearrange("(p t) f -> p t f", t=DN)

            def dense_in(k):
                sp.dma_start(dx[:, :, :], span(x, k)).then_inc(S["dense_in"], 16)

            def dense_out(k):
                sp.wait_ge(S["dense_ready"], k + 1)
                sp.dma_start(span(out, k), dout[:, :, :]).then_inc(S["dense_stored"], 16)

            def dense_part(i):
                if i == 0:
                    sp.wait_ge(S["live_cleared"], 32)
                    dense_in(0)
                last = i == len(DENSE) - 1
                with sp.Fori(dense0[i], dense0[i + 1] - 2 * last) as k:
                    sp.wait_ge(S["dense_used"], k + 1)
                    dense_in(k + 1)
                    dense_out(k)
                if last:
                    sp.wait_ge(S["dense_used"], DSTEPS - 1)
                    dense_in(DSTEPS - 1)
                    dense_out(DSTEPS - 2)
                    dense_out(DSTEPS - 1)

            sp.wait_ge(S["rows_cleared"], 1)
            for half in range(2):
                sp.dma_start(t_live[half * SLOTS:(half + 1) * SLOTS, :].rearrange("(p t) w -> p t w", t=COLS), G[:, :, :]).then_inc(S["live_cleared"], 16)
            sp.dma_start(live_rows.rearrange("(p t) w -> p t w", t=COLS), padrow[:, :].unsqueeze(1).to_broadcast([P, COLS, 4])).then_inc(S["live_rows_cleared"], 16)
            for i, key in enumerate((key_d, key_p)):
                sp.wait_ge(S["keys_ready"], i + 1)
                sp.dma_start(nf[0:P - 1, i:i + 1], key[1:P, 0:1]).then_inc(S["shift_done"], 16)
                if i == 0:
                    dense_part(0)
                    sp.wait_ge(S["sorted_done"], 1)
                    sp.dma_start(prod[0:PAIR_ROWS, :], sort1.rearrange("(p t) c -> p (t c)", t=2 * P)).then_inc(S["reloaded"], 16)
                    dense_part(1)
                    sp.wait_ge(S["sorted_done"], 2)
                    sp.dma_start(pay[:, :, :], sort2.rearrange("(p t) c -> p t c", t=COLS)).then_inc(S["reloaded"], 16)
            dense_part(2)
            locals_ = 0

            def store_local(table, width):
                nonlocal locals_
                tail = table[SLOTS:2 * SLOTS, :].rearrange("(p t) w -> p t w", t=COLS)
                with sp.Fori(0, CHUNKS) as c:
                    sp.wait_ge(S["local_ready"], c + (locals_ + 1))
                    sp.dma_start(tail[:, ds(c * CHUNK, CHUNK), :], gS[:, :, 0:width]).then_inc(S["local_stored"], 16)
                locals_ += CHUNKS

            def store_rows(table, tile, rows_ready):
                sp.wait_ge(S["rows_ready"], rows_ready)
                sp.dma_start(table, tile).then_inc(S["rows_stored"], 16)

            def front(table):
                return table[0:SLOTS, :].rearrange("(p t) w -> p t w", t=COLS)

            def back(table):
                return table[SLOTS:2 * SLOTS, :].rearrange("(p t) w -> p t w", t=COLS)

            store_local(t_gcn, HID)
            store_rows(front(t_gcn), G16, 1)
            dense_part(3)
            sp.wait_ge(S["sorted_done"], 3)
            sp.dma_start(cpay[:, :, :], live_rows.rearrange("(p t) c -> p t c", t=COLS)).then_inc(S["reloaded"], 16)
            sp.wait_ge(S["live_counted"], 1)
            groups = sp.value_load(groups_i[0:1, 0:1], min_val=1, max_val=LIVES)
            store_local(t_x1, F)
            store_rows(front(t_x1), V[:, 1:, :], 2)
            store_local(t_x2, F)
            store_rows(t_prop.rearrange("(p t) w -> p t w", t=COLS), G[:, :, :], 3)
            sp.wait_ge(S["rows_ready"], 4)
            sp.dma_start(t_own.rearrange("(p t) w -> p t w", t=COLS), XS).then_inc(S["own_stored"], 16)

            def store_live(view, tile):
                def part(j):
                    at = slice(j * PART, (j + 1) * PART)
                    sp.dma_start(view[:, at, :], tile[:, at, 0:F]).then_inc(part_stored[j], 16)
                parts(sp, groups, part)

            sp.wait_ge(S["prop_ready"], 1)
            store_live(front(t_live), G)
            sp.wait_ge(S["consts_ready"], 1)
            store_live(back(t_live), XS)
            with sp.Fori(0, STEPS - 3) as r:
                sp.wait_ge(S["prop_ready"], r + 2)
                store_live(front(t_live), G)
            sp.wait_ge(S["sorted_done"], 4)
            for i, at in enumerate(OUT_HALVES):
                sp.dma_start(XS[:, at, :], t_own.rearrange("(p t) w -> p t w", t=COLS)[:, at, :]).then_inc(own_reloaded[i], 16)
            store_rows(front(t_x2), V[:, 1:, :], 5)
            store_rows(t_pair.rearrange("(p t) w -> p t w", t=COLS), XD, 6)
            store_rows(back(t_x3), XS[:, :, 0:F], 7)
            store_rows(front(t_x3), V[:, 1:, :], 7)

        @block.scalar
        def _(act):
            def norm(n, k, width):
                act.wait_ge(S["var_ready"], k)
                nc.scalar.activation(std[0:n, 0:width], var[0:n, 0:width], ACT.Sqrt, bias=eps[0:n, :], scale=1.0 / F).then_inc(S["std_ready"], 1)

            def turned(rows, cols, k):
                act.wait_ge(S["ht_ps"], k)
                nc.scalar.copy(hT[0:rows, 0:cols], psT[0:rows, 0:cols]).then_inc(S["ht_sb"], 1)

            def keep(t, k):
                act.wait_ge(S["outer_turned"], k)
                nc.scalar.copy(outer_t[t % 2], psB[t % 2][:, :]).then_inc(S["outer_kept"], 1)

            def dense(i):
                st = f"dense{i}"
                with act.Fori(0, DENSE[i]) as k:
                    norm(P, k * 2 + (ln0[st] + 1), DN)
                    turned(P, DN * F, k * 2 + (lin0[st] + 1))
                    turned(7 * HID, DN // 7 * P, k * 2 + (lin0[st] + 2))
                    norm(P, k * 2 + (ln0[st] + 2), DN)

            for i in range(3):
                dense(i)
            for st, rows in (("s1", ROOTS_S), ("d1", ROOTS_D)):
                with act.Fori(0, CHUNKS) as c:
                    norm(P, c + (ln0[st] + 1), CHUNK)
                    i = nc.scalar.activation(roots[:, rows, ds(c * CHUNK, CHUNK)], roots[:, rows, ds(c * CHUNK, CHUNK)], ACT.Sqrt)
                    i.then_inc(S["roots_done"], 1)
                    turned(P, CHUNK * F, c + (lin0[st] + 1))
            dense(3)
            with act.Fori(0, CHUNKS) as c:
                turned(7 * HID, 4 * P, c * 2 + (lin0["x1"] + 1))
                turned(7 * HID, 4 * P, c * 2 + (lin0["x1"] + 2))
            turned(HID, P, lin0["x1carry"] + 1)
            with act.Fori(0, 2 * CHUNKS) as c:
                norm(P, c + (ln0["h1d"] + 1), CHUNK)
            norm(P, ln0["spline"] + 1, CHUNK)
            with act.Fori(0, CHUNKS - 1) as c:
                for g in range(CHUNK // GROUP):
                    keep(g, c * (CHUNK // GROUP) + (g + 1))
                norm(P, c + (ln0["spline"] + 2), CHUNK)
            for g in range(CHUNK // GROUP):
                keep(g, (CHUNKS - 1) * (CHUNK // GROUP) + (g + 1))
            with act.Fori(0, CHUNKS) as c:
                norm(P, c + (ln0["att_src"] + 1), CHUNK)
                turned(P, CHUNK * F, c + (lin0["att_src"] + 1))
            with act.Fori(0, CHUNKS) as c:
                norm(P, c + (ln0["att_dst"] + 1), CHUNK)
                turned(P, CHUNK * F, c + (lin0["att_dst"] + 1))
            act.wait_ge(S["exp_ready"], 1)
            nc.scalar.activation(sc4, sc4, ACT.Exp).then_inc(S["exp_done"], 1)
            with act.Fori(0, CHUNKS) as c:
                turned(P, CHUNK * F, c + (lin0["msg"] + 1))

        @block.tensor
        def _(pe):
            pe.wait_ge(S["patterns"], 1)

            def key_matrices(k):
                for j in range(2):
                    pe.wait_ge(S["tail_ready"], k + j + 1)
                    nc.tensor.transpose(psT[:, 0:P], kb[:, :], ident[:, :]).then_inc(S["carry_ready"], 1)

            def carry_row(k, M, rhs, w):
                pe.wait_ge(S["tail_ready"], k)
                nc.tensor.matmul(psY[:, 0:w], M[:, :], rhs, start=True, stop=True).then_inc(S["carry_ready"], 1)

            def turn_row(k):
                pe.wait_ge(S["tail_ready"], k)
                nc.tensor.transpose(psT[:, 0:P], kb[:, :], ident[:, :]).then_inc(S["carry_ready"], 1)

            def turn_rows(half, view):
                for j in range(2):
                    i = nc.tensor.transpose(psT[:, (2 * half + j) * P:(2 * half + j) * P + PAIR_ROWS], view(j), ident[0:PAIR_ROWS, 0:PAIR_ROWS])
                i.then_inc(S["rows_turned"], 1)

            def ranks(k, width):
                pe.wait_ge(S["halves_ready"], 2 * k + 1)
                m, n = FOUR * UPPER, FOUR * NIBBLE
                count = lambda upper, lower, first: nc.tensor.matmul(psT[0:m, 0:n], hot_upper[:, upper], hot_lower[:, lower], start=first, stop=True, skip_group_check=True)
                count(slice(0, m), slice(0, n), True)
                for u in range(1, 7):
                    count(slice(u * m, (u + 1) * m), slice(u * n, (u + 1) * n), False)
                with pe.Fori(1, COLS // FOUR // 7) as g:
                    for u in range(7):
                        count(ds((g * 7 + u) * m, m), ds((g * 7 + u) * n, n), False)
                pe.drain().then_inc(S["counted"], 1)
                pe.wait_ge(S["halves_ready"], 2 * k + 2)
                nc.tensor.matmul(psT[:, 512:512 + UPPER * NIBBLE], ones[0:FOUR * UPPER, :], by_halves, start=True, stop=True).then_inc(S["counted"], 1)
                pe.wait_ge(S["starts_ready"], k + 1)
                for b in range(BANKS):
                    nc.tensor.matmul(psB[b][:, 0:width], ident[:, :], rank[:, 0:width], start=True, stop=True, skip_group_check=True)

                def place(t, u, before):
                    pe.wait_ge(S["onehot_ready"], t + (k * COLS + 1))
                    add = lambda M, slot: nc.tensor.matmul(psB[u % BANKS][:, 0:width], M[:, :], onehot[:, slot % RING, 0:width], start=False, stop=True, skip_group_check=True)
                    if before >= BANKS:
                        pe.wait_ge(S["rank_used"], t + (k * COLS + 1 - BANKS))
                        add(upto_b, u - BANKS)
                    for b in range(1, min(before, BANKS - 1) + 1):
                        add(ones_b, u - b)
                    add(later_b, u).then_inc(S["rank_ready"], 1)

                for u in range(RING):
                    place(u, u, u)
                with pe.Fori(1, COLS // RING) as g:
                    for u in range(RING):
                        place(g * RING + u, u, BANKS)
                for u in range(COLS % RING):
                    place(COLS // RING * RING + u, u, BANKS)

            def turn(n, groups, gw, k):
                pe.wait_ge(S["h_ready"], k)
                for g in range(groups):
                    i = nc.tensor.transpose(psT[0:gw, g * P:g * P + n], hc[0:n, g * gw:(g + 1) * gw], ident[0:n, 0:n])
                i.then_inc(S["ht_ps"], 1)
                pe.wait_ge(S["ht_sb"], k)

            def lin(n, cols, kind, k):
                if kind == "w1":
                    turn(n, cols // GROUP, GROUP * F, k)
                    for g in range(cols // GROUP):
                        i = nc.tensor.matmul(psY[0:n, g * GROUP * HID:(g + 1) * GROUP * HID], hT[:, g * P:g * P + n], w1bd[:, :], start=True, stop=True)
                elif kind == "w2":
                    m = min(cols, 7)
                    turn(n, cols // m, m * HID, k)
                    for g in range(cols // m):
                        o = (g // 2) * 512 + (g % 2) * m * F
                        i = nc.tensor.matmul(psY[0:n, o:o + m * F], hT[0:m * HID, g * P:g * P + n], w2bd[0:m * HID, 0:m * F], start=True, stop=True)
                elif kind in ("was", "wad"):
                    turn(n, cols // GROUP, GROUP * F, k)
                    w = wa_s if kind == "was" else wa_d
                    for g in range(cols // GROUP):
                        i = nc.tensor.matmul(psY[0:n, g * GROUP * HEADS:(g + 1) * GROUP * HEADS], hT[:, g * P:g * P + n], w[:, :], start=True, stop=True)
                i.then_inc(S["y_ready"], 1)

            def spline(c):
                n = CHUNK // GROUP
                for g in range(n + 1):
                    if g < n:
                        pe.wait_ge(S["outer_ready"], c * n + (g + 1))
                        for t in range(GROUP):
                            i = nc.tensor.transpose(psB[g % 2][:, t * P:(t + 1) * P], outer[g % 2][:, t * P:(t + 1) * P], ident[:, :])
                        i.then_inc(S["outer_turned"], 1)
                    if g > 0:
                        pe.wait_ge(S["outer_kept"], c * n + g)
                        if g > 2:
                            pe.wait_ge(S["result_used"], c * n + (g - 2))
                        for t in range(GROUP):
                            i = nc.tensor.matmul(psB[2 + (g - 1) % 2][:, t * P:(t + 1) * P], outer_t[(g - 1) % 2][:, t * P:(t + 1) * P],
                                                 wsp[:, :, :].rearrange("p a o -> p (a o)"), start=True, stop=True)
                        i.then_inc(S["outer_used"], 1)

            def messages(c):
                turn(P, CHUNK // GROUP, GROUP * F, c + (lin0["msg"] + 1))
                n = CHUNK // GROUP
                for g in range(n):
                    if g >= 4:
                        pe.wait_ge(S["wide_used"], c * n + (g - 3))
                    nc.tensor.matmul(psB[g % 4][:, :], hT[:, g * P:(g + 1) * P], wgbd[:, :], start=True, stop=True).then_inc(S["wide_ready"], 1)

            def dense(i):
                with pe.Fori(0, DENSE[i]) as k:
                    lin(P, DN, "w1", k * 2 + (lin0[f"dense{i}"] + 1))
                    lin(P, DN, "w2", k * 2 + (lin0[f"dense{i}"] + 2))

            pe.wait_ge(S["rows_f"], 1)
            turn_rows(0, lambda j: prod[0:PAIR_ROWS, j * P:(j + 1) * P])
            ranks(0, DIGIT)
            key_matrices(0)
            carry_row(3, seg["d", "fwd"], V[:, COLS, 0:1], 1)
            pe.wait_ge(S["loads"], 16 * 30)
            dense(0)
            pe.wait_ge(S["reloaded"], 16)
            pairs = prod[0:PAIR_ROWS, :].rearrange("p (t c) -> p t c", c=2)
            for half in range(2):
                turn_rows(half, lambda j: pairs[:, j * P:(j + 1) * P, half])
            ranks(1, HIGH)
            dense(1)
            key_matrices(3)
            carry_row(6, seg["p", "fwd"], V[:, COLS, 0:1], 1)
            dense(2)
            with pe.Fori(0, CHUNKS) as c:
                lin(P, CHUNK, "w1", c + (lin0["s1"] + 1))
            pe.wait_ge(S["tail_ready"], 7)
            nc.tensor.matmul(psY[:, 0:1], later[:, :], V[:, COLS, HID + 1:HID + 2], start=True, stop=True)
            nc.tensor.matmul(psY[:, 512:513], ones[:, :], V[:, COLS, HID + 1:HID + 2], start=True, stop=True).then_inc(S["carry_ready"], 1)
            carry_row(8, seg["d", "fwd"], V[:, COLS, HID:HID + 1], 1)
            with pe.Fori(0, CHUNKS) as c:
                lin(P, CHUNK, "w1", c + (lin0["d1"] + 1))
            carry_row(9, seg["d", "fwd"], V[:, COLS, 0:HID], HID)
            dense(3)
            turn_row(10)
            with pe.Fori(0, CHUNKS) as c:
                lin(P, CHUNK, "w2", c * 2 + (lin0["x1"] + 1))
                lin(P, CHUNK, "w2", c * 2 + (lin0["x1"] + 2))
            carry_row(11, seg["d", "fwd"], V[:, COLS, 0:HID], HID)
            lin(P, 1, "w2", lin0["x1carry"] + 1)
            carry_row(12, seg["d", "fwd"], V[:, COLS, :], F)
            carry_row(13, seg["d", "fwd"], XS[:, COLS - 1, 0:F], F)
            carry_row(14, fwd_c, last_c[:, :], F)
            with pe.Fori(0, STEPS - 2) as r:
                carry_row(r + 15, fwd_c, last_c[:, :], F)
            k = STEPS + 13
            carry_row(k, seg["d", "bwd"], XD[:, 0, 0:F], F)
            k += 1
            with pe.Fori(0, CHUNKS) as c:
                spline(c)
            carry_row(k, seg["p", "fwd"], V[:, COLS, :], F)
            carry_row(k + 1, seg["p", "bwd"], G[:, 0, :], F)
            with pe.Fori(0, CHUNKS) as c:
                lin(P, CHUNK, "was", c + (lin0["att_src"] + 1))
            with pe.Fori(0, CHUNKS) as c:
                lin(P, CHUNK, "wad", c + (lin0["att_dst"] + 1))
            k += 2
            for h in range(HEADS):
                turn_row(k + h)
            k += HEADS
            carry_row(k, seg["p", "bwd"], w4[:, 0, :], HEADS)
            carry_row(k + 1, seg["p", "fwd"], v4[:, COLS, :], HEADS)
            carry_row(k + 2, seg["p", "bwd"], w4[:, 0, :], HEADS)
            with pe.Fori(0, CHUNKS) as c:
                messages(c)
            carry_row(k + 3, seg["p", "fwd"], V[:, COLS, :], F)

        @block.gpsimd
        def _(pool):
            pool.iota(iota_e[:, :], [[1, COLS]], base=0, channel_multiplier=COLS, allow_small_or_imprecise_dtypes=True)
            pool.iota(iota_a[:, :], [[P, COLS]], base=0, channel_multiplier=1, allow_small_or_imprecise_dtypes=True)
            pool.iota(iota_low[:, :], [[1, DIGIT]], base=0, channel_multiplier=0, allow_small_or_imprecise_dtypes=True)
            pool.iota(iota_high[:, :], [[1, HIGH]], base=-(HIGH // 2), channel_multiplier=0, allow_small_or_imprecise_dtypes=True)
            pool.memset(ones[:, :], 1.0)
            pool.drain()
            pool.affine_select(out=later[:, :], in_=ones[:, :], compare_op=ALU.is_gt, fill=0.0, base=0, pattern=[[1, P]], channel_multiplier=-1)
            pool.affine_select(out=earlier[:, :], in_=ones[:, :], compare_op=ALU.is_gt, fill=0.0, base=0, pattern=[[-1, P]], channel_multiplier=1)
            pool.affine_select(out=ident[:, :], in_=ones[:, :], compare_op=ALU.is_equal, fill=0.0, base=0, pattern=[[-1, P]], channel_multiplier=1)
            pool.drain().then_inc(S["patterns"], 1)

            def offs(t, i):
                return bass.IndirectOffsetOnAxis(ap=i[:, t:t + 1], axis=0)

            def scatter(view, i, rows, limit, done, value):
                for t in range(COLS):
                    pool.indirect_dma_start(view, offs(t, i), rows(t), None, bounds_check=limit, oob_is_err=False).then_inc(scat, 16)
                pool.wait_ge(scat, 16 * COLS * value)
                pool.sem_inc(done, 1)

            def gather(table, i, cols, count, lookups=None):
                for c in range(CHUNKS + 1):
                    if c < CHUNKS and lookups is not None:
                        pool.wait_ge(S["lookup_ready"], lookups + c + 1)
                    if c < CHUNKS:
                        for t in range(c * CHUNK, (c + 1) * CHUNK):
                            pool.indirect_dma_start(cols(t), None, table, offs(t, i)).then_inc(chunk_sem[c], 16)
                    if c > 0:
                        pool.wait_ge(chunk_sem[c - 1], count)
                        pool.sem_inc(S["cols_ready"], 1)

            per = 16 * CHUNK
            info_limit = NODES * (ROW // 2) - 1
            pool.wait_ge(S["pay_ready"], 1)
            scatter(sort1, idx, lambda t: pay[:, t, :], SLOTS - 1, S["sorted_done"], 1)
            info = nodes.rearrange("n (a w) -> (n a) w", w=2)

            def scatter_info(t0, t1):
                for t in range(t0, t1):
                    pool.indirect_dma_start(info, offs(t, idx_cq), cpay[:, t, 0:2], None, bounds_check=info_limit, oob_is_err=False).then_inc(d_info, 16)

            pool.wait_ge(S["node_rows_done"], 48)
            pool.wait_ge(S["pay_ready"], 2)
            scatter_info(0, INFO_SPLIT)
            pool.wait_ge(S["pay_ready"], 3)
            scatter(sort2, idx, lambda t: pay[:, t, :], SLOTS - 1, S["sorted_done"], 2)
            scatter_info(INFO_SPLIT, COLS)
            pool.wait_ge(d_info, 16 * COLS)
            pool.wait_ge(S["pay_ready"], 4)
            scatter(info, idx, lambda t: pay[:, t, :], info_limit, S["info_scattered"], 3)

            gather(nodes, SI, lambda t: XS[:, t, :], per)
            gather(nodes, DI, lambda t: XD[:, t, :], 2 * per)
            pool.wait_ge(S["live_cleared"], 32)
            pool.wait_ge(S["live_rows_cleared"], 16)
            pool.wait_ge(S["pay_ready"], 5)
            scatter(live_rows, idx, lambda t: cpay[:, t, :], SLOTS - 1, S["sorted_done"], 4)
            pool.wait_ge(S["lookup_ready"], 1)
            pool.wait_ge(S["local_stored"], 16 * CHUNKS)
            pool.wait_ge(S["rows_stored"], 16)
            pool.wait_ge(S["own_kept"], 1)
            gather(t_gcn, idx_q, lambda t: G16[:, t, :], 3 * per)
            pool.wait_ge(S["local_stored"], 32 * CHUNKS)
            pool.wait_ge(S["rows_stored"], 32)
            pool.wait_ge(S["live_counted"], 1)
            pool.wait_ge(S["dense_stored"], 16 * DSTEPS)
            gather(t_x1, idx_q, lambda t: G[:, t, :], 4 * per)
            groups = pool.value_load(groups_i[0:1, 0:1], min_val=1, max_val=LIVES)
            lper = 16 * LIVE

            def gather_live(table, i, cols):
                def group(c):
                    for t in range(c * LIVE, (c + 1) * LIVE):
                        pool.indirect_dma_start(cols(t), None, table, offs(t, i)).then_inc(live_chunk[c], 16)
                nest(pool, groups, LIVES, group)

            pool.wait_ge(S["rows_stored"], 48)
            gather_live(t_prop, idx_cq, lambda t: G[:, t, :])
            pool.wait_ge(S["own_stored"], 16)
            gather_live(t_own, idx_cd, lambda t: XS[:, t, :])
            pool.wait_ge(S["own_rows_kept"], 1)
            gather_live(t_own, idx_cq, lambda t: XS[:, t, :])
            with pool.Fori(0, STEPS - 2) as r:
                def part(j):
                    pool.wait_ge(part_stored[j], r * 16 + 32)
                    pool.sem_inc(S["rounds_open"], 1)
                parts(pool, groups, part)
                gather_live(t_live, idx_cl, lambda t: G[:, t, :])
            pool.wait_ge(S["live_out_ready"], 1)

            def group(c):
                for t in range(c * LIVE, (c + 1) * LIVE):
                    pool.indirect_dma_start(t_own, offs(t, idx_cu), XS[:, t, :], None, bounds_check=SLOTS - 1, oob_is_err=False).then_inc(live_chunk[c], 16)
            nest(pool, groups, LIVES, group)
            nest(pool, groups, LIVES, lambda c: pool.wait_ge(live_chunk[c], (STEPS + 2) * lper))
            pool.sem_inc(S["sorted_done"], 1)
            pool.wait_ge(S["out_rows_ready"], 1)
            def scatter_out(t0, t1):
                for t in range(t0, t1):
                    pool.indirect_dma_start(out, offs(t, idx_outd), B[:, t, :], None, bounds_check=N - 1, oob_is_err=False).then_inc(scat, 16)

            scatter_out(0, OUT_SPLIT[0])
            pool.wait_ge(S["rows_stored"], 16 * 5)
            gather(t_pair, idx_perm, lambda t: XS[:, t, :], 5 * per)
            pool.wait_ge(S["local_stored"], 48 * CHUNKS)
            pool.wait_ge(scat, 16 * (COLS * 4 + OUT_SPLIT[0]))
            gather(t_x2, idx_q, lambda t: G[:, t, :], 6 * per, lookups=1)
            pool.wait_ge(S["out_rows_ready"], 2)
            scatter_out(OUT_SPLIT[0], OUT_SPLIT[1])
            pool.wait_ge(S["rows_stored"], 16 * 7)
            gather(t_x3, SI, lambda t: XS[:, t, 0:F], 7 * per)
            scatter_out(OUT_SPLIT[1], COLS)
            pool.wait_ge(scat, 16 * COLS * 5)
            for c in range(CHUNKS):
                pool.wait_ge(S["out_chunk"], c + 1)
                for t in range(c * CHUNK, (c + 1) * CHUNK):
                    pool.indirect_dma_start(out, offs(t, idx), XD[:, t, 0:F], None, bounds_check=N - 1, oob_is_err=False).then_inc(scat, 16)
            pool.wait_ge(S["out_rows_ready"], 3)
            pool.indirect_dma_start(out, offs(0, head_i), head_row[:, :], None, bounds_check=N - 1, oob_is_err=False).then_inc(scat, 16)
            pool.wait_ge(scat, 16 * (COLS * 6 + 1))

        @block.vector
        def _(v):
            state = {"tail": 0, "cols": 0, "local": 0, "wide": 0}
            TT, TS, STT = v.tensor_tensor, v.tensor_scalar, v.scalar_tensor_tensor

            def D():
                v.drain()

            def signal(name):
                v.drain().then_inc(S[name], 1)

            def ask():
                state["tail"] += 1
                signal("tail_ready")
                v.wait_ge(S["carry_ready"], state["tail"])

            v.memset(src_rows[:, :], N)
            signal("src_cleared")
            v.memset(SI[:, :], N)
            v.memset(DI[:, :], N)
            v.memset(ea[:, :, :], 0.0)
            v.memset(w1bd[:, :], 0.0)
            v.memset(w2bd[:, :], 0.0)
            v.memset(zero[:, :], 0.0)
            v.memset(eps[:, :], EPS)
            v.memset(nf[:, :], -1.0)
            v.memset(padrow[:, :], 0.0)
            D()
            v.memset(padrow[:, 2:3], -1.0)
            v.memset(a_c[:, :], 0.0)
            signal("zeroed")
            v.memset(V[:, 0, :], 0.0)
            v.wait_ge(S["patterns"], 1)
            v.wait_ge(S["src_loaded"], 32)
            v.tensor_copy(prod[:, 0:2 * P], src_rows[:, :])
            v.tensor_copy(ones_b[:, :], ones[:, :])
            v.tensor_copy(later_b[:, :], later[:, :])
            TT(upto_b[:, :], ones[:, :], later[:, :], ALU.subtract)
            signal("rows_f")

            def segments(s, key, i):
                g = lambda n: seg[s, n]
                signal("keys_ready")
                v.memset(g("same")[:, 0:1], 0.0)
                TT(g("same")[:, 1:COLS], key[:, 1:COLS], key[:, 0:COLS - 1], ALU.is_equal)
                TT(g("last")[:, 0:COLS - 1], key[:, 1:COLS], key[:, 0:COLS - 1], ALU.not_equal)
                v.wait_ge(S["shift_done"], 16 * (i + 1))
                TT(g("last")[:, COLS - 1:COLS], key[:, COLS - 1:COLS], nf[:, i:i + 1], ALU.not_equal)
                D()
                TS(g("notlast")[:, :], g("last")[:, :], -1.0, 1.0, ALU.mult, ALU.add)
                D()
                TS(g("head")[:, :], key[:, :], key[:, 0:1], None, ALU.is_equal)
                TS(g("tail")[:, :], key[:, :], key[:, COLS - 1:COLS], g("notlast")[:, COLS - 1:COLS], ALU.is_equal, ALU.mult)
                v.tensor_copy(kb[:, :], key[:, 0:1].to_broadcast([P, P]))
                ask()
                STT(g("fwd")[:, :], psT[:, 0:P], key[:, COLS - 1:COLS], later[:, :], ALU.is_equal, ALU.mult)
                v.tensor_copy(kb[:, :], key[:, COLS - 1:COLS].to_broadcast([P, P]))
                ask()
                STT(g("bwd")[:, :], psT[:, 0:P], key[:, 0:1], earlier[:, :], ALU.is_equal, ALU.mult)
                D()

            def scan(s, c, src_, dst_, width, n=CHUNK):
                t0 = c * n
                for f in range(width):
                    v.tensor_tensor_scan(dst_[:, ds(t0 + 1, n), f], seg[s, "same"][:, ds(t0, n)], src_[:, ds(t0, n), f],
                                         dst_[:, ds(t0, 1), f], ALU.mult, ALU.add)
                D()

            def carry_in(s, tile, tmp, width):
                ask()
                v.tensor_copy(carry[:, 0:width], psY[:, 0:width])
                D()
                TT(tmp, bc(seg[s, "head"][:, :], width), bt(carry[:, 0:width], COLS), ALU.mult)
                D()
                TT(tile, tile, tmp, ALU.add)
                D()

            def spread(s, src_, tmp, dst_, width):
                TT(tmp, src_, bc(seg[s, "last"][:, :], width), ALU.mult)
                D()
                for f in range(width):
                    v.tensor_tensor_scan(dst_[:, COLS - 1::-1, f] if dst_.shape[1] == COLS else dst_[:, COLS - 1::-1, f],
                                         seg[s, "notlast"][:, ::-1], tmp[:, ::-1, f], 0.0, ALU.mult, ALU.add)
                D()
                ask()
                v.tensor_copy(carry[:, 0:width], psY[:, 0:width])
                D()
                TT(tmp, bc(seg[s, "tail"][:, :], width), bt(carry[:, 0:width], COLS), ALU.mult)
                D()
                TT(dst_[:, 0:COLS, :], dst_[:, 0:COLS, :], tmp, ALU.add)
                D()

            def count_segments(s):
                v.memset(pos[:, :], 1.0)
                D()
                v.tensor_tensor_scan(V[:, 1:COLS + 1, 0], seg[s, "same"][:, :], pos[:, :], 0.0, ALU.mult, ALU.add)
                ask()
                v.tensor_copy(carry[:, 0:1], psY[:, 0:1])
                D()
                STT(pos[:, :], seg[s, "head"][:, :], carry[:, 0:1], V[:, 1:COLS + 1, 0], ALU.mult, ALU.add)
                D()

            def at_last(s, key, mult, add, index):
                TS(dig[:, :], key[:, :], float(mult), float(add) - NOWHERE, ALU.mult, ALU.add)
                D()
                TT(dig[:, :], dig[:, :], seg[s, "last"][:, :], ALU.mult)
                D()
                TS(index[:, :], dig[:, :], NOWHERE, None, ALU.add)
                D()

            def norm(n, X, cols, k, o):
                v.tensor_reduce(mean[0:n, 0:cols], X, AX.X, ALU.add)
                D()
                STT(xc[0:n, 0:cols, :], bc(mean[0:n, 0:cols], F), -1.0 / F, X, ALU.mult, ALU.add)
                D()
                TT(sq[0:n, 0:cols, :], xc[0:n, 0:cols, :], xc[0:n, 0:cols, :], ALU.mult)
                D()
                v.tensor_reduce(var[0:n, 0:cols], sq[0:n, 0:cols, :], AX.X, ALU.add)
                signal("var_ready")
                v.wait_ge(S["std_ready"], k)
                v.reciprocal(rstd[0:n, 0:cols], std[0:n, 0:cols])
                D()
                STT(o, xc[0:n, 0:cols, :], 0.0, bc(rstd[0:n, 0:cols], F), ALU.max, ALU.mult)
                D()

            def product(k):
                signal("h_ready")
                v.wait_ge(S["y_ready"], k)

            def chunk(tile, c, n=CHUNK):
                return tile[:, ds(c * n, n), :]

            def col(a_, c):
                return a_[:, ds(c * CHUNK, CHUNK)]

            hcf = hc[:, :].rearrange("p (t f) -> p t f", f=F)
            hc16 = hc[:, 0:CHUNK * HID].rearrange("p (t f) -> p t f", f=HID)
            y16 = psY[:, 0:CHUNK * HID].rearrange("p (t f) -> p t f", f=HID)
            y32 = psY[:, :].rearrange("p (b r) -> p b r", b=2)[:, :, 0:14 * F].rearrange("p b (t f) -> p b t f", f=F)

            def dense_step(k, st, j, wait):
                v.wait_ge(S["dense_in"], k * 16 + 16)
                halves = lambda t: t.rearrange("p (b t) f -> p b t f", b=2)
                norm(P, dx, DN, j * 2 + (ln0[st] + 1), hcf)
                product(j * 2 + (y0[st] + 1))
                TT(xc[:, :, 0:HID], y16, bt(b1r[:, :], DN), ALU.add)
                D()
                TS(hc16, xc[:, :, 0:HID], 0.0, None, ALU.max)
                TT(dx, dx, bt(b2r[:, :], DN), ALU.add)
                product(j * 2 + (y0[st] + 2))
                TT(halves(dx1), y32, halves(dx), ALU.add)
                v.drain().then_inc(S["dense_used"], 1)
                norm(P, dx1, DN, j * 2 + (ln0[st] + 2), hcf)
                TT(dx1, dx1, bt(br[:, :], DN), ALU.add)
                D()
                if wait is not None:
                    v.wait_ge(S["dense_stored"], wait)
                STT(dout, hcf, ALPHA, dx1, ALU.mult, ALU.add)
                signal("dense_ready")

            def dense(i):
                if i == 0:
                    dense_step(0, "dense0", 0, None)
                with v.Fori(int(i == 0), DENSE[i]) as j:
                    k = j + dense0[i]
                    dense_step(k, f"dense{i}", j, k * 16)

            def columns(half, tile):
                for j in range(2):
                    v.tensor_copy(tile[:, j::2], psT[:, (2 * half + j) * P:(2 * half + j) * P + PAIR_ROWS])
                D()

            def places(k, width, values):
                def hot(u, col):
                    TS(onehot[:, u, 0:width], values[:, 0:width], dig[:, col], None, ALU.is_equal).then_inc(S["onehot_ready"], 1)

                upper, lower = idx, idx_perm
                TS(upper[:, :], dig_i[:, :], 4, None, ALU.logical_shift_right)
                TS(lower[:, :], dig_i[:, :], NIBBLE - 1, None, ALU.bitwise_and)
                D()
                v.tensor_copy(junk[:, 0:COLS], upper[:, :])
                v.tensor_copy(hist[:, 0:COLS], lower[:, :])
                D()
                TT(hot_upper.rearrange("p (t h) -> p t h", h=UPPER), bc(junk[:, 0:COLS], UPPER), bt(iota_low[:, 0:UPPER], COLS), ALU.is_equal)
                TT(hot_lower.rearrange("p (t l) -> p t l", l=NIBBLE), bc(hist[:, 0:COLS], NIBBLE), bt(iota_low[:, 0:NIBBLE], COLS), ALU.is_equal)
                signal("halves_ready")
                if k == 0:
                    v.memset(G[:, :, :], 0.0)
                    signal("rows_cleared")
                    square = ident[0:FOUR * UPPER, 0:FOUR * UPPER]
                    v.tensor_reduce(of_column[:, :], square.rearrange("p (j h) -> p j h", h=UPPER), AX.X, ALU.add)
                    v.tensor_reduce(of_upper[:, :], square.rearrange("p (j h) -> p h j", h=UPPER), AX.X, ALU.add)
                for u in range(BANKS):
                    hot(u, slice(u, u + 1))
                D()
                v.wait_ge(S["counted"], 2 * k + 1)
                m, n = FOUR * UPPER, FOUR * NIBBLE
                TT(hist[0:m, 0:n].rearrange("p (j l) -> p j l", l=NIBBLE), psT[0:m, 0:n].rearrange("p (j l) -> p j l", l=NIBBLE), bc(of_column[:, :], NIBBLE), ALU.mult)
                D()
                v.tensor_reduce(junk[0:m, 0:NIBBLE], hist[0:m, 0:n].rearrange("p (j l) -> p l j", l=NIBBLE), AX.X, ALU.add)
                D()
                TT(by_halves.rearrange("p (h l) -> p h l", l=NIBBLE), bt(junk[0:m, 0:NIBBLE], UPPER), bc(of_upper[:, :], NIBBLE), ALU.mult)
                signal("halves_ready")
                v.wait_ge(S["counted"], 2 * k + 2)
                v.memset(hist[:, 0:width], 1.0)
                v.tensor_copy(junk[:, 0:width], psT[:, 512:512 + width])
                D()
                v.tensor_tensor_scan(rank[:, 0:width], hist[:, 0:width], junk[:, 0:width], 0.0, ALU.mult, ALU.add)
                D()
                TT(rank[:, 0:width], rank[:, 0:width], junk[:, 0:width], ALU.subtract)
                signal("starts_ready")

                def look(t, u, ahead):
                    v.wait_ge(S["rank_ready"], t + (k * COLS + 1))
                    at = lambda i: slice(i, i + 1) if isinstance(i, int) else ds(i, 1)
                    STT(read_out[u % BANKS][:, 0:width], onehot[:, u, 0:width], 1.0, psB[u % BANKS][:, 0:width], ALU.mult, ALU.mult, accum_out=pos[:, at(t)]).then_inc(S["rank_used"], 1)
                    if ahead:
                        hot((u + BANKS) % RING, at(t + BANKS))

                with v.Fori(0, COLS // RING) as g:
                    for u in range(RING):
                        look(g * RING + u, u, True)
                for u in range(COLS % RING):
                    look(COLS // RING * RING + u, u, u + BANKS < COLS % RING)
                D()

            v.wait_ge(S["rows_turned"], 1)
            columns(0, key_a)
            v.tensor_copy(dig_i[:, :], key_a[:, :])
            D()
            TS(dig_i[:, :], dig_i[:, :], DIGIT - 1, None, ALU.bitwise_and)
            D()
            v.tensor_copy(dig[:, :], dig_i[:, :])
            v.tensor_copy(pay[:, :, 0], key_a[:, :])
            v.tensor_copy(pay[:, :, 1], iota_a[:, :])
            D()
            places(0, DIGIT, iota_low)
            v.tensor_copy(idx[:, :], pos[:, :])
            signal("pay_ready")
            v.wait_ge(S["loads"], 16 * 30)
            v.tensor_copy(key_d[:, :], DI[:, :])
            for side in range(2):
                D()
                TT(prod[:, 0:HEADS * F].rearrange("p (h o) -> p h o", o=F), wg[:, :, :], bt(fcr[:, side * F:(side + 1) * F], HEADS), ALU.mult)
                D()
                v.tensor_reduce(wsum[:, side, :], prod[:, 0:HEADS * F].rearrange("p (h o) -> p h o", o=F), AX.X, ALU.add)
                D()
                if side == 0:
                    v.memset(wgbd[:, :], 0.0)
                    D()
                    for g in range(GROUP):
                        v.tensor_copy(wgbd[g * F:(g + 1) * F, g * HEADS * F:(g + 1) * HEADS * F].rearrange("p (h o) -> p h o", o=F), wg[g * F:(g + 1) * F, :, :])
                w = (wa_s, wa_d)[side]
                v.memset(w[:, :], 0.0)
                D()
                for g in range(GROUP):
                    v.tensor_copy(w[g * F:(g + 1) * F, g * HEADS:(g + 1) * HEADS], wsum[g * F:(g + 1) * F, side, :])
            D()

            segments("d", key_d, 0)
            count_segments("d")
            v.tensor_copy(cpay[:, :, 1], pos[:, :])
            TS(cpay[:, :, 0], iota_e[:, :], 1.0, None, ALU.add)
            at_last("d", key_d, ROW // 2, INFO // 2, idx_cq)
            at_last("d", key_d, 1, 0, idx_outd)
            signal("pay_ready")
            dense(0)
            v.wait_ge(S["rows_turned"], 3)
            columns(0, key_a)
            columns(1, pos)
            v.tensor_copy(pay[:, :, 0], key_a[:, :])
            v.tensor_copy(pay[:, :, 1], pos[:, :])
            v.tensor_copy(dig_i[:, :], key_a[:, :])
            D()
            TS(dig_i[:, :], dig_i[:, :], 8, None, ALU.logical_shift_right)
            D()
            v.tensor_copy(dig[:, :], dig_i[:, :])
            D()
            TS(dig[:, :], dig[:, :], -float(HIGH // 2), None, ALU.add)
            D()
            places(1, HIGH, iota_high)
            v.tensor_copy(idx[:, :], pos[:, :])
            signal("pay_ready")
            dense(1)
            v.wait_ge(S["reloaded"], 32)
            v.tensor_copy(key_p[:, :], pay[:, :, 0])
            v.tensor_copy(idx_perm[:, :], pay[:, :, 1])
            D()
            segments("p", key_p, 1)
            count_segments("p")
            v.tensor_copy(pay[:, :, 0], pos[:, :])
            TS(pay[:, :, 1], iota_e[:, :], 1.0, None, ALU.add)
            at_last("p", key_p, ROW // 2, INFO // 2 + 1, idx)
            at_last("p", key_p, 1, 0, idx_outs)
            signal("pay_ready")

            dense(2)

            def lookup(last, index, at):
                a_, b_ = dig[:, at], hasnot[:, at]
                TS(b_, last, 0.0, None, ALU.is_equal)
                TS(a_, iota_e[:, at], float(SLOTS), None, ALU.add)
                D()
                TT(a_, a_, b_, ALU.mult)
                D()
                TT(a_, a_, last, ALU.add)
                D()
                TT(a_, a_, b_, ALU.add)
                D()
                TS(a_, a_, -1.0, None, ALU.add)
                D()
                v.tensor_copy(index[:, at], a_)

            def inverse_roots(rows, c, k):
                v.wait_ge(S["roots_done"], k)
                v.reciprocal(inv[:, rows, ds(c * CHUNK, CHUNK)], roots[:, rows, ds(c * CHUNK, CHUNK)])

            def s1(c, wait):
                at = ds(c * CHUNK, CHUNK)
                v.wait_ge(S["cols_ready"], c + (col0["xs"] + 1))
                TS(roots[:, GCN_S, at], XS[:, at, INFO + 1], 1.0, None, ALU.add)
                TS(roots[:, OUT_S, at], XS[:, at, INFO + 2], 1.0, None, ALU.max)
                norm(P, XS[:, at, 0:F], CHUNK, c + (ln0["s1"] + 1), hcf)
                inverse_roots(ROOTS_S, c, c + 1)
                product(c + (y0["s1"] + 1))
                TT(G16[:, at, :], y16, bc(col(inv[:, GCN_S, :], c), HID), ALU.mult)
                TT(gS[:, :, HID:2 * HID], y16, bt(b1r[:, :], CHUNK), ALU.add)
                D()
                if wait:
                    v.wait_ge(S["local_stored"], c * 16)
                TS(gS[:, :, 0:HID], gS[:, :, HID:2 * HID], 0.0, None, ALU.max)
                scan("d", c, G16, V, HID)
                signal("local_ready")
            s1(0, False)
            with v.Fori(1, CHUNKS) as c:
                s1(c, True)
            lookup(XS[:, :, INFO], idx_q, slice(0, COLS))
            v.tensor_copy(pos[:, :], dig[:, :])
            signal("lookup_ready")

            live, place, rows = hist[:, 0:COLS], rank[:, 0:COLS], junk[:, 0:COLS]
            count, ofseg = V[:, 1:, HID + 1], V[:, 1:, HID]
            TS(live, hasnot[:, :], -1.0, 1.0, ALU.mult, ALU.add)
            v.memset(place, 1.0)
            D()
            v.tensor_tensor_scan(count, place, live, 0.0, ALU.mult, ALU.add)
            v.tensor_tensor_scan(ofseg, seg["d", "same"][:, :], live, 0.0, ALU.mult, ALU.add)
            ask()
            v.tensor_copy(sm[:, 0:1], psY[:, 0:1])
            TS(sm[:, 1:2], psY[:, 512:513], 1.0 / (P * LIVE), (P * LIVE - 0.5) / (P * LIVE) - 0.5, ALU.mult, ALU.add)
            D()
            v.tensor_copy(groups_i[:, :], sm[:, 1:2])
            D()
            TS(sm[:, 1:2], groups_i[:, :], 1.0, None, ALU.max)
            D()
            v.tensor_copy(groups_i[:, :], sm[:, 1:2])
            TS(sm[:, 2:3], sm[:, 1:2], float(LIVE), None, ALU.mult)
            D()
            v.reciprocal(sm[:, 3:4], sm[:, 2:3])
            TS(sm[:, 4:5], sm[:, 2:3], -1.0, float(COLS), ALU.mult, ALU.add)
            TS(count, count, sm[:, 0:1], -1.0, ALU.add, ALU.add)
            D()
            TS(rows, count, 0.5, sm[:, 3:4], ALU.add, ALU.mult)
            D()
            TS(rows, rows, -0.5, None, ALU.add)
            D()
            v.tensor_copy(idx[:, :], rows)
            D()
            v.tensor_copy(rows, idx[:, :])
            D()
            TS(place, rows, sm[:, 2:3], None, ALU.mult)
            D()
            TT(place, count, place, ALU.subtract)
            D()
            TS(dig[:, :], place, sm[:, 2:3], None, ALU.is_ge)
            TS(place, place, 0.0, None, ALU.is_lt)
            D()
            TT(rows, rows, dig[:, :], ALU.add)
            D()
            TT(rows, rows, place, ALU.subtract)
            D()
            STT(place, rows, sm[:, 4:5], count, ALU.mult, ALU.add)
            D()
            TS(dig[:, :], place, -NOWHERE, None, ALU.add)
            TS(place, place, 1.0, None, ALU.add)
            D()
            TT(dig[:, :], dig[:, :], live, ALU.mult)
            D()
            TS(idx[:, :], dig[:, :], NOWHERE, None, ALU.add)
            ask()
            v.tensor_copy(carry[:, 0:1], psY[:, 0:1])
            D()
            STT(ofseg, seg["d", "head"][:, :], carry[:, 0:1], ofseg, ALU.mult, ALU.add)
            D()
            STT(cpos[:, :], ofseg, 0.0, place, ALU.is_gt, ALU.mult)
            signal("live_counted")
            with v.Fori(0, CHUNKS) as c:
                at = ds(c * CHUNK, CHUNK)
                v.wait_ge(S["cols_ready"], c + (col0["xd"] + 1))
                TS(roots[:, GCN_D, at], XD[:, at, INFO + 1], 1.0, None, ALU.add)
                TS(roots[:, IN_D, at], XD[:, at, INFO + 1], 1.0, None, ALU.max)
                TS(roots[:, OUT_D, at], XD[:, at, INFO + 2], 1.0, None, ALU.max)
                norm(P, XD[:, at, 0:F], CHUNK, c + (ln0["d1"] + 1), hcf)
                inverse_roots(ROOTS_D, c, c + (CHUNKS + 1))
                product(c + (y0["d1"] + 1))
                TT(Z16[:, at, :], y16, bc(col(inv[:, GCN_D, :], c), HID), ALU.mult)
                D()
            v.tensor_copy(cpay[:, :, 0], pos[:, :])
            TS(cpay[:, :, 1], XD[:, :, INFO], -1.0, None, ALU.add)
            v.tensor_copy(cpay[:, :, 2], key_d[:, :])
            v.memset(cpay[:, :, 3], 0.0)
            signal("pay_ready")
            STT(a_d[:, :], inv[:, IN_D, :], 1.0 - ALPHA, inv[:, OUT_D, :], ALU.mult, ALU.mult)
            carry_in("d", V[:, 1:, 0:HID], B[:, :, 0:HID], HID)
            TT(V[:, 1:, 0:HID], V[:, 1:, 0:HID], Z16, ALU.add)
            TT(a_head[:, :], a_d[:, :], seg["d", "head"][:, :], ALU.mult)
            D()
            TT(V[:, 1:, 0:HID], V[:, 1:, 0:HID], bc(inv[:, GCN_D, :], HID), ALU.mult)
            D()
            TT(V[:, 1:, 0:HID], V[:, 1:, 0:HID], bt(b1r[:, :], COLS), ALU.add)
            D()
            STT(G16, V[:, 1:, 0:HID], 0.0, bc(inv[:, GCN_D, :], HID), ALU.max, ALU.mult)
            signal("rows_ready")
            dense(3)
            v.wait_ge(S["rows_stored"], 16)
            v.tensor_copy(Z16, G16)
            D()
            signal("own_kept")
            v.wait_ge(S["reloaded"], 48)
            groups = v.value_load(groups_i[0:1, 0:1], min_val=1, max_val=LIVES)
            key_c = cpay[:, :, 2]
            v.tensor_copy(idx_cq[:, :], cpay[:, :, 0])
            v.tensor_copy(idx_cd[:, :], cpay[:, :, 1])
            v.memset(same_c[:, 0:1], 0.0)
            TT(same_c[:, 1:COLS], cpay[:, 1:COLS, 2], cpay[:, 0:COLS - 1, 2], ALU.is_equal)
            D()
            v.tensor_copy(within_c[:, :], same_c[:, :])
            D()
            v.memset(within_c[:, 0::LIVE], 0.0)
            TS(head_c[:, :], key_c, cpay[:, 0, 2:3], None, ALU.is_equal)
            v.tensor_copy(sm[:, 5:6], cpay[:, ds(groups * LIVE - 1, 1), 2])
            v.tensor_copy(kb[:, :], cpay[:, 0, 2:3].to_broadcast([P, P]))
            ask()
            STT(fwd_c[:, :], psT[:, 0:P], sm[:, 5:6], later[:, :], ALU.is_equal, ALU.mult)
            D()
            with v.Fori(0, CHUNKS) as c:
                v.wait_ge(S["cols_ready"], c + (col0["g"] + 1))
                v.tensor_copy(hc16, G16[:, ds(c * CHUNK, CHUNK), :])
                signal("h_ready")
                scan("d", c, G16, V, HID)
                v.wait_ge(S["y_ready"], c * 2 + (y0["x1"] + 1))
                v.wait_ge(S["local_stored"], c * 16 + 16 * CHUNKS)
                TT(gS[:, :, :].rearrange("p (b t) f -> p b t f", b=2), y32, XS[:, ds(c * CHUNK, CHUNK), 0:F].rearrange("p (b t) f -> p b t f", b=2), ALU.add)
                D()
                TT(gS[:, :, :], gS[:, :, :], bt(b2r[:, :], CHUNK), ALU.add)
                signal("local_ready")
                TT(hc16, V[:, ds(c * CHUNK + 1, CHUNK), 0:HID], Z16[:, ds(c * CHUNK, CHUNK), :], ALU.add)
                D()
                TT(hc16, hc16, bc(col(inv[:, GCN_D, :], c), HID), ALU.mult)
                product(c * 2 + (y0["x1"] + 2))
                TT(xc[:, :, :].rearrange("p (b t) f -> p b t f", b=2), y32, XD[:, ds(c * CHUNK, CHUNK), 0:F].rearrange("p (b t) f -> p b t f", b=2), ALU.add)
                D()
                TT(XD[:, ds(c * CHUNK, CHUNK), 0:F], xc[:, :, :], bt(b2r[:, :], CHUNK), ALU.add)
                D()
            ask()
            v.tensor_copy(hc[:, 0:HID], psY[:, 0:HID])
            TT(junk[:, 0:COLS], inv[:, GCN_D, :], seg["d", "head"][:, :], ALU.mult)
            product(y0["x1carry"] + 1)
            v.tensor_copy(carry[:, :], psY[:, 0:F])
            D()
            for f in range(F):
                STT(V[:, 1:, f], junk[:, 0:COLS], carry[:, f:f + 1], XD[:, :, f], ALU.mult, ALU.add)
            signal("rows_ready")
            v.tensor_copy(XD[:, :, 0:F], V[:, 1:, :])
            D()
            v.wait_ge(S["rows_stored"], 32)

            def own(c):
                at = ds(c * CHUNK, CHUNK)
                TT(G[:, at, :], V[:, ds(c * CHUNK + 1, CHUNK), :], bc(col(a_d, c), F), ALU.mult)
                D()
                TT(G[:, at, :], G[:, at, :], B[:, at, :], ALU.add)
                D()

            def earlier_rows():
                v.tensor_copy(carry[:, :], psY[:, 0:F])
                D()
                for f in range(F):
                    STT(G[:, :, f], a_head[:, :], carry[:, f:f + 1], G[:, :, f], ALU.mult, ALU.add)
                signal("rows_ready")

            with v.Fori(0, CHUNKS) as c:
                norm(P, XD[:, ds(c * CHUNK, CHUNK), 0:F], CHUNK, c + (ln0["h1d"] + 1), hcf)
                STT(chunk(B, c), hcf, ALPHA, bc(col(inv[:, OUT_D, :], c), F), ALU.mult, ALU.mult)
                D()
            with v.Fori(0, CHUNKS) as c:
                at = ds(c * CHUNK, CHUNK)
                v.wait_ge(S["cols_ready"], c + (col0["x1"] + 1))
                norm(P, chunk(G, c), CHUNK, c + (ln0["h1s"] + 1), hcf)
                v.wait_ge(S["local_stored"], c * 16 + 32 * CHUNKS)
                STT(gS[:, :, :], hcf, ALPHA, chunk(G, c), ALU.mult, ALU.add)
                v.drain().then_inc(S["local_ready"], 1)
                TT(hcf, hcf, bc(col(inv[:, OUT_S, :], c), F), ALU.mult)
                D()
                v.tensor_copy(chunk(G, c), hcf)
                STT(XS[:, at, 0:F], hcf, ALPHA, bc(col(hasnot, c), F), ALU.mult, ALU.mult)
                D()
                scan("d", c, G, V, F)
                own(c)
            ask()
            earlier_rows()

            for f in range(F):
                v.tensor_tensor_scan(XS[:, :, f], seg["d", "same"][:, :], XS[:, :, f], 0.0, ALU.mult, ALU.add)
            ask()
            v.tensor_copy(carry[:, :], psY[:, 0:F])
            D()
            for f in range(F):
                STT(XS[:, :, f], seg["d", "head"][:, :], carry[:, f:f + 1], XS[:, :, f], ALU.mult, ALU.add)
            D()
            TT(XS[:, :, 0:F], XS[:, :, 0:F], bc(a_d[:, :], F), ALU.mult)
            v.tensor_copy(XS[:, :, INFO], a_d[:, :])
            v.tensor_copy(XS[:, :, INFO + 1], cpos[:, :])
            D()
            TT(XS[:, :, 0:F], XS[:, :, 0:F], B[:, :, :], ALU.add)
            signal("rows_ready")
            lper = 16 * LIVE

            def keep(c):
                at = slice(c * LIVE, (c + 1) * LIVE)
                v.wait_ge(live_chunk[c], 2 * lper)
                v.tensor_copy(B[:, at, :], XS[:, at, 0:F])
                v.tensor_copy(a_c[:, at], XS[:, at, INFO])
                v.tensor_copy(cpos[:, at], XS[:, at, INFO + 1])
            nest(v, groups, LIVES, keep)
            signal("own_rows_kept")
            TT(a_head[:, :], a_c[:, :], head_c[:, :], ALU.mult)
            TS(dig[:, :], iota_e[:, :], 1.0, None, ALU.add)
            D()
            TT(dig[:, :], dig[:, :], cpos[:, :], ALU.is_equal)
            TS(junk[:, 0:COLS], cpay[:, :, 1], -NOWHERE, None, ALU.add)
            D()
            TT(dig[:, :], dig[:, :], junk[:, 0:COLS], ALU.mult)
            D()
            TS(idx_cu[:, :], dig[:, :], NOWHERE, None, ALU.add)

            rows_f, sums_f, mask_f = (t[:, 0:F * LIVE].rearrange("p (f t) -> p f t", t=LIVE) for t in (hT, hc, junk))
            flat = lambda t: t.rearrange("p f t -> p (f t)")

            def step(tail, count):
                def group(c):
                    at = slice(c * LIVE, (c + 1) * LIVE)
                    v.tensor_copy(mask_f, within_c[:, at].unsqueeze(1).to_broadcast([P, F, LIVE]))
                    v.wait_ge(live_chunk[c], count)
                    first = slice(c * LIVE, c * LIVE + 1)
                    v.tensor_copy(rows_f[:, :, 1:], G[:, c * LIVE + 1:(c + 1) * LIVE, :].rearrange("p t f -> p f t"))
                    if c == 0:
                        v.tensor_copy(rows_f[:, :, 0], G[:, 0, :])
                    else:
                        STT(rows_f[:, :, 0], last_c[:, :], same_c[:, first], G[:, c * LIVE, :], ALU.mult, ALU.add)
                    D()
                    v.tensor_tensor_scan(flat(sums_f), flat(mask_f), flat(rows_f), 0.0, ALU.mult, ALU.add)
                    D()
                    TT(G[:, at, :], sums_f.rearrange("p f t -> p t f"), bc(a_c[:, at], F), ALU.mult)
                    v.tensor_copy(last_c[:, :], sums_f[:, :, LIVE - 1])
                    D()
                    TT(G[:, at, :], G[:, at, :], B[:, at, :], ALU.add)
                nest(v, groups, LIVES, group)
                v.drain().then_inc(S["tail_ready"], 1)
                v.wait_ge(S["carry_ready"], tail)
                v.tensor_copy(carry[:, :], psY[:, 0:F])
                D()

                def part(j):
                    at = slice(j * PART, (j + 1) * PART)
                    for f in range(F):
                        STT(G[:, at, f], a_head[:, at], carry[:, f:f + 1], G[:, at, f], ALU.mult, ALU.add)
                parts(v, groups, part)
                signal("prop_ready")

            step(14, lper)
            nest(v, groups, LIVES, lambda c: v.wait_ge(live_chunk[c], 3 * lper))
            lookup(XS[:, :, INFO + 1], idx_cl, slice(0, COLS))
            signal("consts_ready")
            with v.Fori(0, STEPS - 2) as r:
                step(r + 15, r * lper + 4 * lper)
            state["tail"] += STEPS - 1

            def out_rows(c):
                at = slice(c * LIVE, (c + 1) * LIVE)
                v.tensor_copy(XS[:, at, 0:F], G[:, at, :])
            nest(v, groups, LIVES, out_rows)
            signal("live_out_ready")
            own_x2 = V[:, 1:, :]
            for i, at in enumerate(OUT_HALVES):
                v.wait_ge(own_reloaded[i], 16)
                TT(own_x2[:, at, :], XS[:, at, 0:F], bc(roots[:, OUT_D, at], F), ALU.mult)
                D()
                TT(own_x2[:, at, :], own_x2[:, at, :], XD[:, at, 0:F], ALU.add)
                D()
                TT(B[:, at, :], own_x2[:, at, :], bt(br[:, :], at.stop - at.start), ALU.add)
                signal("out_rows_ready")
            signal("rows_ready")
            spread("d", V[:, 1:, :], G[:, :, :], XD[:, :, 0:F], F)
            v.tensor_copy(XD[:, :, INFO + 2], XD[:, :, INFO + 3])
            v.tensor_copy(XD[:, :, INFO:INFO + 2], ea[:, :, :])
            D()
            v.tensor_copy(XD[:, :, INFO + 3], pos[:, :])
            signal("rows_ready")

            def lookups(c):
                at = ds(c * CHUNK, CHUNK)
                v.wait_ge(S["cols_ready"], c + (col0["pair"] + 1))
                v.tensor_copy(idx_q[:, at], XS[:, at, INFO + 3])
                lookup(XS[:, at, INFO + 2], SI, at)
                signal("lookup_ready")

            def tents(c):
                U = XS[:, ds(c * CHUNK, CHUNK), INFO:INFO + 2]
                h = 2.0 / (BASIS - 1)
                for k in range(BASIS):
                    TS(tent[:, :, k::BASIS], U, 1.0 - k * h, 1.0 / h, ALU.add, ALU.mult)
                D()
                TS(falling[:, :, :], tent[:, :, :], -1.0, 1.0, ALU.mult, ALU.add)
                TS(tent[:, :, :], tent[:, :, :], 1.0, None, ALU.add)
                D()
                TT(tent[:, :, :], tent[:, :, :], falling[:, :, :], ALU.min)
                D()
                TS(tent[:, :, :], tent[:, :, :], 0.0, None, ALU.max)
                D()

            def rows_in(c):
                lookups(c)
                norm(P, XS[:, ds(c * CHUNK, CHUNK), 0:F], CHUNK, c + (ln0["spline"] + 1), hcf)

            def spline(c, first=False, last=False):
                n = CHUNK // GROUP
                for g in range(n + 1):
                    if g < n:
                        if g >= 2:
                            v.wait_ge(S["outer_turned"], c * n + (g - 1))
                        at = slice(g * GROUP, (g + 1) * GROUP)
                        TT(outer[g % 2].rearrange("p (t b f) -> p t b f", b=BASIS, f=F),
                           hcf[:, at, :].unsqueeze(2).to_broadcast([P, GROUP, BASIS, F]),
                           tent[:, at, BASIS:2 * BASIS].unsqueeze(3).to_broadcast([P, GROUP, BASIS, F]), ALU.mult).then_inc(S["outer_ready"], 1)
                    if g == 1 and not first:
                        scan("p", c - 1, XD, V, F)
                    if g == n - 1 and not last:
                        D()
                        v.wait_ge(S["outer_turned"], c * n + g)
                        rows_in(c + 1)
                    if g > 0:
                        at = slice((g - 1) * GROUP, g * GROUP)
                        v.wait_ge(S["outer_used"], c * n + g)
                        TT(prod[:, :].rearrange("p (t a o) -> p t a o", a=BASIS, o=F),
                           psB[2 + (g - 1) % 2][:, :].rearrange("p (t a o) -> p t a o", a=BASIS, o=F),
                           tent[:, at, 0:BASIS].unsqueeze(3).to_broadcast([P, GROUP, BASIS, F]), ALU.mult)
                        v.drain().then_inc(S["result_used"], 1)
                        v.tensor_reduce(XD[:, ds(c * CHUNK + (g - 1) * GROUP, GROUP), 0:F], prod[:, :].rearrange("p (t a o) -> p t o a", a=BASIS, o=F), AX.X, ALU.add)
                        D()
                if last:
                    scan("p", c, XD, V, F)
                else:
                    tents(c + 1)

            v.wait_ge(S["rows_stored"], 16 * 5)
            rows_in(0)
            tents(0)
            spline(0, first=True)
            with v.Fori(1, CHUNKS - 1) as c:
                spline(c)
            spline(CHUNKS - 1, last=True)
            ask()
            v.tensor_copy(carry[:, :], psY[:, 0:F])
            D()
            for f in range(F):
                STT(V[:, 1:, f], seg["p", "head"][:, :], carry[:, f:f + 1], V[:, 1:, f], ALU.mult, ALU.add)
            D()
            for at, chunks in ((slice(0, COLS - CHUNK), CHUNKS - 1), (slice(COLS - CHUNK, COLS), CHUNKS)):
                v.wait_ge(S["cols_ready"], col0["x2"] + chunks)
                TT(V[:, 1:, :][:, at, :], V[:, 1:, :][:, at, :], G[:, at, :], ALU.add)
            signal("rows_ready")
            spread("p", V[:, 1:, :], XD[:, :, 0:F], G, F)

            with v.Fori(0, CHUNKS) as c:
                norm(P, chunk(G, c), CHUNK, c + (ln0["att_src"] + 1), hcf)
                product(c + (y0["att_src"] + 1))
                TS(chunk(sc4, c), psY[:, 0:CHUNK * HEADS].rearrange("p (t h) -> p t h", h=HEADS), fbr[:, 0:1], None, ALU.add)
                TT(chunk(G, c), chunk(G, c), bt(br[:, :], CHUNK), ALU.add)
                D()
            TS(neg_same[:, :], seg["p", "same"][:, :], -1.0, HUGE, ALU.add, ALU.mult)
            TS(neg_head[:, :], seg["p", "head"][:, :], -1.0, HUGE, ALU.add, ALU.mult)
            TS(neg_bwd[:, :], seg["p", "bwd"][:, :], -1.0, HUGE, ALU.add, ALU.mult)
            with v.Fori(0, CHUNKS) as c:
                v.wait_ge(S["cols_ready"], c + (col0["x3"] + 1))
                norm(P, XS[:, ds(c * CHUNK, CHUNK), 0:F], CHUNK, c + (ln0["att_dst"] + 1), hcf)
                signal("h_ready")
                v.tensor_copy(XS[:, ds(c * CHUNK, CHUNK), 0:F], hcf)
                v.wait_ge(S["y_ready"], c + (y0["att_dst"] + 1))
                TT(chunk(sc4, c), chunk(sc4, c), psY[:, 0:CHUNK * HEADS].rearrange("p (t h) -> p t h", h=HEADS), ALU.add)
                D()
                STT(chunk(sc4, c), chunk(sc4, c), SLOPE, chunk(sc4, c), ALU.mult, ALU.max)
                D()
            for h in range(HEADS):
                v.tensor_tensor_scan(v4[:, 1:COLS + 1, h], neg_same[:, :], sc4[:, :, h], 0.0, ALU.add, ALU.max)
            D()
            for h in range(HEADS):
                v.tensor_copy(kb[:, :], v4[:, COLS, h:h + 1].to_broadcast([P, P]))
                ask()
                TT(junk[:, 0:P], psT[:, 0:P], neg_bwd[:, :], ALU.add)
                D()
                v.tensor_reduce(carry[:, h:h + 1], junk[:, 0:P], AX.X, ALU.max)
                D()
                TS(pos[:, :], neg_head[:, :], carry[:, h:h + 1], None, ALU.add)
                D()
                TT(v4[:, 1:COLS + 1, h], v4[:, 1:COLS + 1, h], pos[:, :], ALU.max)
                D()
            tmp4 = XD[:, :, 0:HEADS]
            spread("p", v4[:, 1:, :], tmp4, w4, HEADS)
            TT(sc4, sc4, w4[:, 0:COLS, :], ALU.subtract)
            signal("exp_ready")
            TT(pos[:, :], seg["p", "head"][:, :], seg["p", "last"][:, :], ALU.mult)
            v.tensor_copy(dig[:, :], idx_outs[:, :])
            D()
            STT(junk[:, 0:COLS], dig[:, :], -NOWHERE, pos[:, :], ALU.add, ALU.mult)
            STT(dig[:, :], seg["p", "head"][:, :], NOWHERE, dig[:, :], ALU.mult, ALU.max)
            D()
            v.tensor_copy(idx[:, :], dig[:, :])
            v.tensor_reduce(sm[:, 6:7], junk[:, 0:COLS], AX.X, ALU.add)
            D()
            TS(head_i[:, :], sm[:, 6:7], NOWHERE, None, ALU.add)
            v.wait_ge(S["exp_done"], 1)
            for h in range(HEADS):
                v.tensor_tensor_scan(v4[:, 1:COLS + 1, h], seg["p", "same"][:, :], sc4[:, :, h], 0.0, ALU.mult, ALU.add)
            D()
            carry_in("p", v4[:, 1:, :], tmp4, HEADS)
            spread("p", v4[:, 1:, :], tmp4, w4, HEADS)
            v.reciprocal(v4[:, 1:, :], w4[:, 0:COLS, :])
            D()
            STT(sc4, sc4, 1.0 / HEADS, v4[:, 1:, :], ALU.mult, ALU.mult)
            D()
            n = CHUNK // GROUP
            with v.Fori(0, CHUNKS) as c:
                at = ds(c * CHUNK, CHUNK)
                v.tensor_copy(hcf, XS[:, at, 0:F])
                signal("h_ready")
                v.tensor_copy(att[:, :].rearrange("p (t h) -> p t h", h=HEADS), chunk(sc4, c))
                D()
                for g in range(n):
                    v.wait_ge(S["wide_ready"], c * n + (g + 1))
                    TT(prod[:, :].rearrange("p (k o) -> p k o", o=F), psB[g % 4][:, :].rearrange("p (k o) -> p k o", o=F),
                       bc(att[:, g * GROUP * HEADS:(g + 1) * GROUP * HEADS], F), ALU.mult)
                    v.drain().then_inc(S["wide_used"], 1)
                    v.tensor_reduce(XD[:, ds(c * CHUNK + g * GROUP, GROUP), 0:F], prod[:, :].rearrange("p (t h o) -> p t o h", h=HEADS, o=F), AX.X, ALU.add)
                    D()
                scan("p", c, XD, V, F)
                TT(XD[:, at, 0:F], V[:, ds(c * CHUNK + 1, CHUNK), :], chunk(G, c), ALU.add)
                signal("out_chunk")
            ask()
            v.tensor_copy(carry[:, :], psY[:, 0:F])
            TT(V[:, 1:, :], XD[:, :, 0:F], bc(pos[:, :], F), ALU.mult)
            D()
            v.tensor_reduce(head_row[:, :], V[:, 1:, :].rearrange("p t f -> p f t"), AX.X, ALU.add)
            D()
            TT(head_row[:, :], head_row[:, :], carry[:, :], ALU.add)
            signal("out_rows_ready")


_INS = ["x", "src", "dst", "edge_attr_2", "L0_gnn_W1", "L0_gnn_b1", "L0_gnn_W2", "L0_gnn_b2", "L2_gnn_weight",
        "L3_gnn_w", "L3_gnn_fc_w", "L3_gnn_fc_b", "L3_gnn_bias"]


def kernel(**inputs):
    import numpy as _np
    import concourse.bacc as _bacc
    from concourse import mybir as _mybir
    from concourse.bass_utils import run_bass_kernel_spmd as _run

    nc = _bacc.Bacc("TRN2", target_bir_lowering=False, num_devices=1)
    arrays, args = {}, []
    for name in _INS:
        a = _np.ascontiguousarray(inputs[name])
        arrays[f"in_{name}_dram"] = a
        args.append(nc.dram_tensor(f"in_{name}_dram", a.shape, _mybir.dt.from_np(a.dtype), kind="ExternalInput").ap())
    args.append(nc.dram_tensor("out_0_dram", (N, F), F32, kind="ExternalOutput").ap())
    gnn_kernel(nc, *args)
    r = _run(nc, [arrays], core_ids=[0])
    return r.results[0]["out_0_dram"]
```
